# Optimizing a Trainium2 kernel written in Bass

```python
import numpy as np
import jax
import jax.numpy as jnp

def _softmax(x, axis=-1):
    return jax.nn.softmax(x, axis=axis)

def _gelu(x):
    return jax.nn.gelu(x, approximate=True)

def _silu(x):
    return jax.nn.silu(x)

def _sigmoid(x):
    return jax.nn.sigmoid(x)

def _layernorm(x, axis=-1, eps=1e-05):
    m = jnp.mean(x, axis=axis, keepdims=True)
    v = jnp.var(x, axis=axis, keepdims=True)
    return (x - m) / jnp.sqrt(v + eps)

def _scatter_add(tgt, idx, src, axis=0):
    return tgt.at[idx].add(src)

def _segment_sum(src, seg, n):
    return jax.ops.segment_sum(src, seg, n)
kernel_name = 'mk_prb_d4_jaxref_r8_78a222'

def setup_inputs(seed: int=0):
    np.random.seed(seed)
    _w = jnp.asarray

    def _L0_attn_setup():
        import jax, jax.numpy as jnp
        import numpy as np
        D_MODEL = 128
        N_HEADS = 16
        D_LATENT = 32
        HEAD_DIM = D_MODEL // N_HEADS

        def apply_rope(x):
            B, T, H, D = x.shape
            inv_freq = 1.0 / 10000.0 ** (jnp.arange(0, D, 2, dtype=jnp.float32) / D)
            t = jnp.arange(T, dtype=jnp.float32)
            freqs = t[:, None] * inv_freq[None, :]
            sin_f = jnp.sin(freqs)[None, :, None, :]
            cos_f = jnp.cos(freqs)[None, :, None, :]
            x1, x2 = jnp.split(x, 2, axis=-1)
            return jnp.concatenate([x1 * cos_f - x2 * sin_f, x1 * sin_f + x2 * cos_f], axis=-1)
        key = jax.random.key(seed)
        ks = jax.random.split(key, 10)
        B, T = (4, 512)
        s = lambda fan_in: 1.0 / np.sqrt(fan_in)
        return {'x': jax.random.normal(ks[0], (B, T, D_MODEL), dtype=jnp.float32), 'Wq': jax.random.normal(ks[1], (D_MODEL, D_MODEL), dtype=jnp.float32) * s(D_MODEL), 'bq': jnp.zeros((D_MODEL,), jnp.float32), 'Wdown': jax.random.normal(ks[2], (D_MODEL, D_LATENT), dtype=jnp.float32) * s(D_MODEL), 'bdown': jnp.zeros((D_LATENT,), jnp.float32), 'Wup': jax.random.normal(ks[3], (D_LATENT, 2 * D_MODEL), dtype=jnp.float32) * s(D_LATENT), 'bup': jnp.zeros((2 * D_MODEL,), jnp.float32), 'Wout': jax.random.normal(ks[4], (D_MODEL, D_MODEL), dtype=jnp.float32) * s(D_MODEL), 'bout': jnp.zeros((D_MODEL,), jnp.float32)}
    _L0_attn_in = _L0_attn_setup()

    def _L0_ffn_setup():
        import jax, jax.numpy as jnp
        import numpy as np
        D, F, E, K = (128, 344, 8, 2)
        key = jax.random.key(seed)
        k0, k1, k2, k3, k4 = jax.random.split(key, 5)
        s = 0.02
        x = jax.random.normal(k0, (2, 64, D), jnp.float32)
        Ws = jax.random.normal(k1, (D, E), jnp.float32) * s
        bs = jnp.zeros((E,), jnp.float32)
        Wg = jax.random.normal(k2, (E, D, F), jnp.float32) * s
        Wu = jax.random.normal(k3, (E, D, F), jnp.float32) * s
        Wd = jax.random.normal(k4, (E, F, D), jnp.float32) * s
        return {'x': x, 'Ws': Ws, 'bs': bs, 'Wg': Wg, 'Wu': Wu, 'Wd': Wd}
    _L0_ffn_in = _L0_ffn_setup()

    def _L1_attn_setup():
        import jax, jax.numpy as jnp
        import numpy as np
        B_, L, D_MODEL = (2, 256, 128)
        EXPAND, D_INNER, D_STATE, DT_RANK, D_CONV = (2, 256, 16, 64, 4)
        DT_MIN, DT_MAX = (0.001, 0.1)
        key = jax.random.key(seed)
        ks = jax.random.split(key, 8)
        s = lambda fan: 1.0 / np.sqrt(fan)
        A0 = jnp.broadcast_to(jnp.arange(1, D_STATE + 1, dtype=jnp.float32), (D_INNER, D_STATE))
        return {'x': jax.random.normal(ks[0], (B_, L, D_MODEL), jnp.float32), 'W_in': jax.random.normal(ks[1], (D_MODEL, 2 * D_INNER), jnp.float32) * s(D_MODEL), 'conv_k': jax.random.normal(ks[2], (D_CONV, D_INNER // EXPAND, D_INNER), jnp.float32) * s(D_CONV * D_INNER // EXPAND), 'conv_b': jnp.zeros((D_INNER,), jnp.float32), 'W_x': jax.random.normal(ks[3], (D_INNER, DT_RANK + 2 * D_STATE), jnp.float32) * s(D_INNER), 'W_dt': jax.random.normal(ks[4], (DT_RANK, D_INNER), jnp.float32) * s(DT_RANK), 'b_dt': jnp.zeros((D_INNER,), jnp.float32), 'A_log': jnp.log(A0), 'D': jnp.ones((D_INNER,), jnp.float32), 'W_out': jax.random.normal(ks[5], (D_INNER, D_MODEL), jnp.float32) * s(D_INNER)}
    _L1_attn_in = _L1_attn_setup()

    def _L1_ffn_setup():
        import jax, jax.numpy as jnp
        import numpy as np
        key = jax.random.key(seed)
        k1, k2, k3, k4 = jax.random.split(key, 4)
        B, T, M = (4, 256, 128)
        E, F = (16, 512)
        x = jax.random.normal(k1, (B, T, M), dtype=jnp.float32) * 0.02
        Wg = jax.random.normal(k2, (M, E), dtype=jnp.float32) * 0.02
        w1 = jax.random.normal(k3, (E, M, F), dtype=jnp.float32) * 0.02
        w2 = jax.random.normal(k4, (E, F, M), dtype=jnp.float32) * 0.02
        return {'x': x, 'Wg': Wg, 'w1': w1, 'w2': w2}
    _L1_ffn_in = _L1_ffn_setup()

    def _L2_attn_setup():
        import jax, jax.numpy as jnp
        import numpy as np
        B, L, C, H = (8, 128, 128, 16)
        key = jax.random.key(seed)
        k0, k1, k2 = jax.random.split(key, 3)
        s = 0.02
        return {'x': jax.random.normal(k0, (B, L, C), jnp.float32), 'W_qkv': jax.random.normal(k1, (C, 3 * C), jnp.float32) * s, 'b_qkv': jnp.zeros((3 * C,), jnp.float32), 'W_proj': jax.random.normal(k2, (C, C), jnp.float32) * s, 'b_proj': jnp.zeros((C,), jnp.float32)}
    _L2_attn_in = _L2_attn_setup()

    def _L2_ffn_setup():
        import jax, jax.numpy as jnp
        import numpy as np
        E = 32
        K = 4
        H = 128
        I = 96
        ROUTED_SCALING_FACTOR = 1.0
        key = jax.random.key(seed)
        k0, k1, k2, k3, k4, k5 = jax.random.split(key, 6)
        return {'hidden_states': jax.random.normal(k0, (1, 256, H), jnp.float32), 'gate_w': jax.random.normal(k1, (E, H), jnp.float32) * 0.02, 'w1': jax.random.normal(k2, (E, H, I), jnp.float32) * 0.02, 'w3': jax.random.normal(k3, (E, H, I), jnp.float32) * 0.02, 'w2': jax.random.normal(k4, (E, I, H), jnp.float32) * 0.02, 'e_bias': jax.random.normal(k5, (E,), jnp.float32) * 0.02}
    _L2_ffn_in = _L2_ffn_setup()

    def _L3_attn_setup():
        import jax, jax.numpy as jnp
        import numpy as np
        SEGMENT_LENGTH = 64
        DILATION_RATE = 4
        NUM_HEADS = 16
        HEAD_DIM = 64

        def dilated_mask(seq_len):
            pos = jnp.arange(seq_len)
            seg = pos // SEGMENT_LENGTH
            local = seg[None, :] == seg[:, None]
            diff = jnp.abs(pos[None, :] - pos[:, None])
            dil = (diff > 0) & (diff % DILATION_RATE == 0) & (diff <= DILATION_RATE * SEGMENT_LENGTH)
            allowed = local | dil
            return jnp.where(allowed, 0.0, -jnp.inf).astype(jnp.float32)
        key = jax.random.key(seed)
        ks = jax.random.split(key, 5)
        B, S, D = (2, 256, 128)
        scale = 1.0 / np.sqrt(D)
        return {'hidden_states': jax.random.normal(ks[0], (B, S, D), jnp.float32), 'w_q': jax.random.normal(ks[1], (D, NUM_HEADS * HEAD_DIM), jnp.float32) * scale, 'w_k': jax.random.normal(ks[2], (D, NUM_HEADS * HEAD_DIM), jnp.float32) * scale, 'w_v': jax.random.normal(ks[3], (D, NUM_HEADS * HEAD_DIM), jnp.float32) * scale, 'w_o': jax.random.normal(ks[4], (NUM_HEADS * HEAD_DIM, D), jnp.float32) * scale}
    _L3_attn_in = _L3_attn_setup()

    def _L3_ffn_setup():
        import jax, jax.numpy as jnp
        import numpy as np
        TOP_K = 4
        key = jax.random.key(seed)
        ks = jax.random.split(key, 5)
        B, T, D = (2, 128, 128)
        P, PD = (32, 32)
        return {'x': jax.random.normal(ks[0], (B, T, D), dtype=jnp.float32), 'hasher_w': jax.random.normal(ks[1], (PD, D), dtype=jnp.float32) * 0.03, 'keys': jax.random.normal(ks[2], (P, PD), dtype=jnp.float32) * 0.1, 'values_down': jax.random.normal(ks[3], (P, D, PD), dtype=jnp.float32) * 0.01, 'values_up': jax.random.normal(ks[4], (P, PD, D), dtype=jnp.float32) * 0.01, 'scale': jnp.full((1,), 0.1, dtype=jnp.float32)}
    _L3_ffn_in = _L3_ffn_setup()
    _d = {'L0_attn_x': _L0_attn_in['x'], 'L0_attn_Wq': _L0_attn_in['Wq'], 'L0_attn_bq': _L0_attn_in['bq'], 'L0_attn_Wdown': _L0_attn_in['Wdown'], 'L0_attn_bdown': _L0_attn_in['bdown'], 'L0_attn_Wup': _L0_attn_in['Wup'], 'L0_attn_bup': _L0_attn_in['bup'], 'L0_attn_Wout': _L0_attn_in['Wout'], 'L0_attn_bout': _L0_attn_in['bout'], 'L0_ffn_Ws': _L0_ffn_in['Ws'], 'L0_ffn_bs': _L0_ffn_in['bs'], 'L0_ffn_Wg': _L0_ffn_in['Wg'], 'L0_ffn_Wu': _L0_ffn_in['Wu'], 'L0_ffn_Wd': _L0_ffn_in['Wd'], 'L1_attn_W_in': _L1_attn_in['W_in'], 'L1_attn_conv_k': _L1_attn_in['conv_k'], 'L1_attn_conv_b': _L1_attn_in['conv_b'], 'L1_attn_W_x': _L1_attn_in['W_x'], 'L1_attn_W_dt': _L1_attn_in['W_dt'], 'L1_attn_b_dt': _L1_attn_in['b_dt'], 'L1_attn_A_log': _L1_attn_in['A_log'], 'L1_attn_D': _L1_attn_in['D'], 'L1_attn_W_out': _L1_attn_in['W_out'], 'L1_ffn_Wg': _L1_ffn_in['Wg'], 'L1_ffn_w1': _L1_ffn_in['w1'], 'L1_ffn_w2': _L1_ffn_in['w2'], 'L2_attn_W_qkv': _L2_attn_in['W_qkv'], 'L2_attn_b_qkv': _L2_attn_in['b_qkv'], 'L2_attn_W_proj': _L2_attn_in['W_proj'], 'L2_attn_b_proj': _L2_attn_in['b_proj'], 'L2_ffn_gate_w': _L2_ffn_in['gate_w'], 'L2_ffn_w1': _L2_ffn_in['w1'], 'L2_ffn_w3': _L2_ffn_in['w3'], 'L2_ffn_w2': _L2_ffn_in['w2'], 'L2_ffn_e_bias': _L2_ffn_in['e_bias'], 'L3_attn_w_q': _L3_attn_in['w_q'], 'L3_attn_w_k': _L3_attn_in['w_k'], 'L3_attn_w_v': _L3_attn_in['w_v'], 'L3_attn_w_o': _L3_attn_in['w_o'], 'L3_ffn_hasher_w': _L3_ffn_in['hasher_w'], 'L3_ffn_keys': _L3_ffn_in['keys'], 'L3_ffn_values_down': _L3_ffn_in['values_down'], 'L3_ffn_values_up': _L3_ffn_in['values_up'], 'L3_ffn_scale': _L3_ffn_in['scale']}
    _x0 = _d['L0_attn_x']
    _d['L0_attn_x'] = jax.random.normal(jax.random.fold_in(jax.random.key(seed), 1), (2, 1024, 128), dtype=_x0.dtype)
    del _x0
    return _d

def reference(L0_attn_x, L0_attn_Wq, L0_attn_bq, L0_attn_Wdown, L0_attn_bdown, L0_attn_Wup, L0_attn_bup, L0_attn_Wout, L0_attn_bout, L0_ffn_Ws, L0_ffn_bs, L0_ffn_Wg, L0_ffn_Wu, L0_ffn_Wd, L1_attn_W_in, L1_attn_conv_k, L1_attn_conv_b, L1_attn_W_x, L1_attn_W_dt, L1_attn_b_dt, L1_attn_A_log, L1_attn_D, L1_attn_W_out, L1_ffn_Wg, L1_ffn_w1, L1_ffn_w2, L2_attn_W_qkv, L2_attn_b_qkv, L2_attn_W_proj, L2_attn_b_proj, L2_ffn_gate_w, L2_ffn_w1, L2_ffn_w3, L2_ffn_w2, L2_ffn_e_bias, L3_attn_w_q, L3_attn_w_k, L3_attn_w_v, L3_attn_w_o, L3_ffn_hasher_w, L3_ffn_keys, L3_ffn_values_down, L3_ffn_values_up, L3_ffn_scale):

    def _L0_attn_ref(x, Wq, bq, Wdown, bdown, Wup, bup, Wout, bout):
        import jax, jax.numpy as jnp
        import numpy as np
        D_MODEL = 128
        N_HEADS = 16
        D_LATENT = 32
        HEAD_DIM = D_MODEL // N_HEADS

        def apply_rope(x):
            B, T, H, D = x.shape
            inv_freq = 1.0 / 10000.0 ** (jnp.arange(0, D, 2, dtype=jnp.float32) / D)
            t = jnp.arange(T, dtype=jnp.float32)
            freqs = t[:, None] * inv_freq[None, :]
            sin_f = jnp.sin(freqs)[None, :, None, :]
            cos_f = jnp.cos(freqs)[None, :, None, :]
            x1, x2 = jnp.split(x, 2, axis=-1)
            return jnp.concatenate([x1 * cos_f - x2 * sin_f, x1 * sin_f + x2 * cos_f], axis=-1)
        B, T, D = x.shape
        H, Dh = (N_HEADS, HEAD_DIM)
        q = x @ Wq + bq
        kv_latent = x @ Wdown + bdown
        kv = kv_latent @ Wup + bup
        q = q.reshape(B, T, H, Dh)
        kv = kv.reshape(B, T, H, 2 * Dh)
        k, v = jnp.split(kv, 2, axis=-1)
        q = apply_rope(q)
        k = apply_rope(k)
        att = jnp.einsum('bthd,btgd->bthg', q, k) / jnp.sqrt(jnp.float32(Dh))
        att = jax.nn.softmax(att, axis=-1)
        out = jnp.einsum('bthg,btgd->bthd', att, v)
        out = out.reshape(B, T, D)
        return out @ Wout + bout

    def _L0_ffn_ref(x, Ws, bs, Wg, Wu, Wd):
        import jax, jax.numpy as jnp
        import numpy as np
        D, F, E, K = (128, 344, 8, 2)
        b, n, d = x.shape
        xt = x.reshape(-1, d)
        logits = xt @ Ws + bs
        topk_w, topk_idx = jax.lax.top_k(logits, K)
        topk_w = jax.nn.softmax(topk_w, axis=-1)
        combine = jnp.sum(jax.nn.one_hot(topk_idx, E, dtype=xt.dtype) * topk_w[..., None], axis=1)
        g = jnp.einsum('td,edf->tef', xt, Wg)
        u = jnp.einsum('td,edf->tef', xt, Wu)
        h = jax.nn.silu(g) * u
        y = jnp.einsum('tef,efd->ted', h, Wd)
        out = jnp.einsum('ted,te->td', y, combine)
        return out.reshape(b, n, d)

    def _L1_attn_ref(x, W_in, conv_k, conv_b, W_x, W_dt, b_dt, A_log, D, W_out):
        import jax, jax.numpy as jnp
        import numpy as np
        B_, L, D_MODEL = (2, 256, 128)
        EXPAND, D_INNER, D_STATE, DT_RANK, D_CONV = (2, 256, 16, 64, 4)
        DT_MIN, DT_MAX = (0.001, 0.1)
        xz = x @ W_in
        xs, res = jnp.split(xz, 2, axis=-1)
        xc = jax.lax.conv_general_dilated(xs, conv_k, window_strides=(1,), padding=[(D_CONV - 1, 0)], dimension_numbers=('NWC', 'WIO', 'NWC'), feature_group_count=EXPAND) + conv_b
        u = jax.nn.silu(xc)
        dbc = u @ W_x
        dt_raw = dbc[..., :DT_RANK]
        Bm = dbc[..., DT_RANK:DT_RANK + D_STATE]
        Cm = dbc[..., DT_RANK + D_STATE:]
        delta = jax.nn.softplus(dt_raw @ W_dt + b_dt)
        delta = jnp.clip(delta, DT_MIN, DT_MAX)
        A = -jnp.exp(A_log)
        dA = jnp.exp(delta[..., None] * A)
        dBu = delta[..., None] * u[..., None] * Bm[:, :, None, :]

        def step(h, inp):
            dA_t, dBu_t, C_t = inp
            h = dA_t * h + dBu_t
            y_t = jnp.einsum('bdn,bn->bd', h, C_t)
            return (h, y_t)
        h0 = jnp.zeros((x.shape[0], D_INNER, D_STATE), dA.dtype)
        _, y = jax.lax.scan(step, h0, (dA.transpose(1, 0, 2, 3), dBu.transpose(1, 0, 2, 3), Cm.transpose(1, 0, 2)))
        y = y.transpose(1, 0, 2) + u * D
        out = y * jax.nn.silu(res) @ W_out
        return out

    def _L1_ffn_ref(x, Wg, w1, w2):
        import jax, jax.numpy as jnp
        import numpy as np
        d = x.shape[-1]
        xr = x.reshape(-1, d)
        S = xr.shape[0]
        E = Wg.shape[1]
        C = (S + E - 1) // E
        gate = jax.nn.softmax(xr @ Wg, axis=-1)
        idx = jnp.argmax(gate, axis=1)
        gates_s = jnp.take_along_axis(gate, idx[:, None], axis=1)[:, 0]
        onehot = jax.nn.one_hot(idx, E, dtype=jnp.int32)
        loc = jnp.sum((jnp.cumsum(onehot, axis=0) - 1) * onehot, axis=1)
        valid = loc < C
        loc_pad = jnp.minimum(loc, C)
        dispatched = jnp.zeros((E, C + 1, d), dtype=x.dtype).at[idx, loc_pad].set(xr)
        dispatched = dispatched[:, :C]
        h = jax.nn.relu(jnp.einsum('ecm,emf->ecf', dispatched, w1))
        expert_out = jnp.einsum('ecf,efm->ecm', h, w2)
        gathered = expert_out[idx, jnp.minimum(loc, C - 1)]
        combined = gathered * (gates_s * valid.astype(x.dtype))[:, None]
        return combined.reshape(x.shape)

    def _L2_attn_ref(x, W_qkv, b_qkv, W_proj, b_proj):
        import jax, jax.numpy as jnp
        import numpy as np
        B, L, C, H = (8, 128, 128, 16)
        Bb, Ll, Cc = x.shape
        d = Cc // H
        qkv = x @ W_qkv + b_qkv
        q, k, v = jnp.split(qkv, 3, axis=2)
        q = q.reshape(Bb, Ll, H, d).transpose(0, 2, 1, 3)
        k = k.reshape(Bb, Ll, H, d).transpose(0, 2, 1, 3)
        v = v.reshape(Bb, Ll, H, d).transpose(0, 2, 1, 3)
        scale = 1.0 / np.sqrt(d).astype(np.float32)
        attn = jnp.einsum('bhid,bhjd->bhij', q, k) * scale
        causal = jnp.tril(jnp.ones((Ll, Ll), dtype=bool))
        attn = jnp.where(causal[None, None, :, :], attn, -jnp.inf)
        attn = jax.nn.softmax(attn, axis=2)
        y = jnp.einsum('bhij,bhjd->bhid', attn, v)
        y = y.transpose(0, 2, 1, 3).reshape(Bb, Ll, Cc)
        return y @ W_proj + b_proj

    def _L2_ffn_ref(hidden_states, gate_w, w1, w3, w2, e_bias):
        import jax, jax.numpy as jnp
        import numpy as np
        E = 32
        K = 4
        H = 128
        I = 96
        ROUTED_SCALING_FACTOR = 1.0
        orig_shape = hidden_states.shape
        x = hidden_states.reshape(-1, orig_shape[-1])
        T = x.shape[0]
        router_logits = x @ gate_w.T
        scores = jax.nn.sigmoid(router_logits.astype(jnp.float32))
        _, topk_ids = jax.lax.top_k(scores + e_bias[None, :], K)
        topk_w = jnp.take_along_axis(scores, topk_ids, axis=1)
        topk_w = topk_w / jnp.sum(topk_w, axis=1, keepdims=True)
        combine = jnp.zeros((T, E), jnp.float32).at[jnp.arange(T)[:, None], topk_ids].add(topk_w)
        g = jnp.einsum('th,ehi->tei', x, w1)
        u = jnp.einsum('th,ehi->tei', x, w3)
        a = jax.nn.silu(g) * u * combine[:, :, None].astype(x.dtype)
        out = jnp.einsum('tei,eih->th', a, w2)
        out = out * ROUTED_SCALING_FACTOR
        return out.reshape(orig_shape)

    def _L3_attn_ref(hidden_states, w_q, w_k, w_v, w_o):
        import jax, jax.numpy as jnp
        import numpy as np
        SEGMENT_LENGTH = 64
        DILATION_RATE = 4
        NUM_HEADS = 16
        HEAD_DIM = 64

        def dilated_mask(seq_len):
            pos = jnp.arange(seq_len)
            seg = pos // SEGMENT_LENGTH
            local = seg[None, :] == seg[:, None]
            diff = jnp.abs(pos[None, :] - pos[:, None])
            dil = (diff > 0) & (diff % DILATION_RATE == 0) & (diff <= DILATION_RATE * SEGMENT_LENGTH)
            allowed = local | dil
            return jnp.where(allowed, 0.0, -jnp.inf).astype(jnp.float32)
        B, S, D = hidden_states.shape
        H, Dh = (NUM_HEADS, HEAD_DIM)
        scaling = Dh ** (-0.5)
        q = (hidden_states @ w_q).reshape(B, S, H, Dh)
        k = (hidden_states @ w_k).reshape(B, S, H, Dh)
        v = (hidden_states @ w_v).reshape(B, S, H, Dh)
        mask = dilated_mask(S)
        scores = jnp.einsum('bqhd,bkhd->bhqk', q, k) * scaling + mask[None, None]
        attn = jax.nn.softmax(scores.astype(jnp.float32), axis=-1).astype(q.dtype)
        out = jnp.einsum('bhqk,bkhd->bqhd', attn, v).reshape(B, S, H * Dh)
        return out @ w_o

    def _L3_ffn_ref(x, hasher_w, keys, values_down, values_up, scale):
        import jax, jax.numpy as jnp
        import numpy as np
        TOP_K = 4
        h = jnp.einsum('btd,pd->btp', x, hasher_w)
        sim = jnp.einsum('btp,np->btn', h, keys)
        vals, idx = jax.lax.top_k(sim, TOP_K)
        w = jax.nn.softmax(vals, axis=-1)
        out = jnp.zeros_like(x)
        for k in range(TOP_K):
            ik = idx[..., k]
            vd = values_down[ik]
            vu = values_up[ik]
            proj = jax.nn.silu(jnp.einsum('btd,btdp->btp', x, vd))
            o = jnp.einsum('btp,btpd->btd', proj, vu)
            out = out + o * w[..., k:k + 1]
        return x + out * scale
    x = L0_attn_x
    xn = _layernorm(x, axis=-1)
    x = x + _L0_attn_ref(xn, L0_attn_Wq, L0_attn_bq, L0_attn_Wdown, L0_attn_bdown, L0_attn_Wup, L0_attn_bup, L0_attn_Wout, L0_attn_bout) + _L0_ffn_ref(xn, L0_ffn_Ws, L0_ffn_bs, L0_ffn_Wg, L0_ffn_Wu, L0_ffn_Wd)
    xn = _layernorm(x, axis=-1)
    x = x + _L1_attn_ref(xn, L1_attn_W_in, L1_attn_conv_k, L1_attn_conv_b, L1_attn_W_x, L1_attn_W_dt, L1_attn_b_dt, L1_attn_A_log, L1_attn_D, L1_attn_W_out) + _L1_ffn_ref(xn, L1_ffn_Wg, L1_ffn_w1, L1_ffn_w2)
    xn = _layernorm(x, axis=-1)
    x = x + _L2_attn_ref(xn, L2_attn_W_qkv, L2_attn_b_qkv, L2_attn_W_proj, L2_attn_b_proj) + _L2_ffn_ref(xn, L2_ffn_gate_w, L2_ffn_w1, L2_ffn_w3, L2_ffn_w2, L2_ffn_e_bias)
    xn = _layernorm(x, axis=-1)
    x = x + _L3_attn_ref(xn, L3_attn_w_q, L3_attn_w_k, L3_attn_w_v, L3_attn_w_o) + _L3_ffn_ref(xn, L3_ffn_hasher_w, L3_ffn_keys, L3_ffn_values_down, L3_ffn_values_up, L3_ffn_scale)
    return x

_drawn_inputs = setup_inputs


def setup_inputs(seed=0):
    import zlib

    import numpy as np

    out = dict(_drawn_inputs(seed))
    spreads = {'L0_attn_bq': (0.0, 0.27),
     'L0_attn_bdown': (0.0, 0.1),
     'L0_attn_bup': (0.0, 0.1),
     'L0_attn_bout': (0.0, 0.1),
     'L0_ffn_bs': (0.0, 0.8),
     'L1_attn_conv_b': (0.0, 0.1),
     'L1_attn_b_dt': (0.0, 2.0),
     'L1_attn_D': (1.0, 0.2),
     'L2_attn_b_qkv': (0.0, 0.8),
     'L2_attn_b_proj': (0.0, 0.421)}
    factors = {'L0_ffn_Ws': 8.0,
     'L0_ffn_Wg': 8.0,
     'L0_ffn_Wu': 8.0,
     'L0_ffn_Wd': 8.0,
     'L1_attn_W_dt': 8.0,
     'L1_ffn_Wg': 8.0,
     'L1_ffn_w1': 8.0,
     'L1_ffn_w2': 8.0,
     'L2_attn_W_qkv': 27.141,
     'L2_ffn_gate_w': 8.0,
     'L2_ffn_w1': 8.0,
     'L2_ffn_w3': 8.0,
     'L2_ffn_w2': 8.0,
     'L2_ffn_e_bias': 8.0,
     'L3_ffn_hasher_w': 64.0,
     'L3_ffn_keys': 64.0,
     'L3_ffn_values_down': 64.0,
     'L3_ffn_values_up': 64.0,
     'L2_attn_W_proj': 4.665}
    for name, (base, spread) in spreads.items():
        noise = np.random.default_rng([zlib.crc32(name.encode()), seed]).standard_normal(out[name].shape)
        drawn = base * np.exp(spread * noise) if base else spread * noise
        out[name] = jnp.asarray(drawn.astype(out[name].dtype))
    for name, factor in factors.items():
        out[name] = (out[name] * factor).astype(out[name].dtype)
    return out
```

```python
from contextlib import ExitStack

import numpy as np

import concourse.bass as bass
from concourse import mybir

F32 = mybir.dt.float32
BF16 = mybir.dt.bfloat16
U32 = mybir.dt.uint32
ALU = mybir.AluOpType
ACT = mybir.ActivationFunctionType
AX = mybir.AxisListType

P = 128
D = 128
B = 2
T = 1024
NT = B * T
TILES = NT // P
CH = 512
NCH = NT // CH
EPS = 1e-5

SPLIT_Q = (0, 0, 0, 1, 1, 2)
SPLIT_K = (0, 1, 2, 0, 1, 0)


class Count:

    def __init__(self, sem, base=0):
        self.sem, self.base, self.n = sem, base, 0

    def inc(self, instruction):
        instruction.then_inc(self.sem, 1)
        self.n += 1
        return self.base + self.n

    def wait(self, engine):
        engine.wait_ge(self.sem, self.base + self.n)


class Tensors:
    pass


def open_scope(nc, g=None):
    s = Tensors()
    s.count = 0
    if g is not None:
        g.count += 1
    tag = f"_{g.count}" if g is not None else ""
    s.ctx = ExitStack()
    s.sb = lambda name, shape, dt=F32: s.ctx.enter_context(nc.sbuf_tensor(name + tag, shape, dt))

    def sem(name):
        handle = s.ctx.enter_context(nc.semaphore(name + tag))
        if g is not None:
            g.used.append(handle)
        return handle
    s.sem = sem
    s.used = []
    return s


def clear_semaphores(nc, semaphores):
    numbers = sorted(sem.num for sem in semaphores)
    with nc.Block() as block:

        @block.gpsimd
        def _(pool):
            while numbers:
                first = last = numbers.pop(0)
                while numbers and numbers[0] <= last + 1:
                    last = numbers.pop(0)
                pool.sem_clear(range(first, last + 1))


def setup(nc, g, A):
    s = open_scope(nc, g)
    with s.ctx:
        loaded = s.sem("setup_loaded")
        copied = s.sem("setup_copied")
        block = s.ctx.enter_context(nc.Block())

        @block.sync
        def _(sp):
            sp.dma_start(g.x[:], A["x"].rearrange("(i p) d -> p i d", p=P)).then_inc(loaded, 16)
            sp.dma_start(g.ident[:], A["ident"]).then_inc(loaded, 16)
            sp.wait_ge(loaded, 32)

        @block.vector
        def _(dve):
            dve.wait_ge(loaded, 32)
            nc.vector.tensor_copy(g.identb[:], g.ident[:]).then_inc(copied, 1)
            dve.wait_ge(copied, 1)


def residual_norm(nc, g, first, last):
    s = open_scope(nc, g)
    ps = g.ps
    with s.ctx:
        stats = s.sb("ln_stats", [P, TILES, 6])
        mv = s.sb("ln_mv", [P, TILES, 2])
        std = s.sb("ln_std", [P, TILES])
        rstd = s.sb("ln_rstd", [P, TILES])
        xn = g.xn
        turned = s.sem("ln_turned")
        added = s.sem("ln_added")
        ve = s.sem("ln_vector_done")
        have_std = s.sem("ln_have_std")
        normed = s.sem("ln_normed")
        xturned = s.sem("ln_xturned")
        xcopied = s.sem("ln_xcopied")
        block = s.ctx.enter_context(nc.Block())

        @block.tensor
        def _(pe):
            if not first:
                for q in range(4):
                    for k in range(4):
                        i = 4 * q + k
                        mm = nc.tensor.transpose(ps[:, q, k * P:(k + 1) * P], g.branchT[:, i * P:(i + 1) * P], g.ident[:])
                    mm.then_inc(turned, 1)
            if not last:
                for q in range(4):
                    pe.wait_ge(normed, q + 1)
                    for k in range(4):
                        i = 4 * q + k
                        mm = nc.tensor.transpose(ps[:, 4 + q, k * P:(k + 1) * P], xn[:, i, :], g.ident[:])
                    mm.then_inc(xturned, 1)

        @block.vector
        def _(dve):
            if not first:
                for q in range(4):
                    dve.wait_ge(turned, q + 1)
                    nc.vector.tensor_tensor(g.x[:, 4 * q:4 * q + 4, :], g.x[:, 4 * q:4 * q + 4, :],
                                            ps[:, q, :].rearrange("p (k d) -> p k d", d=D), ALU.add).then_inc(added, 1)
            if last:
                dve.wait_ge(added, 4)
                return
            done = Count(ve)
            for i in range(TILES):
                if not first:
                    dve.wait_ge(added, i // 4 + 1)
                done.inc(nc.vector.bn_stats(stats[:, i, :], g.x[:, i, :]))
            done.wait(dve)
            for i in range(TILES):
                done.inc(nc.vector.bn_aggr(mv[:, i, :], stats[:, i, :]))
            done.wait(dve)
            done.inc(nc.vector.tensor_scalar(mv[:, :, 1], mv[:, :, 1], EPS, None, ALU.add))
            dve.wait_ge(have_std, 1)
            done.inc(nc.vector.reciprocal(rstd[:], std[:]))
            done.wait(dve)
            for i in range(TILES):
                op = nc.vector.tensor_scalar(xn[:, i, :], g.x[:, i, :], mv[:, i, 0:1], rstd[:, i:i + 1],
                                             ALU.subtract, ALU.mult)
                if i % 4 == 3:
                    op.then_inc(normed, 1)
            for q in range(0, 4, 2):
                dve.wait_ge(xturned, q + 1)
                nc.vector.tensor_copy(g.xnT[:, q * CH:(q + 1) * CH], ps[:, 4 + q, :]).then_inc(xcopied, 1)
            dve.wait_ge(xcopied, 4)

        @block.scalar
        def _(act):
            if last:
                return
            act.wait_ge(ve, 2 * TILES + 1)
            nc.scalar.activation(std[:], mv[:, :, 1], ACT.Sqrt).then_inc(have_std, 1)
            for q in range(1, 4, 2):
                act.wait_ge(xturned, q + 1)
                nc.scalar.copy(g.xnT[:, q * CH:(q + 1) * CH], ps[:, 4 + q, :]).then_inc(xcopied, 1)


def finish(nc, g, out):
    s = open_scope(nc, g)
    with s.ctx:
        stored = s.sem("x_stored")
        block = s.ctx.enter_context(nc.Block())

        @block.sync
        def _(sp):
            sp.dma_start(out.rearrange("(i p) d -> p i d", p=P), g.x[:]).then_inc(stored, 16)
            sp.wait_ge(stored, 16)


HEADS, HD = 16, 8


def head_mixing(nc, g, W):
    s = open_scope(nc, g)
    ps = g.ps
    scale = float(HD) ** -0.5
    HH = HEADS // 2
    with s.ctx:
        wq = s.sb("wq", [P, 2, P])
        wup = s.sb("wup", [32, 3, P])
        wdown = s.sb("wdown", [P, 32])
        bdown = s.sb("bdown", [32, 1])
        bias = s.sb("bias", [P, 5, P])
        cos = s.sb("cos", [P, T // P, HD])
        sin = s.sb("sin", [P, T // P, HD])
        wout = s.sb("wout", [P, P])
        bout = s.sb("bout", [P, 1])
        xs = s.sb("xs", [P, 2, P])
        lat = s.sb("lat", [32, 2, P])
        proj = s.sb("proj", [P, 2, 5, P])
        rc = s.sb("rc", [P, 2, 2, P])
        rs = s.sb("rs", [P, 2, 2, P])
        qk = s.sb("qk", [P, 2, 2, P])
        prod = s.sb("prod", [P, 2, HEADS, HEADS, HD])
        att = s.sb("att", [P, 2, HEADS, HEADS])
        top = s.sb("top", [P, 2, HEADS])
        less = s.sb("less", [P, 2, HEADS, HEADS])
        prob = s.sb("prob", [P, 2, HEADS, HEADS])
        total = s.sb("total", [P, 2, HEADS])
        inv = s.sb("inv", [P, 2, HEADS])
        mixed = s.sb("mixed", [P, 2, HEADS, HD])
        norm = s.sb("norm", [P, 2, P])
        oT = s.sb("oT", [P, 2, P])
        loaded = s.sem("hm_loaded")
        staged = s.sem("hm_x_staged")
        latd = s.sem("hm_latent")
        latc = s.sem("hm_latent_copied")
        projd = s.sem("hm_projected")
        biased = s.sem("hm_biased")
        roped = s.sem("hm_roped")
        multd = s.sem("hm_scores_mult_dve")
        multp = s.sem("hm_scores_mult_pool")
        vec = s.sem("hm_vector_steps")
        expd = s.sem("hm_exp")
        wmd = s.sem("hm_weigh_mult_dve")
        wmp = s.sem("hm_weigh_mult_pool")
        normd = s.sem("hm_normal")
        turned = s.sem("hm_turned")
        tcopied = s.sem("hm_turned_copied")
        outd = s.sem("hm_out")
        outc = s.sem("hm_out_copied")
        block = s.ctx.enter_context(nc.Block())
        tiles = dict(wq=wq, wup=wup, wdown=wdown, bdown=bdown, bias=bias, cos=cos, sin=sin, wout=wout, bout=bout)
        ALL = 16 * len(tiles)
        VS = 7

        @block.sync
        def _(sp):
            for n, t in tiles.items():
                sp.dma_start(t[:], W[n]).then_inc(loaded, 16)
            sp.wait_ge(loaded, ALL)

        @block.scalar
        def _(act):
            act.wait_ge(loaded, ALL)
            with act.Fori(0, TILES // 2) as i:
                for e in range(2):
                    act.wait_ge(projd, i * 2 + e)
                    nc.scalar.copy(xs[:, e, :], g.xnT[:, bass.ds((i * 2 + e) * P, P)]).then_inc(staged, 1)
                    act.wait_ge(latd, i * 2 + e + 1)
                    nc.scalar.activation(lat[:, e, :], ps[0:32, 4 + e, 256:384], ACT.Identity, bias=bdown[:]).then_inc(latc, 1)
                for e in range(2):
                    act.wait_ge(vec, i * 2 * VS + (4 * (e + 1)))
                    act.wait_ge(wmd, i * 2)
                    act.wait_ge(wmp, i * 2)
                    nc.scalar.activation(prob[:, e], less[:, e], ACT.Exp, scale=scale).then_inc(expd, 1)
                for e in range(2):
                    act.wait_ge(turned, i * 2 + e + 1)
                    nc.scalar.copy(oT[:, e, :], ps[:, 4 + e, 0:P]).then_inc(tcopied, 1)
                for e in range(2):
                    act.wait_ge(outd, i * 2 + e + 1)
                    nc.scalar.activation(g.branchT[:, bass.ds((i * 2 + e) * P, P)], ps[:, 6 + e, 0:P], ACT.Identity,
                                         bias=bout[:]).then_inc(outc, 1)
            act.wait_ge(outc, TILES)

        @block.tensor
        def _(pe):
            pe.wait_ge(loaded, ALL)
            with pe.Fori(0, TILES // 2) as i:
                for e in range(2):
                    pe.wait_ge(staged, i * 2 + e + 1)
                    pe.wait_ge(biased, i * 2)
                    nc.tensor.matmul(ps[0:32, 4 + e, 256:384], wdown[:], xs[:, e, :], start=True, stop=True).then_inc(latd, 1)
                    nc.tensor.matmul(ps[:, e, 0:256], xs[:, e, :], wq[:].rearrange("p a n -> p (a n)"), start=True, stop=True)
                    pe.wait_ge(latc, i * 2 + e + 1)
                    nc.tensor.matmul(ps[:, 2 + e, 0:384], lat[:, e, :], wup[:].rearrange("p a n -> p (a n)"),
                                     start=True, stop=True).then_inc(projd, 1)
                for e in range(2):
                    pe.wait_ge(normd, i * 2 + e + 1)
                    nc.tensor.transpose(ps[:, 4 + e, 0:P], norm[:, e, :], g.ident[:]).then_inc(turned, 1)
                for e in range(2):
                    pe.wait_ge(tcopied, i * 2 + e + 1)
                    nc.tensor.matmul(ps[:, 6 + e, 0:P], wout[:], oT[:, e, :], start=True, stop=True).then_inc(outd, 1)

        def scores_product(eng, e, h0):
            q = qk[:, e, 0, :].rearrange("p (h d) -> p h d", d=HD)[:, h0:h0 + HH, None, :].to_broadcast([P, HH, HEADS, HD])
            k = qk[:, e, 1, :].rearrange("p (g d) -> p g d", d=HD)[:, None, :, :].to_broadcast([P, HH, HEADS, HD])
            return eng.tensor_tensor(prod[:, e, h0:h0 + HH], q, k, ALU.mult)

        def weigh_product(eng, e, h0):
            a = prob[:, e, h0:h0 + HH, None, :].to_broadcast([P, HH, HD, HEADS])
            v = proj[:, e, 4, :].rearrange("p (g d) -> p d g", d=HD)[:, None, :, :].to_broadcast([P, HH, HD, HEADS])
            dst = prod[:, e, h0:h0 + HH].rearrange("p h g d -> p h (g d)").rearrange("p h (d g) -> p h d g", g=HEADS)
            return eng.tensor_tensor(dst, a, v, ALU.mult)

        @block.gpsimd
        def _(pool):
            pool.wait_ge(loaded, ALL)
            with pool.Fori(0, TILES // 2) as i:
                for e in range(2):
                    n = (i * 2 + e) * 3
                    pool.wait_ge(biased, i * 2 + e + 1)
                    where = bass.ds((i * 2 + e) % (T // P), 1)
                    c = cos[:, where, :].to_broadcast([P, HEADS, HD])
                    sn = sin[:, where, :].to_broadcast([P, HEADS, HD])
                    v = lambda t: t.rearrange("p (h d) -> p h d", d=HD)
                    for j in range(2):
                        nc.gpsimd.tensor_tensor(v(rc[:, e, j, :]), v(proj[:, e, 2 * j, :]), c, ALU.mult)
                        last = nc.gpsimd.tensor_tensor(v(rs[:, e, j, :]), v(proj[:, e, 2 * j + 1, :]), sn, ALU.mult)
                    last.then_inc(roped, 1)
                    pool.wait_ge(roped, n + 1)
                    pool.wait_ge(multd, i * 2)
                    nc.gpsimd.tensor_tensor(qk[:, e], rc[:, e], rs[:, e], ALU.add).then_inc(roped, 1)
                    pool.wait_ge(roped, n + 2)
                    pool.wait_ge(vec, i * 2 * VS)
                    scores_product(nc.gpsimd, e, HH).then_inc(roped, 1)
                    pool.wait_ge(roped, n + 3)
                    pool.sem_inc(multp, 1)
                for e in range(2):
                    pool.wait_ge(expd, i * 2 + e + 1)
                    weigh_product(nc.gpsimd, e, HH).then_inc(wmp, 1)

        @block.vector
        def _(dve):
            dve.wait_ge(loaded, ALL)
            with dve.Fori(0, TILES // 2) as i:
                for e in range(2):
                    dve.wait_ge(projd, i * 2 + e + 1)
                    dve.wait_ge(wmp, i * 2)
                    nc.vector.tensor_tensor(proj[:, e, 0:2, :], ps[:, e, 0:256].rearrange("p (a n) -> p a n", a=2), bias[:, 0:2, :], ALU.add)
                    nc.vector.tensor_tensor(proj[:, e, 2:5, :], ps[:, 2 + e, 0:384].rearrange("p (a n) -> p a n", a=3), bias[:, 2:5, :],
                                            ALU.add).then_inc(biased, 1)
                base = i * 2 * VS
                for e in range(2):
                    n = base + 4 * e
                    dve.wait_ge(roped, (i * 2 + e) * 3 + 2)
                    scores_product(nc.vector, e, 0).then_inc(multd, 1)
                    dve.wait_ge(multd, i * 2 + e + 1)
                    dve.wait_ge(multp, i * 2 + e + 1)
                    nc.vector.tensor_reduce(att[:, e].rearrange("p h g -> p (h g)"), prod[:, e].rearrange("p h g d -> p (h g) d"),
                                            AX.X, ALU.add).then_inc(vec, 1)
                    dve.wait_ge(vec, n + 1)
                    nc.vector.tensor_reduce(top[:, e], att[:, e], AX.X, ALU.max).then_inc(vec, 1)
                    dve.wait_ge(vec, n + 2)
                    nc.vector.tensor_tensor(less[:, e], att[:, e], top[:, e, :, None].to_broadcast([P, HEADS, HEADS]),
                                            ALU.subtract).then_inc(vec, 2)
                for e in range(2):
                    n = base + 8 + 3 * e
                    dve.wait_ge(expd, i * 2 + e + 1)
                    nc.vector.tensor_reduce(total[:, e], prob[:, e], AX.X, ALU.add).then_inc(vec, 1)
                    weigh_product(nc.vector, e, 0).then_inc(wmd, 1)
                    dve.wait_ge(vec, n + 1)
                    nc.vector.reciprocal(inv[:, e], total[:, e]).then_inc(vec, 1)
                    dve.wait_ge(wmd, i * 2 + e + 1)
                    dve.wait_ge(wmp, i * 2 + e + 1)
                    nc.vector.tensor_reduce(mixed[:, e].rearrange("p h d -> p (h d)"),
                                            prod[:, e].rearrange("p h g d -> p h (g d)").rearrange("p h (d g) -> p (h d) g", g=HEADS),
                                            AX.X, ALU.add).then_inc(vec, 1)
                    dve.wait_ge(vec, n + 3)
                    dve.wait_ge(turned, i * 2)
                    nc.vector.tensor_tensor(norm[:, e, :].rearrange("p (h d) -> p h d", d=HD), mixed[:, e],
                                            inv[:, e, :, None].to_broadcast([P, HEADS, HD]), ALU.mult).then_inc(normd, 1)


def split_qk(nc, g, qk, W, qscale):
    s = open_scope(nc, g)
    ps = g.ps
    with s.ctx:
        wqk = s.sb("wqk", [P, 2, P])
        bias = s.sb("qk_bias", [P, 2])
        whole = s.sb("whole", [P, 2, CH])
        rest = s.sb("rest", [P, 2, CH])
        parts = s.sb("parts", [P, 2, 3, CH], BF16)
        loaded = s.sem("qk_loaded")
        product = s.sem("qk_product")
        wholed = s.sem("qk_whole")
        hi_done = s.sem("hi_done")
        rest_done = s.sem("rest_done")
        mid_done = s.sem("mid_done")
        lo_done = s.sem("lo_done")
        stored = [s.sem(f"parts_stored{j}") for j in range(2)]
        block = s.ctx.enter_context(nc.Block())

        @block.sync
        def _(sp):
            sp.dma_start(wqk[:], W["wqk"]).then_inc(loaded, 16)
            sp.dma_start(bias[:], W["bqk"]).then_inc(loaded, 16)
            with sp.Fori(0, NCH) as c:
                for j in range(2):
                    sp.wait_ge(lo_done, c * 2 + (j + 1))
                    dst = qk[j].rearrange("s p n -> p s n")[:, :, bass.ds(c * CH, CH)]
                    sp.dma_start(dst, parts[:, j, :, :]).then_inc(stored[j], 16)
            for j in range(2):
                sp.wait_ge(stored[j], 16 * NCH)

        @block.tensor
        def _(pe):
            pe.wait_ge(loaded, 32)
            with pe.Fori(0, NCH) as c:
                for j in range(2):
                    pe.wait_ge(wholed, c * 2 + j)
                    nc.tensor.matmul(ps[:, j, :], wqk[:, j, :], g.xnT[:, bass.ds(c * CH, CH)],
                                     start=True, stop=True).then_inc(product, 1)

        @block.scalar
        def _(act):
            with act.Fori(0, NCH) as c:
                for j in range(2):
                    act.wait_ge(wholed, c * 2 + (j + 1))
                    act.wait_ge(stored[j], c * 16)
                    nc.scalar.copy(parts[:, j, 0, :], whole[:, j, :]).then_inc(hi_done, 1)
                    act.wait_ge(rest_done, c * 2 + (j + 1))
                    nc.scalar.copy(parts[:, j, 1, :], rest[:, j, :]).then_inc(mid_done, 1)

        @block.vector
        def _(dve):
            dve.wait_ge(loaded, 32)
            with dve.Fori(0, NCH) as c:
                for j in range(2):
                    dve.wait_ge(product, c * 2 + (j + 1))
                    dve.wait_ge(lo_done, c * 2 + j)
                    nc.vector.tensor_scalar(whole[:, j, :], ps[:, j, :], bias[:, j:j + 1], qscale if j == 0 else 1.0,
                                            ALU.add, ALU.mult).then_inc(wholed, 1)
                    dve.wait_ge(hi_done, c * 2 + (j + 1))
                    nc.vector.tensor_tensor(rest[:, j, :], whole[:, j, :], parts[:, j, 0, :], ALU.subtract).then_inc(rest_done, 1)
                    dve.wait_ge(mid_done, c * 2 + (j + 1))
                    nc.vector.tensor_tensor(parts[:, j, 2, :], rest[:, j, :], parts[:, j, 1, :], ALU.subtract).then_inc(lo_done, 1)


def value_tiles(nc, g, Vp, W):
    s = open_scope(nc, g)
    with s.ctx:
        wv = s.sb("wv", [P, P])
        bv = s.sb("bv", [P, P])
        loaded = s.sem("v_loaded")
        product = s.sem("v_product")
        written = s.sem("v_written")
        block = s.ctx.enter_context(nc.Block())

        @block.sync
        def _(sp):
            sp.dma_start(wv[:], W["wv"]).then_inc(loaded, 16)
            sp.dma_start(bv[:], W["bv"]).then_inc(loaded, 16)
            sp.wait_ge(loaded, 32)

        @block.tensor
        def _(pe):
            pe.wait_ge(loaded, 32)
            for i in range(TILES):
                mm = nc.tensor.matmul(g.ps[:, i // 4, (i % 4) * P:(i % 4 + 1) * P], g.xnT[:, i * P:(i + 1) * P], wv[:],
                                      start=True, stop=True)
                if i % 4 == 3:
                    mm.then_inc(product, 1)

        @block.vector
        def _(dve):
            dve.wait_ge(loaded, 32)
            for q in range(TILES // 4):
                dve.wait_ge(product, q + 1)
                nc.vector.tensor_tensor(Vp[:, 4 * q:4 * q + 4, :], g.ps[:, q, :].rearrange("p (i n) -> p i n", n=P),
                                        bv[:, None, :].to_broadcast([P, 4, P]), ALU.add).then_inc(written, 1)
            dve.wait_ge(written, TILES // 4)


STACK = HD * len(SPLIT_Q)
QUAD = 4
STEPS = B * HEADS // QUAD
KT = T // P


def stage_heads(sp, nc, qk, Q, K, n, landed):
    b, h0 = n // 4, (n % 4) * 4
    for dst, which, terms in ((Q, 0, SPLIT_Q), (K, 1, SPLIT_K)):
        src = qk[which].rearrange("s (h j) n -> s j h n", j=HD)
        for t, part in enumerate(terms):
            sp.dma_start(dst[HD * t:HD * (t + 1), :, :],
                         src[part][:, bass.ds(h0, 4), bass.ds(b * T, T)]).then_inc(landed, 16)


def column_softmax_attention(nc, g, qk, Vp, W):
    s = open_scope(nc, g)
    ps = g.ps
    AV = 6
    UN = KT * QUAD
    RING = 3
    PR = 8
    with s.ctx:
        Q = [s.sb(f"Q{i}", [P, QUAD, T], BF16) for i in range(2)]
        K = [s.sb(f"K{i}", [P, QUAD, T], BF16) for i in range(2)]
        V = [s.sb(f"V{i}", [P, KT, QUAD, HD]) for i in range(2)]
        probs = s.sb("probs", [P, PR, T])
        negmax = s.sb("negmax", [P, PR])
        total = s.sb("total", [P, PR])
        inv = s.sb("inv", [P, 2, QUAD])
        vdiv = s.sb("vdiv", [P, 2, QUAD, 32])
        outT = s.sb("outT", [P, 4, NT])
        mask = s.sb("mask", [P, P])
        maskb = s.sb("maskb", [P, P], BF16)
        wout = s.sb("wout", [P, 4, P])
        bout = s.sb("bout", [P, 1])
        const = s.sem("ca_const")
        cleared = s.sem("ca_cleared")
        vcleared = s.sem("ca_v_cleared")
        maskd = s.sem("ca_mask")
        landed = [s.sem(f"ca_landed{i}") for i in range(2)]
        vstaged = s.sem("ca_v_staged")
        sc = s.sem("ca_scores")
        mx = s.sem("ca_max")
        ex = s.sem("ca_exp")
        invd = s.sem("ca_inverse")
        vd = s.sem("ca_v_divided")
        av = s.sem("ca_weighed")
        oc = s.sem("ca_out_copied")
        oproj = s.sem("ca_projected")
        ocopy = s.sem("ca_projected_copied")
        block = s.ctx.enter_context(nc.Block())

        @block.sync
        def _(sp):
            sp.dma_start(mask[:], W["mask"]).then_inc(const, 16)
            sp.dma_start(wout[:], W["wout"]).then_inc(const, 16)
            sp.dma_start(bout[:], W["bout"]).then_inc(const, 16)
            sp.wait_ge(cleared, 4)
            for e in range(2):
                stage_heads(sp, nc, qk, Q[e], K[e], e, landed[e])
            with sp.Fori(0, STEPS // 2 - 1) as i:
                for e in range(2):
                    sp.wait_ge(sc, i * 2 * UN + (e + 1) * UN)
                    stage_heads(sp, nc, qk, Q[e], K[e], i * 2 + (e + 2), landed[e])
            sp.wait_ge(const, 48)
            for e in range(2):
                sp.wait_ge(landed[e], 16 * 12 * STEPS // 2)

        @block.gpsimd
        def _(pool):
            nc.gpsimd.memset(vdiv[:], 0.0).then_inc(vcleared, 1)
            pool.wait_ge(vcleared, 1)

            def stage_v(n, e):
                nc.gpsimd.tensor_copy(V[e][:], Vp[:, bass.ds((n // 4) * KT, KT), bass.ds((n % 4) * QUAD * HD, QUAD * HD)]
                                      .rearrange("p i (h d) -> p i h d", d=HD)).then_inc(vstaged, 1)

            def divide(n, e):
                for jt in range(KT):
                    pool.wait_ge(invd, n * KT + (jt + 1))
                    pool.wait_ge(vstaged, n + 1)
                    pool.wait_ge(av, n * KT + max(jt - 1, 0))
                    nc.gpsimd.tensor_tensor(vdiv[:, jt % 2, :, 0:HD], V[e][:, jt],
                                            inv[:, jt % 2, :, None].to_broadcast([P, QUAD, HD]), ALU.mult).then_inc(vd, 1)

            for e in range(2):
                nc.gpsimd.tensor_copy(V[e][:], Vp[:, 0:KT, e * QUAD * HD:(e + 1) * QUAD * HD]
                                      .rearrange("p i (h d) -> p i h d", d=HD)).then_inc(vstaged, 1)
            with pool.Fori(0, STEPS // 2 - 1) as i:
                for e in range(2):
                    divide(i * 2 + e, e)
                    pool.wait_ge(vd, i * 2 * KT + (e + 1) * KT)
                    stage_v(i * 2 + (e + 2), e)
            for e in range(2):
                divide(STEPS - 2 + e, e)

        @block.tensor
        def _(pe):
            def scores(n, e, rnd, u):
                jt, h = u // QUAD, u % QUAD
                if u == 0:
                    pe.wait_ge(landed[e], rnd * 192 + 192)
                if u >= RING:
                    pe.wait_ge(ex, n * UN + (u - RING + 1))
                else:
                    pe.wait_ge(ex, n * UN)
                bank = 2 * (u % RING)
                for half in range(2):
                    a, b = max(jt * P, half * CH), (half + 1) * CH
                    if a >= b:
                        continue
                    diag = jt // 4 == half
                    mm = nc.tensor.matmul(ps[:, bank + half, a % CH:CH], K[e][:, h, jt * P:(jt + 1) * P], Q[e][:, h, a:b],
                                          start=True, stop=not diag)
                    if diag:
                        a = jt % 4 * P
                        mm = nc.tensor.matmul(ps[:, bank + half, a:a + P], g.identb[:], maskb[:], start=False, stop=True)
                mm.then_inc(sc, 1)

            def weigh(n, jt):
                pe.wait_ge(vd, n * KT + (jt + 1))
                if jt == 0:
                    pe.wait_ge(oc, n)
                for half in range(2):
                    a, b = max(jt * P, half * CH), (half + 1) * CH
                    if a >= b:
                        continue
                    for h in range(QUAD):
                        mm = nc.tensor.matmul(ps[32 * h:32 * h + 32, AV + half, a % CH:CH], vdiv[:, jt % 2, h, :],
                                              probs[:, (jt * QUAD + h) % PR, a:b],
                                              start=(jt == 0), stop=(jt == (3 if half == 0 else KT - 1)))
                mm.then_inc(av, 1)

            def step(n, e, rnd):
                for u in range(UN):
                    scores(n, e, rnd, u)
                    if u % QUAD == QUAD - 1 and u > QUAD:
                        weigh(n, u // QUAD - 1)
                weigh(n, KT - 1)

            pe.wait_ge(const, 48)
            pe.wait_ge(maskd, 1)
            with pe.Fori(0, STEPS // 2) as i:
                for e in range(2):
                    step(i * 2 + e, e, i)
            pe.wait_ge(oc, STEPS)
            for c in range(NCH):
                if c >= 2:
                    pe.wait_ge(ocopy, c - 1)
                for q in range(4):
                    mm = nc.tensor.matmul(ps[:, c % 2, :], wout[:, q, :], outT[:, q, c * CH:(c + 1) * CH],
                                          start=(q == 0), stop=(q == 3))
                mm.then_inc(oproj, 1)

        @block.scalar
        def _(act):
            with act.Fori(0, STEPS) as n:
                for u in range(UN):
                    jt = u // QUAD
                    act.wait_ge(mx, n * UN + (u + 1))
                    if u % QUAD == 0:
                        act.wait_ge(av, n * KT + max(jt - 1, 0))
                    bank = 2 * (u % RING)
                    src = ps[:, bank:bank + 2, :].rearrange("p b n -> p (b n)")[:, jt * P:T]
                    nc.scalar.activation(probs[:, u % PR, jt * P:T], src, ACT.Exp, bias=negmax[:, u % PR:u % PR + 1],
                                         accum_out=total[:, u % PR:u % PR + 1]).then_inc(ex, 1)
                act.wait_ge(av, n * KT + KT)
                dst = outT[:, bass.ds(n % 4, 1), bass.ds((n // 4) * T, T)].rearrange("p a n -> p (a n)")
                nc.scalar.copy(dst, ps[:, AV:AV + 2, :].rearrange("p b n -> p (b n)")).then_inc(oc, 1)
            for c in range(NCH):
                act.wait_ge(oproj, c + 1)
                nc.scalar.activation(g.branchT[:, c * CH:(c + 1) * CH], ps[:, c % 2, :], ACT.Identity,
                                     bias=bout[:]).then_inc(ocopy, 1)
            act.wait_ge(ocopy, NCH)

        @block.vector
        def _(dve):
            for t in (*Q, *K):
                nc.vector.memset(t[:], 0.0).then_inc(cleared, 1)
            dve.wait_ge(const, 48)
            nc.vector.tensor_copy(maskb[:], mask[:]).then_inc(maskd, 1)

            def inverse(n, jt):
                dve.wait_ge(ex, n * UN + (jt + 1) * QUAD)
                dve.wait_ge(vd, n * KT + max(jt - 1, 0))
                a = jt % 2 * QUAD
                nc.vector.reciprocal(inv[:, jt % 2, :], total[:, a:a + QUAD]).then_inc(invd, 1)

            with dve.Fori(0, STEPS) as n:
                for u in range(UN):
                    jt = u // QUAD
                    dve.wait_ge(sc, n * UN + (u + 1))
                    if u % QUAD == 0:
                        dve.wait_ge(ex, n * UN + max(u - QUAD, 0))
                    bank = 2 * (u % RING)
                    src = ps[:, bank:bank + 2, :].rearrange("p b n -> p (b n)")[:, jt * P:T]
                    nc.vector.tensor_reduce(negmax[:, u % PR:u % PR + 1], src, AX.X, ALU.max, negate=True).then_inc(mx, 1)
                    if u % QUAD == 1 and jt:
                        inverse(n, jt - 1)
                inverse(n, KT - 1)


def route(nc, g, W, combT, experts, top, kind):
    s = open_scope(nc, g)
    ps = g.ps
    E = experts
    with s.ctx:
        wr = s.sb("wr", [P, E])
        br = s.sb("br", [P, E])
        wh = s.sb("wh", [P, 32])
        hT = s.sb("hT", [32, NT])
        wkeys = s.sb("wkeys", [32, E])
        scale = s.sb("scale", [P, 1])
        iota = s.sb("iota", [P, E])
        logit = s.sb("logit", [P, TILES, E])
        val = s.sb("val", [P, TILES, E])
        pick = s.sb("pick", [P, TILES, E])
        top8 = s.sb("top8", [P, TILES, 8])
        idx8 = s.sb("idx8", [P, TILES, 8], U32)
        idxf = s.sb("idxf", [P, TILES, 8])
        same = s.sb("same", [P, top, TILES, E])
        total = s.sb("total", [P, TILES])
        inv = s.sb("inv", [P, TILES])
        rest = s.sb("rest", [P, TILES, E])
        parts = s.sb("parts", [P, TILES, 3, E], BF16)
        loaded = s.sem("rt_loaded")
        hashed = s.sem("rt_hashed")
        hcopied = s.sem("rt_hash_copied")
        product = s.sem("rt_logits")
        activ = s.sem("rt_activated")
        ve = s.sem("rt_vector_done")
        split = s.sem("rt_split")
        turned = s.sem("rt_turned")
        copied = s.sem("rt_copied")
        block = s.ctx.enter_context(nc.Block())
        tiles = dict(wr=wr, br=br, iota=iota)
        if kind == "keys":
            tiles = dict(wh=wh, wkeys=wkeys, scale=scale, iota=iota)
        ALL = 16 * len(tiles)

        @block.sync
        def _(sp):
            for n, t in tiles.items():
                sp.dma_start(t[:], W[n]).then_inc(loaded, 16)
            sp.wait_ge(loaded, ALL)

        @block.tensor
        def _(pe):
            pe.wait_ge(loaded, ALL)
            if kind == "keys":
                for c in range(NCH):
                    nc.tensor.matmul(ps[0:32, 1 + c, :], wh[:], g.xnT[:, c * CH:(c + 1) * CH], start=True, stop=True).then_inc(hashed, 1)
                pe.wait_ge(hcopied, NCH)
            for i in range(TILES):
                lhs, rhs = (hT, wkeys) if kind == "keys" else (g.xnT, wr)
                mm = nc.tensor.matmul(ps[:, 0, i * E:(i + 1) * E], lhs[:, i * P:(i + 1) * P], rhs[:], start=True, stop=True)
            mm.then_inc(product, 1)
            pe.wait_ge(split, 1)
            for c in range(NCH):
                for k in range(4):
                    mm = nc.tensor.matmul(ps[0:3 * E, 4 + c, k * P:(k + 1) * P],
                                          parts[:, 4 * c + k].rearrange("p s e -> p (s e)"), g.identb[:], start=True, stop=True)
                mm.then_inc(turned, 1)

        @block.scalar
        def _(act):
            if kind == "keys":
                for c in range(NCH):
                    act.wait_ge(hashed, c + 1)
                    nc.scalar.copy(hT[:, c * CH:(c + 1) * CH], ps[0:32, 1 + c, :]).then_inc(hcopied, 1)
            act.wait_ge(ve, 1)
            if kind == "sigmoid":
                nc.scalar.activation(val[:], logit[:], ACT.Sigmoid).then_inc(activ, 1)
            else:
                act.wait_ge(ve, 2 + TILES)
                nc.scalar.activation(val[:], rest[:], ACT.Exp).then_inc(activ, 1)
            for c in range(NCH):
                act.wait_ge(turned, c + 1)
                nc.scalar.copy(combT[:, c * CH:(c + 1) * CH], ps[0:3 * E, 4 + c, :]).then_inc(copied, 1)
            act.wait_ge(copied, NCH)

        @block.vector
        def _(dve):
            done = Count(ve)
            wide = lambda t, k: t[:, :, k:k + 1].to_broadcast([P, TILES, E])
            dve.wait_ge(loaded, ALL)
            dve.wait_ge(product, 1)
            lg = ps[:, 0, 0:TILES * E].rearrange("p (i e) -> p i e", e=E)
            if kind == "softmax":
                done.inc(nc.vector.tensor_tensor(logit[:], lg, br[:, None, :].to_broadcast([P, TILES, E]), ALU.add))
            else:
                done.inc(nc.vector.tensor_copy(logit[:], lg))
            done.wait(dve)
            chosen_by = logit
            if kind == "sigmoid":
                dve.wait_ge(activ, 1)
                done.inc(nc.vector.tensor_tensor(rest[:], val[:], br[:, None, :].to_broadcast([P, TILES, E]), ALU.add))
                done.wait(dve)
                chosen_by = rest
            for i in range(TILES):
                done.inc(nc.vector.max(top8[:, i, :], chosen_by[:, i, :]))
            done.wait(dve)
            if kind != "sigmoid":
                done.inc(nc.vector.tensor_tensor(rest[:], logit[:], wide(top8, 0), ALU.subtract))
            for i in range(TILES):
                done.inc(nc.vector.max_index(idx8[:, i, :], top8[:, i, :], chosen_by[:, i, :]))
            done.wait(dve)
            done.inc(nc.vector.tensor_copy(idxf[:], idx8[:]))
            done.wait(dve)
            for k in range(top):
                done.inc(nc.vector.tensor_tensor(same[:, k], iota[:, None, :].to_broadcast([P, TILES, E]), wide(idxf, k), ALU.is_equal))
            done.wait(dve)
            done.inc(nc.vector.tensor_tensor(pick[:], same[:, 0], same[:, 1], ALU.add))
            for k in range(2, top):
                done.wait(dve)
                done.inc(nc.vector.tensor_tensor(pick[:], pick[:], same[:, k], ALU.add))
            dve.wait_ge(activ, 1)
            done.wait(dve)
            done.inc(nc.vector.tensor_tensor(pick[:], pick[:], val[:], ALU.mult))
            done.wait(dve)
            done.inc(nc.vector.tensor_reduce(total[:], pick[:], AX.X, ALU.add))
            done.wait(dve)
            done.inc(nc.vector.reciprocal(inv[:], total[:]))
            done.wait(dve)
            if kind == "keys":
                done.inc(nc.vector.tensor_scalar(inv[:], inv[:], scale[:, 0:1], None, ALU.mult))
                done.wait(dve)
            done.inc(nc.vector.tensor_tensor(val[:], pick[:], inv[:, :, None].to_broadcast([P, TILES, E]), ALU.mult))
            done.wait(dve)
            done.inc(nc.vector.tensor_copy(parts[:, :, 0, :], val[:]))
            done.wait(dve)
            done.inc(nc.vector.tensor_tensor(rest[:], val[:], parts[:, :, 0, :], ALU.subtract))
            done.wait(dve)
            done.inc(nc.vector.tensor_copy(parts[:, :, 1, :], rest[:]))
            done.wait(dve)
            nc.vector.tensor_tensor(parts[:, :, 2, :], rest[:], parts[:, :, 1, :], ALU.subtract).then_inc(split, 1)


def gated_experts(nc, g, W, experts, hidden, top, kind, gated=True, add=False, add_xn=False):
    units = experts * hidden
    FT = -(-units // P)
    s = open_scope(nc, g)
    ps = g.ps
    GB, UB, CB, OB = 0, 2, 4, 6
    with s.ctx:
        combT = s.sb("combT", [3 * experts, NT], BF16)
        route(nc, g, W, combT, experts, top, kind)
        wg = s.sb("wg", [P, FT, P])
        wu = s.sb("wu", [P, FT, P]) if gated else None
        wd = s.sb("wd", [P, FT, P])
        sel = s.sb("sel", [3 * experts, FT, P], BF16)
        act_g = s.sb("act_g", [P, 2, CH])
        gu = s.sb("gu", [P, 2, CH])
        hid = s.sb("hid", [P, 2, CH])
        PIECE = 4
        pieces = -(-FT // PIECE)
        loaded = [s.sem(f"ge_loaded{k}") for k in range(pieces)]
        up = s.sem("ge_up")
        silud = s.sem("ge_silu")
        gud = s.sem("ge_gu")
        hidd = s.sem("ge_hidden")
        down = s.sem("ge_down")
        stored = s.sem("ge_out_copied")
        summed = s.sem("ge_out_summed")
        block = s.ctx.enter_context(nc.Block())
        todo = [("wg", wg), ("wd", wd), ("sel", sel)] + ([("wu", wu)] if gated else [])

        @block.sync
        def _(sp):
            for k in range(pieces):
                a, b = k * PIECE, min((k + 1) * PIECE, FT)
                for n, t in todo:
                    sp.dma_start(t[:, a:b, :], W[n][:, a:b, :]).then_inc(loaded[k], 16)
            for k in range(pieces):
                sp.wait_ge(loaded[k], 16 * len(todo))

        @block.tensor
        def _(pe):
            with pe.Fori(0, NCH) as c:
                where = bass.ds(c * CH, CH)
                n = c * FT

                def down_proj(f):
                    pe.wait_ge(hidd, n + (f + 1))
                    if f == 0:
                        pe.wait_ge(stored, c)
                    nc.tensor.matmul(ps[:, OB, :], wd[:, f, :], hid[:, f % 2, :], start=(f == 0), stop=(f == FT - 1)).then_inc(down, 1)

                for f in range(FT):
                    if f % PIECE == 0:
                        pe.wait_ge(loaded[f // PIECE], 16 * len(todo))
                    if f >= 2:
                        pe.wait_ge(hidd, n + (f - 1))
                    nc.tensor.matmul(ps[:, GB + f % 2, :], wg[:, f, :], g.xnT[:, where], start=True, stop=True).then_inc(up, 1)
                    if gated:
                        nc.tensor.matmul(ps[:, UB + f % 2, :], wu[:, f, :], g.xnT[:, where], start=True, stop=True)
                    nc.tensor.matmul(ps[:, CB + f % 2, :], sel[:, f, :], combT[:, where], start=True, stop=True).then_inc(up, 1)
                    if f >= 1:
                        down_proj(f - 1)
                down_proj(FT - 1)

        @block.scalar
        def _(act):
            with act.Fori(0, NCH) as c:
                n = c * FT
                for f in range(FT):
                    act.wait_ge(up, n * 2 + (2 * f + 1))
                    act.wait_ge(gud if gated else hidd, n + (f - 1) if f >= 2 else n)
                    nc.scalar.activation(act_g[:, f % 2, :], ps[:, GB + f % 2, :], ACT.Silu).then_inc(silud, 1)

        @block.vector
        def _(dve):
            with dve.Fori(0, NCH) as c:
                n = c * FT
                where = bass.ds(c * CH, CH)
                for f in range(FT):
                    dve.wait_ge(up, n * 2 + (2 * f + 2))
                    dve.wait_ge(silud, n + (f + 1))
                    if f >= 2:
                        dve.wait_ge(down, n + (f - 1))
                    if gated:
                        nc.vector.tensor_tensor(gu[:, f % 2, :], act_g[:, f % 2, :], ps[:, UB + f % 2, :], ALU.mult).then_inc(gud, 1)
                        dve.wait_ge(gud, n + (f + 1))
                    nc.vector.tensor_tensor(hid[:, f % 2, :], (gu if gated else act_g)[:, f % 2, :], ps[:, CB + f % 2, :],
                                            ALU.mult).then_inc(hidd, 1)
                dve.wait_ge(down, n + FT)
                if add:
                    nc.vector.tensor_tensor(g.branchT[:, where], g.branchT[:, where], ps[:, OB, :], ALU.add).then_inc(stored, 1)
                else:
                    nc.vector.tensor_copy(g.branchT[:, where], ps[:, OB, :]).then_inc(stored, 1)
                if add_xn:
                    dve.wait_ge(stored, c + 1)
                    nc.vector.tensor_tensor(g.branchT[:, where], g.branchT[:, where], g.xnT[:, where], ALU.add).then_inc(summed, 1)
            dve.wait_ge(stored, NCH)
            if add_xn:
                dve.wait_ge(summed, NCH)


DI, NS, DTR, TAPS = 256, 16, 64, 4
G = DI // P
PADT = T + TAPS - 1
DT_MIN, DT_MAX = 0.001, 0.1


def scan_inputs(nc, g, W, t):
    s = open_scope(nc, g)
    ps = g.ps
    XS, RES, CV, DTB, BCB = 0, 2, 4, 6, 7
    with s.ctx:
        win = s.sb("win", [P, 4, P])
        convk = s.sb("convk", [P, G, TAPS, P])
        convb = s.sb("convb", [P, G])
        wxdt = s.sb("wxdt", [P, G, DTR])
        wxbc = s.sb("wxbc", [P, G, 96])
        wdt = s.sb("wdt", [DTR, G, P])
        bdt = s.sb("bdt", [P, G])
        alog = s.sb("alog", [P, G, NS])
        xs = s.sb("xs", [P, G, B * PADT])
        dtraw = s.sb("dtraw", [DTR, 2, CH])
        rest = s.sb("rest", [96, 2, CH])
        mid = s.sb("mid", [96, 2, CH], BF16)
        loaded = s.sem("si_loaded")
        cleared = s.sem("si_cleared")
        xsd, xsc = s.sem("si_xs"), s.sem("si_xs_copied")
        resd, resc = s.sem("si_res"), s.sem("si_res_silu")
        cvd, cvc = s.sem("si_conv"), s.sem("si_u")
        prd, dtc = s.sem("si_dt_bc"), s.sem("si_dt_copied")
        bcs = s.sem("si_bc_split")
        dpd, dpc = s.sem("si_dt_projected"), s.sem("si_dt_clamped")
        expd, lnd, clipd, dud = s.sem("si_exp"), s.sem("si_ln"), s.sem("si_clipped"), s.sem("si_du")
        block = s.ctx.enter_context(nc.Block())
        tiles = dict(win=win, convk=convk, convb=convb, wxdt=wxdt, wxbc=wxbc, wdt=wdt, bdt=bdt, alog=alog)
        ALL = 16 * (len(tiles) + 2)

        @block.sync
        def _(sp):
            for n, d in tiles.items():
                sp.dma_start(d[:], W[n]).then_inc(loaded, 16)
            sp.dma_start(t.seln[:], W["seln"]).then_inc(loaded, 16)
            sp.dma_start(t.Dskip[:], W["D"]).then_inc(loaded, 16)
            sp.wait_ge(loaded, ALL)

        def at(c, tap=TAPS - 1):
            return bass.ds(c * CH + (c // 2) * (TAPS - 1) + tap, CH)

        @block.tensor
        def _(pe):
            pe.wait_ge(loaded, ALL)
            pe.wait_ge(cleared, 1)
            with pe.Fori(0, NCH) as c:
                here = bass.ds(c * CH, CH)
                pe.wait_ge(xsc, c)
                pe.wait_ge(dpc, c)
                for k in range(G):
                    mm = nc.tensor.matmul(ps[:, XS + k, :], win[:, k, :], g.xnT[:, here], start=True, stop=True)
                mm.then_inc(xsd, 1)
                pe.wait_ge(resc, c)
                for k in range(G):
                    mm = nc.tensor.matmul(ps[:, RES + k, :], win[:, G + k, :], g.xnT[:, here], start=True, stop=True)
                mm.then_inc(resd, 1)
                pe.wait_ge(xsc, c + 1)
                pe.wait_ge(cvc, c)
                for k in range(G):
                    for tap in range(TAPS):
                        mm = nc.tensor.matmul(ps[:, CV + k, :], convk[:, k, tap, :], xs[:, k, at(c, tap)],
                                              start=(tap == 0), stop=(tap == TAPS - 1))
                mm.then_inc(cvd, 1)
                pe.wait_ge(cvc, c + 1)
                pe.wait_ge(dtc, c)
                pe.wait_ge(bcs, c * 5)
                for k in range(G):
                    nc.tensor.matmul(ps[0:DTR, DTB, :], wxdt[:, k, :], t.uT[:, k, here], start=(k == 0), stop=(k == G - 1))
                for k in range(G):
                    mm = nc.tensor.matmul(ps[0:96, BCB, :], wxbc[:, k, :], t.uT[:, k, here], start=(k == 0), stop=(k == G - 1))
                mm.then_inc(prd, 1)
                pe.wait_ge(dtc, c + 1)
                for k in range(G):
                    mm = nc.tensor.matmul(ps[:, XS + k, :], wdt[:, k, :], dtraw[:, 0, :], start=True, stop=True)
                mm.then_inc(dpd, 1)

        @block.scalar
        def _(act):
            act.wait_ge(loaded, ALL)
            with act.Fori(0, NCH) as c:
                here = bass.ds(c * CH, CH)
                act.wait_ge(xsd, c + 1)
                nc.scalar.copy(xs[:, :, at(c)], ps[:, XS:XS + G, :]).then_inc(xsc, 1)
                act.wait_ge(resd, c + 1)
                nc.scalar.activation(t.sres[:, :, here], ps[:, RES:RES + G, :], ACT.Silu).then_inc(resc, 1)
                act.wait_ge(cvd, c + 1)
                nc.scalar.activation(t.uT[:, 0, here], ps[:, CV, :], ACT.Silu, bias=convb[:, 0:1])
                nc.scalar.activation(t.uT[:, 1, here], ps[:, CV + 1, :], ACT.Silu, bias=convb[:, 1:2]).then_inc(cvc, 1)
                act.wait_ge(prd, c + 1)
                act.wait_ge(dpd, c)
                nc.scalar.copy(dtraw[:, 0, :], ps[0:DTR, DTB, :]).then_inc(dtc, 1)
            act.wait_ge(dpc, NCH)
            nc.scalar.activation(t.delta[:], t.delta[:], ACT.Exp).then_inc(expd, 1)
            nc.scalar.activation(t.A[:], alog[:], ACT.Exp).then_inc(expd, 1)
            act.wait_ge(expd, 2)
            nc.scalar.activation(t.delta[:], t.delta[:], ACT.Ln, bias=1.0).then_inc(lnd, 1)

        @block.gpsimd
        def _(pool):
            nc.gpsimd.memset(xs[:], 0.0).then_inc(cleared, 1)

        @block.vector
        def _(dve):
            dve.wait_ge(loaded, ALL)
            with dve.Fori(0, NCH) as c:
                here = bass.ds(c * CH, CH)
                n = c * 5
                dve.wait_ge(prd, c + 1)
                nc.vector.tensor_copy(t.bc[:, here], ps[0:96, BCB, :]).then_inc(bcs, 1)
                dve.wait_ge(bcs, n + 1)
                nc.vector.tensor_tensor(rest[:, 0, :], ps[0:96, BCB, :], t.bc[:, here], ALU.subtract).then_inc(bcs, 1)
                dve.wait_ge(bcs, n + 2)
                nc.vector.tensor_copy(mid[:, 0, :], rest[:, 0, :]).then_inc(bcs, 1)
                dve.wait_ge(bcs, n + 3)
                nc.vector.tensor_copy(t.bc[32:64, here], mid[32:64, 0, :]).then_inc(bcs, 1)
                nc.vector.tensor_tensor(t.bc[64:96, here], rest[64:96, 0, :], mid[64:96, 0, :], ALU.subtract).then_inc(bcs, 1)
                dve.wait_ge(dpd, c + 1)
                nc.vector.tensor_scalar(t.delta[:, 0, here], ps[:, XS, :], bdt[:, 0:1], 0.0, ALU.add, ALU.min)
                nc.vector.tensor_scalar(t.delta[:, 1, here], ps[:, XS + 1, :], bdt[:, 1:2], 0.0, ALU.add, ALU.min).then_inc(dpc, 1)
            dve.wait_ge(lnd, 1)
            nc.vector.tensor_scalar(t.delta[:], t.delta[:], DT_MIN, DT_MAX, ALU.max, ALU.min).then_inc(clipd, 1)
            nc.vector.tensor_scalar(t.A[:], t.A[:], -1.0, None, ALU.mult).then_inc(clipd, 1)
            dve.wait_ge(clipd, 2)
            nc.vector.tensor_tensor(t.du[:], t.delta[:], t.uT[:], ALU.mult).then_inc(dud, 1)
            dve.wait_ge(dud, 1)


def state_scan(nc, g, W, t):
    s = open_scope(nc, g)
    ps = g.ps
    BB, CB, Y = 0, 2, 4
    with s.ctx:
        bsp = s.sb("b_spread", [P, 2, T])
        csp = s.sb("c_spread", [P, 2, T])
        decay = s.sb("decay", [P, 2, G, T])
        drive = s.sb("drive", [P, 2, G, T])
        state = s.sb("state", [P, G, T])
        read = s.sb("read", [P, 2, G, T])
        zero = s.sb("zero", [P, CH], BF16)
        skip = read[:, 0]
        gated = t.du
        wo = s.sb("wo", [P, G, P])
        loaded = s.sem("ss_loaded")
        zeroed = s.sem("ss_zeroed")
        spread = s.sem("ss_spread")
        copied = s.sem("ss_spread_copied")
        decayd = s.sem("ss_decay")
        drived = s.sem("ss_drive")
        scand = s.sem("ss_scan")
        readd = s.sem("ss_read")
        summed = s.sem("ss_summed")
        ycopied = s.sem("ss_y_copied")
        gatedd = s.sem("ss_gated")
        outd = s.sem("ss_out")
        outc = s.sem("ss_out_copied")
        block = s.ctx.enter_context(nc.Block())

        @block.sync
        def _(sp):
            sp.dma_start(wo[:], W["wo"]).then_inc(loaded, 16)
            sp.wait_ge(loaded, 16)

        @block.tensor
        def _(pe):
            pe.wait_ge(zeroed, 1)
            pe.wait_ge(loaded, 16)

            def spread_state(b, m):
                n = m + b * NS
                for j, bank in ((0, BB), (1, CB)):
                    pe.wait_ge(copied, n * 2 + j)
                    for half in range(2):
                        mm = nc.tensor.matmul(ps[:, bank + half, :], t.seln[:, bass.ds(m + j * NS, 1), :].rearrange("k a p -> k (a p)"),
                                              t.bc[:, b * T + half * CH:b * T + (half + 1) * CH], start=True, stop=True)
                    mm.then_inc(spread, 1)

            def sum_state(m, e):
                for k in range(G):
                    pe.wait_ge(readd, m * G + (k + 1))
                    for half in range(2):
                        mm = nc.tensor.matmul(ps[:, Y + 2 * k + half, :], g.ident[:], read[:, e, k, half * CH:(half + 1) * CH],
                                              start=False, stop=False, skip_group_check=True)
                mm.then_inc(summed, 1)

            for b in range(B):
                pe.wait_ge(ycopied, b * G)
                for k in range(2 * G):
                    nc.tensor.matmul(ps[:, Y + k, :], zero[:, 0:P], zero[:], start=True, stop=False, skip_group_check=True)
                spread_state(b, 0)
                with pe.Fori(0, NS // 2 - 1) as i:
                    for e in range(2):
                        spread_state(b, i * 2 + (e + 1))
                        sum_state(i * 2 + (b * NS + e), e)
                spread_state(b, NS - 1)
                sum_state(b * NS + NS - 2, 0)
                sum_state(b * NS + NS - 1, 1)
            for c in range(NCH):
                pe.wait_ge(gatedd, (c // 2 + 1) * G)
                if c >= 2:
                    pe.wait_ge(outc, c - 1)
                for k in range(G):
                    mm = nc.tensor.matmul(ps[:, BB + c % 2, :], wo[:, k, :], gated[:, k, c * CH:(c + 1) * CH],
                                          start=(k == 0), stop=(k == G - 1))
                mm.then_inc(outd, 1)

        @block.scalar
        def _(act):
            for b in range(B):
                with act.Fori(0, NS // 2) as i:
                    for e in range(2):
                        m = i * 2 + e
                        n = i * 2 + (b * NS + e)
                        act.wait_ge(spread, n * 2 + 1)
                        act.wait_ge(drived, i * 2 * G + (b * NS * G))
                        nc.scalar.copy(bsp[:, e, :], ps[:, BB:BB + 2, :].rearrange("p b n -> p (b n)")).then_inc(copied, 1)
                        act.wait_ge(scand, i * 2 * G + (b * NS * G))
                        for k in range(G):
                            nc.scalar.activation(decay[:, e, k, :], t.delta[:, k, b * T:(b + 1) * T], ACT.Exp,
                                                 scale=t.A[:, k, bass.ds(m, 1)]).then_inc(decayd, 1)
                        act.wait_ge(spread, n * 2 + 2)
                        act.wait_ge(readd, i * 2 * G + (b * NS * G))
                        nc.scalar.copy(csp[:, e, :], ps[:, CB:CB + 2, :].rearrange("p b n -> p (b n)")).then_inc(copied, 1)
            for c in range(NCH):
                act.wait_ge(outd, c + 1)
                nc.scalar.copy(g.branchT[:, c * CH:(c + 1) * CH], ps[:, BB + c % 2, :]).then_inc(outc, 1)
            act.wait_ge(outc, NCH)

        @block.gpsimd
        def _(pool):
            for b in range(B):
                with pool.Fori(0, NS // 2) as i:
                    for e in range(2):
                        n = i * 2 + (b * NS + e)
                        pool.wait_ge(copied, n * 2 + 1)
                        pool.wait_ge(scand, i * 2 * G + (b * NS * G))
                        for k in range(G):
                            nc.gpsimd.tensor_tensor(drive[:, e, k, :], t.du[:, k, b * T:(b + 1) * T], bsp[:, e, :],
                                                    ALU.mult).then_inc(drived, 1)

        @block.vector
        def _(dve):
            nc.vector.memset(zero[:], 0.0).then_inc(zeroed, 1)
            for b in range(B):
                with dve.Fori(0, NS // 2) as i:
                    for e in range(2):
                        n = i * 2 + (b * NS + e)
                        dve.wait_ge(summed, i * 2 + b * NS)
                        dve.wait_ge(readd, i * 2 * G + (b * NS + e) * G)
                        for k in range(G):
                            dve.wait_ge(decayd, n * G + (k + 1))
                            dve.wait_ge(drived, n * G + (k + 1))
                            nc.vector.tensor_tensor_scan(state[:, k, :], decay[:, e, k, :], drive[:, e, k, :], 0.0,
                                                         ALU.mult, ALU.add).then_inc(scand, 1)
                        for k in range(G):
                            dve.wait_ge(scand, n * G + (k + 1))
                            dve.wait_ge(copied, n * 2 + 2)
                            nc.vector.tensor_tensor(read[:, e, k, :], state[:, k, :], csp[:, e, :], ALU.mult).then_inc(readd, 1)
                dve.wait_ge(summed, (b + 1) * NS)
                here = slice(b * T, (b + 1) * T)
                for k in range(G):
                    nc.vector.scalar_tensor_tensor(skip[:, k, :], t.uT[:, k, here], t.Dskip[:, k:k + 1],
                                                   ps[:, Y + 2 * k:Y + 2 * k + 2, :].rearrange("p b n -> p (b n)"),
                                                   ALU.mult, ALU.add).then_inc(ycopied, 1)
                dve.wait_ge(ycopied, (b + 1) * G)
                for k in range(G):
                    nc.vector.tensor_tensor(gated[:, k, here], skip[:, k, :], t.sres[:, k, here], ALU.mult).then_inc(gatedd, 1)
            dve.wait_ge(gatedd, B * G)


def selective_scan(nc, g, W):
    s = open_scope(nc, g)
    t = Tensors()
    with s.ctx:
        t.sres = s.sb("sres", [P, G, NT])
        t.uT = s.sb("uT", [P, G, NT])
        t.delta = s.sb("delta", [P, G, NT])
        t.du = s.sb("du", [P, G, NT])
        t.A = s.sb("A", [P, G, NS])
        t.bc = s.sb("bc", [96, NT], BF16)
        t.seln = s.sb("seln", [96, 2 * NS, P], BF16)
        t.Dskip = s.sb("Dskip", [P, G])
        scan_inputs(nc, g, W, t)
        state_scan(nc, g, W, t)


ES, CAP, FH = 16, P, 512
FS = FH // P
DUMP = ES * CAP


def switch_route(nc, g, W, r):
    s = open_scope(nc, g)
    ps = g.ps
    with s.ctx:
        wr = s.sb("wr", [P, ES])
        iota = s.sb("iota", [P, ES])
        tri = s.sb("tri", [P, P], BF16)
        ones = s.sb("ones", [P, P], BF16)
        token = s.sb("token", [P, TILES])
        restart = s.sb("restart", [P, ES, TILES])
        logit = s.sb("logit", [P, TILES, ES])
        less = s.sb("less", [P, TILES, ES])
        ex = s.sb("ex", [P, TILES, ES])
        top8 = s.sb("top8", [P, TILES, 8])
        idx8 = s.sb("idx8", [P, TILES, 8], U32)
        idxf = s.sb("idxf", [P, TILES])
        hot = s.sb("hot", [P, TILES, ES])
        hotb = s.sb("hotb", [P, TILES, ES], BF16)
        tot = s.sb("tot", [P, ES, TILES])
        upto = s.sb("upto", [P, ES, TILES])
        place = s.sb("place", [P, TILES, ES])
        loc = s.sb("loc", [P, TILES])
        valid = s.sb("valid", [P, TILES])
        total = s.sb("total", [P, TILES])
        row = s.sb("row", [P, 4, TILES])
        loaded = s.sem("sr_loaded")
        product = s.sem("sr_logits")
        expd = s.sem("sr_exp")
        hotd = s.sem("sr_hot")
        counted = s.sem("sr_counted")
        ve = s.sem("sr_vector_done")
        block = s.ctx.enter_context(nc.Block())
        tiles = dict(wr=wr, iota=iota, tri=tri, ones=ones, token=token, restart=restart)
        ALL = 16 * len(tiles)

        @block.sync
        def _(sp):
            for n, d in tiles.items():
                sp.dma_start(d[:], W[n]).then_inc(loaded, 16)
            sp.wait_ge(loaded, ALL)

        @block.tensor
        def _(pe):
            pe.wait_ge(loaded, ALL)
            for i in range(TILES):
                mm = nc.tensor.matmul(ps[:, 0, i * ES:(i + 1) * ES], g.xnT[:, i * P:(i + 1) * P], wr[:], start=True, stop=True)
            mm.then_inc(product, 1)
            pe.wait_ge(hotd, 1)
            flat = hotb[:].rearrange("p i e -> p (i e)")
            nc.tensor.matmul(ps[:, 1, 0:TILES * ES], tri[:], flat, start=True, stop=True)
            nc.tensor.matmul(ps[:, 2, 0:TILES * ES], ones[:], flat, start=True, stop=True).then_inc(counted, 1)

        @block.scalar
        def _(act):
            act.wait_ge(expd, 1)
            nc.scalar.activation(ex[:], less[:], ACT.Exp).then_inc(expd, 1)
            act.wait_ge(expd, 2)

        @block.vector
        def _(dve):
            done = Count(ve)

            def then(instruction):
                done.inc(instruction)
                done.wait(dve)
            wide = lambda a: a[:, :, None].to_broadcast([P, TILES, ES])
            dve.wait_ge(loaded, ALL)
            dve.wait_ge(product, 1)
            then(nc.vector.tensor_copy(logit[:], ps[:, 0, 0:TILES * ES].rearrange("p (i e) -> p i e", e=ES)))
            for i in range(TILES):
                done.inc(nc.vector.max(top8[:, i, :], logit[:, i, :]))
            done.wait(dve)
            nc.vector.tensor_tensor(less[:], logit[:], top8[:, :, 0:1].to_broadcast([P, TILES, ES]), ALU.subtract).then_inc(expd, 1)
            for i in range(TILES):
                done.inc(nc.vector.max_index(idx8[:, i, :], top8[:, i, :], logit[:, i, :]))
            done.wait(dve)
            then(nc.vector.tensor_copy(idxf[:], idx8[:, :, 0]))
            then(nc.vector.tensor_tensor(hot[:], iota[:, None, :].to_broadcast([P, TILES, ES]), wide(idxf), ALU.is_equal))
            nc.vector.tensor_copy(hotb[:], hot[:]).then_inc(hotd, 1)
            dve.wait_ge(expd, 2)
            then(nc.vector.tensor_reduce(total[:], ex[:], AX.X, ALU.add))
            then(nc.vector.reciprocal(total[:], total[:]))
            dve.wait_ge(counted, 1)
            then(nc.vector.tensor_copy(tot[:], ps[:, 2, 0:TILES * ES].rearrange("p (i e) -> p e i", e=ES)))
            then(nc.vector.tensor_tensor_scan(upto[:].rearrange("p e i -> p (e i)"), restart[:].rearrange("p e i -> p (e i)"),
                                              tot[:].rearrange("p e i -> p (e i)"), 0.0, ALU.mult, ALU.add))
            then(nc.vector.tensor_tensor(upto[:], upto[:], tot[:], ALU.subtract))
            then(nc.vector.tensor_tensor(place[:], ps[:, 1, 0:TILES * ES].rearrange("p (i e) -> p i e", e=ES),
                                         upto[:].rearrange("p e i -> p i e"), ALU.add))
            then(nc.vector.tensor_tensor(place[:], place[:], hot[:], ALU.mult))
            then(nc.vector.tensor_reduce(loc[:], place[:], AX.X, ALU.add))
            then(nc.vector.tensor_scalar(valid[:], loc[:], CAP + 0.5, None, ALU.is_lt))
            then(nc.vector.tensor_tensor(r.factor[:], total[:], valid[:], ALU.mult))
            then(nc.vector.tensor_scalar(loc[:], loc[:], float(CAP), -1.0, ALU.min, ALU.add))
            then(nc.vector.scalar_tensor_tensor(row[:, 0], idxf[:], float(CAP), loc[:], ALU.mult, ALU.add))
            then(nc.vector.tensor_tensor(row[:, 1], row[:, 0], token[:], ALU.subtract))
            then(nc.vector.tensor_tensor(row[:, 2], row[:, 1], valid[:], ALU.mult))
            then(nc.vector.tensor_tensor(row[:, 3], row[:, 2], token[:], ALU.add))
            then(nc.vector.tensor_copy(r.gather[:], row[:, 0]))
            then(nc.vector.tensor_copy(r.scatter[:], row[:, 3]))


def switch_experts(nc, g, W, dispatch, expert_out):
    s = open_scope(nc, g)
    ps = g.ps
    r = Tensors()
    HB, OB, TB = 0, 2, 4
    with s.ctx:
        r.factor = s.sb("factor", [P, TILES])
        r.gather = s.sb("gather", [P, TILES], U32)
        r.scatter = s.sb("scatter", [P, TILES], U32)
        switch_route(nc, g, W, r)
        zero = s.sb("zero", [P, ES, D])
        rows = s.sb("rows", [P, ES, D])
        rowsT = s.sb("rowsT", [P, ES * CAP])
        w1 = s.sb("w1", [P, 2, FH])
        w2 = s.sb("w2", [P, 2, FS, D])
        hid = s.sb("hid", [P, 2, FS, CAP])
        eo = s.sb("eo", [P, 2, D])
        back = s.sb("back", [P, TILES, D])
        zeroed = s.sem("se_zeroed")
        cleared = s.sem("se_table_cleared")
        sent = s.sem("se_sent")
        rowsl = s.sem("se_rows_loaded")
        turned = s.sem("se_turned")
        tcopied = s.sem("se_turned_copied")
        wl = [s.sem(f"se_weights_loaded{e}") for e in range(2)]
        hd, hc = s.sem("se_hidden"), s.sem("se_hidden_relu")
        od, oc = s.sem("se_out"), s.sem("se_out_copied")
        os_ = [s.sem(f"se_out_stored{e}") for e in range(2)]
        got = s.sem("se_got")
        addd = s.sem("se_added")
        block = s.ctx.enter_context(nc.Block())

        @block.sync
        def _(sp):
            sp.wait_ge(zeroed, 1)
            sp.dma_start(dispatch[0:DUMP, :].rearrange("(e p) d -> p e d", p=P), zero[:]).then_inc(cleared, 16)
            for e in range(2):
                sp.dma_start(w1[:, e, :], W["w1"][e]).then_inc(wl[e], 16)
                sp.dma_start(w2[:, e], W["w2"][e]).then_inc(wl[e], 16)
            sp.wait_ge(sent, 16 * TILES)
            sp.dma_start(rows[:], dispatch[0:DUMP, :].rearrange("(e p) d -> p e d", p=P)).then_inc(rowsl, 16)
            with sp.Fori(0, ES // 2 - 1) as i:
                for e in range(2):
                    sp.wait_ge(od, i * 2 + (e + 1))
                    nxt = bass.ds(i * 2 + (e + 2), 1)
                    sp.dma_start(w1[:, e, :], W["w1"][nxt].rearrange("a p f -> p (a f)")).then_inc(wl[e], 16)
                    sp.dma_start(w2[:, e], W["w2"][nxt].rearrange("a p f m -> p (a f) m")).then_inc(wl[e], 16)
                    sp.wait_ge(oc, i * 2 + (e + 1))
                    sp.dma_start(expert_out[bass.ds((i * 2 + e) * CAP, CAP), :], eo[:, e, :]).then_inc(os_[e], 16)
            for e in range(2):
                sp.wait_ge(oc, ES - 1 + e)
                sp.dma_start(expert_out[(ES - 2 + e) * CAP:(ES - 1 + e) * CAP, :], eo[:, e, :]).then_inc(os_[e], 16)
            for e in range(2):
                sp.wait_ge(os_[e], 16 * ES // 2)
                sp.wait_ge(wl[e], 32 * ES // 2)

        @block.gpsimd
        def _(pool):
            pool.wait_ge(cleared, 16)
            for i in range(TILES):
                nc.gpsimd.indirect_dma_start(dispatch, bass.IndirectOffsetOnAxis(ap=r.scatter[:, i:i + 1], axis=0),
                                             g.xn[:, i, :], None).then_inc(sent, 16)
            for e in range(2):
                pool.wait_ge(os_[e], 16 * ES // 2)
            for i in range(TILES):
                nc.gpsimd.indirect_dma_start(back[:, i, :], None, expert_out,
                                             bass.IndirectOffsetOnAxis(ap=r.gather[:, i:i + 1], axis=0)).then_inc(got, 16)
            pool.wait_ge(sent, 16 * TILES)
            pool.wait_ge(got, 16 * TILES)

        @block.tensor
        def _(pe):
            pe.wait_ge(rowsl, 16)
            for q in range(4):
                for k in range(4):
                    mm = nc.tensor.transpose(ps[:, TB + q, k * P:(k + 1) * P], rows[:, 4 * q + k, :], g.ident[:])
                mm.then_inc(turned, 1)
            pe.wait_ge(tcopied, 4)
            with pe.Fori(0, ES // 2) as i:
                for e in range(2):
                    pe.wait_ge(wl[e], i * 32 + 32)
                    pe.wait_ge(hc, i * 2)
                    for f in range(FS):
                        mm = nc.tensor.matmul(ps[:, HB + e, f * CAP:(f + 1) * CAP], w1[:, e, f * P:(f + 1) * P],
                                              rowsT[:, bass.ds((i * 2 + e) * CAP, CAP)], start=True, stop=True)
                    mm.then_inc(hd, 1)
                for e in range(2):
                    pe.wait_ge(hc, i * 2 + (e + 1))
                    pe.wait_ge(oc, i * 2)
                    for f in range(FS):
                        mm = nc.tensor.matmul(ps[:, OB + e, 0:D], hid[:, e, f, :], w2[:, e, f, :], start=(f == 0), stop=(f == FS - 1))
                    mm.then_inc(od, 1)

        @block.scalar
        def _(act):
            with act.Fori(0, ES // 2) as i:
                for e in range(2):
                    act.wait_ge(hd, i * 2 + (e + 1))
                    act.wait_ge(od, i * 2)
                    nc.scalar.activation(hid[:, e].rearrange("p f n -> p (f n)"), ps[:, HB + e, :], ACT.Relu).then_inc(hc, 1)

        @block.vector
        def _(dve):
            nc.vector.memset(zero[:], 0.0).then_inc(zeroed, 1)
            for q in range(4):
                dve.wait_ge(turned, q + 1)
                nc.vector.tensor_copy(rowsT[:, q * CH:(q + 1) * CH], ps[:, TB + q, :]).then_inc(tcopied, 1)
            with dve.Fori(0, ES // 2) as i:
                for e in range(2):
                    dve.wait_ge(od, i * 2 + (e + 1))
                    dve.wait_ge(os_[e], i * 16)
                    nc.vector.tensor_copy(eo[:, e, :], ps[:, OB + e, 0:D]).then_inc(oc, 1)
            dve.wait_ge(got, 16 * TILES)
            for i in range(TILES):
                nc.vector.scalar_tensor_tensor(g.x[:, i, :], back[:, i, :], r.factor[:, i:i + 1], g.x[:, i, :],
                                               ALU.mult, ALU.add).then_inc(addd, 1)
            dve.wait_ge(addd, TILES)


PAIRS = 8
HEAD3 = 64
NEAR = 2


def near_tiles(qt):
    return range(max(0, qt - NEAR), min(KT - 1, qt + NEAR) + 1)


def dilated_attention(nc, g, W):
    s = open_scope(nc, g)
    ps = g.ps
    TB, OB = 4, 6
    WIDE = (2 * NEAR + 1) * P
    UN = 2 * KT
    with s.ctx:
        w = s.sb("w3", [P, 3, P])
        wo = s.sb("wo3", [P, PAIRS, P])
        mask = s.sb("mask3", [P, WIDE])
        Q = [[s.sb(f"Q3_{b}{h}", [P, T]) for h in range(2)] for b in range(B)]
        K = [s.sb(f"K3_{b}", [P, T]) for b in range(B)]
        V = [s.sb(f"V3_{b}", [P, KT, P]) for b in range(B)]
        masked = [s.sb(f"masked{h}", [P, WIDE]) for h in range(2)]
        probs = [[s.sb(f"probs3_{k}{h}", [P, WIDE]) for h in range(2)] for k in range(2)]
        probsT = [[s.sb(f"probsT3_{k}{h}", [P, WIDE]) for h in range(2)] for k in range(2)]
        mx = s.sb("mx3", [P, UN])
        negmax = s.sb("negmax3", [P, UN])
        total = s.sb("total3", [P, UN])
        inv = s.sb("inv3", [P, UN])
        outT = s.sb("outT3", [P, PAIRS, NT])
        const = s.sem("da_const")
        wloaded = s.sem("da_weights")
        cleared = s.sem("da_cleared")
        projected = s.sem("da_projected")
        qcopied = s.sem("da_q_copied")
        kvcopied = s.sem("da_kv_copied")
        sc = s.sem("da_scores")
        mxd = s.sem("da_max")
        maxd = s.sem("da_masked")
        ex = s.sem("da_exp")
        negcleared = s.sem("da_negmax_cleared")
        invd = s.sem("da_inverse")
        divd = s.sem("da_divided")
        tr = s.sem("da_turned")
        ev_dve = s.sem("da_turned_copied_dve")
        ev_act = s.sem("da_turned_copied_act")
        av = s.sem("da_weighed")
        oc = s.sem("da_out_copied")
        oproj = s.sem("da_out_projected")
        ocopy = s.sem("da_out_stored")
        block = s.ctx.enter_context(nc.Block())

        def groups(engine, body):
            with engine.Fori(0, PAIRS - 1) as hp:
                for b in range(B):
                    body(hp, b, hp * B + b, True)
            for b in range(B):
                body(PAIRS - 1, b, (PAIRS - 1) * B + b, b == 0)

        @block.sync
        def _(sp):
            sp.dma_start(w[:], W["wqkv"][0]).then_inc(wloaded, 16)
            sp.dma_start(mask[:], W["mask"]).then_inc(const, 16)
            sp.dma_start(wo[:], W["wo"]).then_inc(const, 16)
            with sp.Fori(0, PAIRS - 1) as hp:
                sp.wait_ge(projected, hp * 6 + 6)
                sp.dma_start(w[:], W["wqkv"][bass.ds(hp + 1, 1)].rearrange("a p s n -> (a p) s n")).then_inc(wloaded, 16)
            sp.wait_ge(wloaded, 16 * PAIRS)
            sp.wait_ge(const, 32)

        @block.tensor
        def _(pe):
            def project(which, b, n):
                if which == "q":
                    pe.wait_ge(wloaded, (n // B) * 16 + 16)
                    pe.wait_ge(ex, n * UN)
                elif which == "k":
                    pe.wait_ge(ex, n * UN)
                else:
                    pe.wait_ge(qcopied, n * 2 + 2)
                for c in range(2):
                    if which != "v":
                        j = 0 if which == "q" else 1
                        mm = nc.tensor.matmul(ps[:, 2 * j + c, :], w[:, j, :], g.xnT[:, b * T + c * CH:b * T + (c + 1) * CH],
                                              start=True, stop=True)
                    else:
                        for k in range(4):
                            a = b * T + (4 * c + k) * P
                            mm = nc.tensor.matmul(ps[:, c, k * P:(k + 1) * P], g.xnT[:, a:a + P], w[:, 2, :], start=True, stop=True)
                mm.then_inc(projected, 1)

            def scores(b, n, qt, h):
                u = 2 * qt + h
                if qt == 0:
                    pe.wait_ge(qcopied, n * 2 + 2)
                    pe.wait_ge(kvcopied, n * 2 + 2)
                else:
                    pe.wait_ge(maxd, n * UN + (u - 1))
                kts = near_tiles(qt)
                for a in range(0, len(kts), 4):
                    k0, k1 = kts[a], kts[min(a + 4, len(kts)) - 1] + 1
                    mm = nc.tensor.matmul(ps[:, 2 * h + a // 4, 0:(k1 - k0) * P], Q[b][h][:, qt * P:(qt + 1) * P],
                                          K[b][:, k0 * P:k1 * P], start=True, stop=True)
                mm.then_inc(sc, 1)

            def turn(n, qt, h):
                u = 2 * qt + h
                pe.wait_ge(divd, n * UN + (u + 1))
                pe.wait_ge(ev_dve, n * UN + u)
                pe.wait_ge(ev_act, n * UN + u)
                m = len(near_tiles(qt))
                for k in range(m):
                    bank, at = (TB, k) if k < (m + 1) // 2 else (TB + 1, k - (m + 1) // 2)
                    mm = nc.tensor.transpose(ps[:, bank, at * P:(at + 1) * P], probs[qt % 2][h][:, k * P:(k + 1) * P], g.ident[:])
                mm.then_inc(tr, 1)

            def weigh(b, n, qt):
                pe.wait_ge(ev_dve, n * UN + (2 * qt + 2))
                pe.wait_ge(ev_act, n * UN + (2 * qt + 2))
                if qt % 4 == 0:
                    pe.wait_ge(oc, n * 2 + max(qt // 4 - 1, 0))
                kts = near_tiles(qt)
                for k, kt in enumerate(kts):
                    for h in range(2):
                        mm = nc.tensor.matmul(ps[HEAD3 * h:HEAD3 * (h + 1), OB + qt // 4, qt % 4 * P:(qt % 4 + 1) * P],
                                              V[b][:, kt, HEAD3 * h:HEAD3 * (h + 1)], probsT[qt % 2][h][:, k * P:(k + 1) * P],
                                              start=(k == 0), stop=(k == len(kts) - 1))
                mm.then_inc(av, 1)

            def group(hp, b, n, more):
                for i in range(KT):
                    scores(b, n, i, 0)
                    if i >= 1:
                        turn(n, i - 1, 0)
                    if i >= 2:
                        weigh(b, n, i - 2)
                    scores(b, n, i, 1)
                    if i >= 1:
                        turn(n, i - 1, 1)
                last = KT - 1
                weigh(b, n, last - 1)
                if more:
                    project("q", 1 - b, n + 1)
                turn(n, last, 0)
                if more:
                    project("k", 1 - b, n + 1)
                turn(n, last, 1)
                if more:
                    project("v", 1 - b, n + 1)
                weigh(b, n, last)

            for which in "qkv":
                project(which, 0, 0)
            groups(pe, group)
            pe.wait_ge(oc, 2 * B * PAIRS)
            pe.wait_ge(const, 32)
            for c in range(NCH):
                for q in range(PAIRS):
                    mm = nc.tensor.matmul(ps[:, c, :], wo[:, q, :], outT[:, q, c * CH:(c + 1) * CH],
                                          start=(q == 0), stop=(q == PAIRS - 1))
                mm.then_inc(oproj, 1)

        @block.scalar
        def _(act):
            def copy_q(b, n):
                act.wait_ge(projected, n * 3 + 1)
                src = ps[:, 0:2, :].rearrange("p c n -> p (c n)")
                for h in range(2):
                    rows = slice(HEAD3 * h, HEAD3 * (h + 1))
                    nc.scalar.activation(Q[b][h][rows, :], src[rows, :], ACT.Copy, scale=HEAD3 ** -0.5).then_inc(qcopied, 1)

            def exp(n, qt, h):
                u = 2 * qt + h
                m = len(near_tiles(qt)) * P
                act.wait_ge(mxd, n * UN + (u + 1))
                act.wait_ge(tr, n * UN + max(u - 3, 0))
                nc.scalar.activation(probs[qt % 2][h][:, 0:m], masked[h][:, 0:m], ACT.Exp, bias=negmax[:, u:u + 1],
                                     accum_out=total[:, u:u + 1]).then_inc(ex, 1)

            def copy_turned(n, qt, h):
                m = len(near_tiles(qt))
                first = (m + 1) // 2
                act.wait_ge(tr, n * UN + (2 * qt + h + 1))
                act.wait_ge(av, n * KT + max(qt - 1, 0))
                nc.scalar.copy(probsT[qt % 2][h][:, first * P:m * P], ps[:, TB + 1, 0:(m - first) * P]).then_inc(ev_act, 1)

            def copy_out(hp, b, n, half):
                act.wait_ge(av, n * KT + 4 * (half + 1))
                dst = outT[:, bass.ds(hp, 1), b * T + half * CH:b * T + (half + 1) * CH].rearrange("p a n -> p (a n)")
                nc.scalar.copy(dst, ps[:, OB + half, :]).then_inc(oc, 1)

            def group(hp, b, n, more):
                for i in range(KT):
                    for h in range(2):
                        exp(n, i, h)
                        if i >= 1:
                            copy_turned(n, i - 1, h)
                    if i == 6:
                        copy_out(hp, b, n, 0)
                if more:
                    copy_q(1 - b, n + 1)
                for h in range(2):
                    copy_turned(n, KT - 1, h)
                copy_out(hp, b, n, 1)

            act.wait_ge(cleared, 2 * B)
            copy_q(0, 0)
            groups(act, group)
            for c in range(1, NCH, 2):
                act.wait_ge(oproj, c + 1)
                nc.scalar.copy(g.branchT[:, c * CH:(c + 1) * CH], ps[:, c, :]).then_inc(ocopy, 1)
            act.wait_ge(ocopy, NCH)

        @block.gpsimd
        def _(pool):
            for b in range(B):
                for h in range(2):
                    nc.gpsimd.memset(Q[b][h][:], 0.0).then_inc(cleared, 1)

        @block.vector
        def _(dve):
            def copy_kv(b, n):
                dve.wait_ge(projected, n * 3 + 2)
                nc.vector.tensor_copy(K[b][:], ps[:, 2:4, :].rearrange("p c n -> p (c n)")).then_inc(kvcopied, 1)
                dve.wait_ge(projected, n * 3 + 3)
                nc.vector.tensor_copy(V[b][:], ps[:, 0:2, :].rearrange("p c (k d) -> p (c k) d", d=P)).then_inc(kvcopied, 1)

            def largest(n, qt, h):
                u = 2 * qt + h
                kts = near_tiles(qt)
                m = len(kts) * P
                a = (kts[0] - qt + NEAR) * P
                dve.wait_ge(sc, n * UN + (u + 1))
                if u == 0:
                    dve.wait_ge(ex, n * UN)
                    dve.wait_ge(divd, n * UN)
                    nc.vector.memset(negmax[:], 0.0).then_inc(negcleared, 1)
                else:
                    inverse(n, u - 1)
                nc.vector.tensor_tensor_reduce(masked[h][:, 0:m], ps[:, 2 * h:2 * h + 2, :].rearrange("p c n -> p (c n)")[:, 0:m],
                                               mask[:, a:a + m], 1.0, -3.0e38, ALU.add, ALU.max,
                                               accum_out=mx[:, u:u + 1]).then_inc(maxd, 1)
                if u == 0:
                    dve.wait_ge(negcleared, n + 1)
                dve.wait_ge(maxd, n * UN + (u + 1))
                nc.vector.tensor_scalar(negmax[:, u:u + 1], mx[:, u:u + 1], -1.0, None, ALU.mult).then_inc(mxd, 1)

            def inverse(n, u):
                dve.wait_ge(ex, n * UN + (u + 1))
                nc.vector.reciprocal(inv[:, u:u + 1], total[:, u:u + 1]).then_inc(invd, 1)

            def divide(n, u):
                m = len(near_tiles(u // 2)) * P
                p = probs[u // 2 % 2][u % 2]
                dve.wait_ge(invd, n * UN + (u + 1))
                nc.vector.tensor_scalar(p[:, 0:m], p[:, 0:m], inv[:, u:u + 1], None, ALU.mult).then_inc(divd, 1)

            def copy_turned(n, qt, h):
                m = (len(near_tiles(qt)) + 1) // 2 * P
                dve.wait_ge(tr, n * UN + (2 * qt + h + 1))
                dve.wait_ge(av, n * KT + max(qt - 1, 0))
                nc.vector.tensor_copy(probsT[qt % 2][h][:, 0:m], ps[:, TB, 0:m]).then_inc(ev_dve, 1)

            def group(hp, b, n, more):
                for i in range(KT):
                    for h in range(2):
                        largest(n, i, h)
                        if i or h:
                            divide(n, 2 * i + h - 1)
                        if i >= 1:
                            copy_turned(n, i - 1, h)
                inverse(n, UN - 1)
                divide(n, UN - 1)
                copy_turned(n, KT - 1, 0)
                if more:
                    dve.wait_ge(projected, n * 3 + 5)
                    nc.vector.tensor_copy(K[1 - b][:], ps[:, 2:4, :].rearrange("p c n -> p (c n)")).then_inc(kvcopied, 1)
                copy_turned(n, KT - 1, 1)
                if more:
                    dve.wait_ge(projected, n * 3 + 6)
                    nc.vector.tensor_copy(V[1 - b][:], ps[:, 0:2, :].rearrange("p c (k d) -> p (c k) d", d=P)).then_inc(kvcopied, 1)

            dve.wait_ge(const, 32)
            copy_kv(0, 0)
            groups(dve, group)
            for c in range(0, NCH, 2):
                dve.wait_ge(oproj, c + 1)
                nc.vector.tensor_copy(g.branchT[:, c * CH:(c + 1) * CH], ps[:, c, :]).then_inc(ocopy, 1)


def program(nc, A, out, scratch, layers=(0, 1, 2, 3), parts=("attn", "ffn")):
    g = open_scope(nc)
    with g.ctx:
        g.x = g.sb("x", [P, TILES, D])
        g.xn = g.sb("xn", [P, TILES, D])
        g.xnT = g.sb("xnT", [P, NT])
        g.branchT = g.sb("branchT", [P, NT])
        g.ident = g.sb("ident", [P, P])
        g.identb = g.sb("identb", [P, P], BF16)
        g.ps = g.ctx.enter_context(nc.psum_tensor("ps", [P, 8, CH], F32))
        setup(nc, g, A)
        for n, layer in enumerate(layers):
            if n == 2:
                clear_semaphores(nc, g.used)
            residual_norm(nc, g, first=(n == 0), last=False)
            LAYERS[layer](nc, g, A, scratch, parts)
        residual_norm(nc, g, first=False, last=True)
        finish(nc, g, out)


def weights(A, layer):
    return {k[3:]: v for k, v in A.items() if k.startswith(f"L{layer}_")}


def layer0(nc, g, A, scratch, parts):
    W = weights(A, 0)
    if "attn" in parts:
        head_mixing(nc, g, W)
    if "ffn" in parts:
        gated_experts(nc, g, W, experts=8, hidden=344, top=2, kind="softmax", add="attn" in parts)


def clear_branch(nc, g):
    with ExitStack() as ctx:
        done = ctx.enter_context(nc.semaphore("branch_cleared"))
        block = ctx.enter_context(nc.Block())

        @block.vector
        def _(dve):
            nc.vector.memset(g.branchT[:], 0.0).then_inc(done, 1)
            dve.wait_ge(done, 1)


def layer1(nc, g, A, scratch, parts):
    W = weights(A, 1)
    if "attn" in parts:
        selective_scan(nc, g, W)
    else:
        clear_branch(nc, g)
    if "ffn" in parts:
        switch_experts(nc, g, W, scratch["dispatch"], scratch["expert_out"])


def layer2(nc, g, A, scratch, parts):
    W = weights(A, 2)
    if "attn" in parts:
        s = open_scope(nc, g)
        with s.ctx:
            Vp = s.sb("Vp", [P, TILES, P])
            split_qk(nc, g, scratch["qk"], W, float(HD) ** -0.5)
            value_tiles(nc, g, Vp, W)
            column_softmax_attention(nc, g, scratch["qk"], Vp, W)
    if "ffn" in parts:
        gated_experts(nc, g, W, experts=32, hidden=96, top=4, kind="sigmoid", add="attn" in parts)


def layer3(nc, g, A, scratch, parts):
    W = weights(A, 3)
    if "attn" in parts:
        dilated_attention(nc, g, W)
    if "ffn" in parts:
        gated_experts(nc, g, W, experts=32, hidden=32, top=4, kind="keys", gated=False, add="attn" in parts, add_xn=True)


LAYERS = {0: layer0, 1: layer1, 2: layer2, 3: layer3}


def _layouts(i):
    f, bf = np.float32, np.dtype("bfloat16")
    A = {"x": i["L0_attn_x"].reshape(NT, D), "ident": np.eye(P, dtype=f)}

    def wide_rows(w):
        out = np.zeros((P, 4, P), f)
        for h in range(HEADS):
            out[32 * (h % 4):32 * (h % 4) + 8, h // 4, :] = w[8 * h:8 * h + 8, :]
        return out

    swap = np.array([8 * h + (j + 4) % 8 for h in range(HEADS) for j in range(8)])
    kcols = np.array([16 * h + j for h in range(HEADS) for j in range(8)])
    inv = (1.0 / 10000.0 ** (np.arange(0, 8, 2, dtype=f) / f(8))).astype(f)
    freqs = np.arange(T, dtype=f)[:, None] * inv[None, :]
    rows = lambda a: a.astype(f).reshape(T // P, P, 8).transpose(1, 0, 2)
    A["L0_cos"] = rows(np.concatenate([np.cos(freqs), np.cos(freqs)], 1))
    A["L0_sin"] = rows(np.concatenate([-np.sin(freqs), np.sin(freqs)], 1))
    Wq, bq, Wup, bup = i["L0_attn_Wq"], i["L0_attn_bq"], i["L0_attn_Wup"], i["L0_attn_bup"]
    A["L0_wq"] = np.stack([Wq, Wq[:, swap]], 1)
    A["L0_wup"] = np.stack([Wup[:, kcols], Wup[:, kcols[swap]], Wup[:, kcols + 8]], 1)
    A["L0_bias"] = np.broadcast_to(np.stack([bq, bq[swap], bup[kcols], bup[kcols[swap]], bup[kcols + 8]]), (P, 5, P))
    A["L0_wdown"], A["L0_bdown"] = i["L0_attn_Wdown"], i["L0_attn_bdown"][:, None]
    A["L0_wout"] = i["L0_attn_Wout"]
    A["L0_bout"] = i["L0_attn_bout"][:, None]

    half = lambda v: v.reshape(G, P).T
    wx = i["L1_attn_W_x"].reshape(G, P, DTR + 2 * NS).transpose(1, 0, 2)
    A["L1_win"] = i["L1_attn_W_in"].reshape(D, 4, P)
    A["L1_convk"] = i["L1_attn_conv_k"].reshape(TAPS, P, G, P).transpose(1, 2, 0, 3)
    A["L1_convb"] = half(i["L1_attn_conv_b"])
    A["L1_wxdt"] = wx[:, :, 0:DTR]
    A["L1_wxbc"] = np.concatenate([wx[:, :, DTR:]] * 3, 2)
    A["L1_wdt"] = i["L1_attn_W_dt"].reshape(DTR, G, P)
    A["L1_bdt"] = half(i["L1_attn_b_dt"])
    A["L1_alog"] = i["L1_attn_A_log"].reshape(G, P, NS).transpose(1, 0, 2)
    A["L1_D"] = half(i["L1_attn_D"])
    A["L1_wo"] = i["L1_attn_W_out"].reshape(G, P, D).transpose(1, 0, 2)
    A["L1_seln"] = np.broadcast_to(np.concatenate([np.eye(2 * NS)] * 3)[:, :, None], (96, 2 * NS, P)).astype(bf)
    A["L1_wr"] = i["L1_ffn_Wg"]
    A["L1_iota"] = np.broadcast_to(np.arange(ES, dtype=f), (P, ES))
    A["L1_tri"] = (np.arange(P)[:, None] <= np.arange(P)[None, :]).astype(bf)
    A["L1_ones"] = np.ones((P, P), bf)
    A["L1_token"] = (DUMP + np.arange(NT)).reshape(TILES, P).T.astype(f)
    A["L1_restart"] = np.broadcast_to((np.arange(TILES) > 0).astype(f), (P, ES, TILES))
    A["L1_w1"] = i["L1_ffn_w1"]
    A["L1_w2"] = i["L1_ffn_w2"].reshape(ES, FS, P, D).transpose(0, 2, 1, 3)
    wqkv, bqkv = i["L2_attn_W_qkv"], i["L2_attn_b_qkv"]
    A["L2_wqk"] = wqkv[:, 0:2 * P].reshape(D, 2, P)
    A["L2_bqk"] = bqkv[0:2 * P].reshape(2, P).T
    A["L2_wv"] = wqkv[:, 2 * P:]
    A["L2_bv"] = np.broadcast_to(bqkv[2 * P:], (P, P))
    A["L2_mask"] = np.where(np.arange(P)[None, :] < np.arange(P)[:, None], f(-1e30), f(0)).astype(f)
    A["L2_wout"] = wide_rows(i["L2_attn_W_proj"])
    A["L2_bout"] = i["L2_attn_b_proj"][:, None]

    pairs = lambda w: w.reshape(D, PAIRS, 2 * HEAD3).transpose(1, 0, 2)
    A["L3_wqkv"] = np.stack([pairs(i[f"L3_attn_w_{n}"]) for n in "qkv"], 2)
    A["L3_wo"] = i["L3_attn_w_o"].reshape(PAIRS, 2 * HEAD3, D).transpose(1, 0, 2)
    query, key = np.arange(P)[:, None], np.arange((2 * NEAR + 1) * P)[None, :] - NEAR * P
    gap = np.abs(key - query)
    seen = (key // 64 == query // 64) | ((gap > 0) & (gap % 4 == 0) & (gap <= 256))
    A["L3_mask"] = np.where(seen, f(0), f(-1e30)).astype(f)

    def experts(layer, up, gate, down, n, hidden):
        ft = -(-n * hidden // P)
        pad = ft * P - n * hidden

        def cols(w):
            w = np.pad(w.transpose(1, 0, 2).reshape(D, n * hidden), ((0, 0), (0, pad)))
            return w.reshape(D, ft, P)
        A[f"L{layer}_wg"] = cols(gate)
        if up is not None:
            A[f"L{layer}_wu"] = cols(up)
        w = np.pad(down.reshape(n * hidden, D), ((0, pad), (0, 0)))
        A[f"L{layer}_wd"] = w.reshape(ft, P, D).transpose(1, 0, 2)
        owner = np.arange(ft * P) // hidden
        one = (owner[None, :] == np.arange(n)[:, None]).astype(bf)
        A[f"L{layer}_sel"] = np.concatenate([one] * 3).reshape(3 * n, ft, P)
        A[f"L{layer}_iota"] = np.broadcast_to(np.arange(n, dtype=f), (P, n))

    experts(0, i["L0_ffn_Wu"], i["L0_ffn_Wg"], i["L0_ffn_Wd"], 8, 344)
    A["L0_wr"] = i["L0_ffn_Ws"]
    A["L0_br"] = np.broadcast_to(i["L0_ffn_bs"], (P, 8))
    experts(2, i["L2_ffn_w3"], i["L2_ffn_w1"], i["L2_ffn_w2"], 32, 96)
    A["L2_wr"] = i["L2_ffn_gate_w"].T
    A["L2_br"] = np.broadcast_to(i["L2_ffn_e_bias"], (P, 32))
    experts(3, None, i["L3_ffn_values_down"], i["L3_ffn_values_up"], 32, 32)
    A["L3_wh"] = i["L3_ffn_hasher_w"].T
    A["L3_wkeys"] = i["L3_ffn_keys"].T
    A["L3_scale"] = np.broadcast_to(i["L3_ffn_scale"], (P, 1))
    return {k: np.ascontiguousarray(v) for k, v in A.items()}


def _make(nc, A, out_shape, **options):
    aps = {k: nc.dram_tensor("in_" + k, v.shape, mybir.dt.from_np(v.dtype), kind="ExternalInput").ap() for k, v in A.items()}
    out = nc.dram_tensor("out_x", out_shape, F32, kind="ExternalOutput").ap()
    scratch = {"qk": nc.dram_tensor("qk_parts", (2, 3, P, NT), BF16, kind="Internal").ap(),
               "dispatch": nc.dram_tensor("dispatch", (DUMP + NT, D), F32, kind="Internal").ap(),
               "expert_out": nc.dram_tensor("expert_out", (DUMP, D), F32, kind="Internal").ap()}
    program(nc, aps, out, scratch, **options)


def kernel(**inputs):
    import concourse.bacc as bacc
    from concourse.bass_utils import run_bass_kernel_spmd

    nc = bacc.Bacc("TRN2", target_bir_lowering=False, num_devices=1)
    A = _layouts({k: np.asarray(v) for k, v in inputs.items()})
    _make(nc, A, (NT, D))
    r = run_bass_kernel_spmd(nc, [{"in_" + k: v for k, v in A.items()}], core_ids=[0])
    return r.results[0]["out_x"].reshape(B, T, D)
```

```python
from contextlib import ExitStack

import numpy as np

import concourse.bass as bass
from concourse import mybir

F32 = mybir.dt.float32
BF16 = mybir.dt.bfloat16
U32 = mybir.dt.uint32
ALU = mybir.AluOpType
ACT = mybir.ActivationFunctionType
AX = mybir.AxisListType

P = 128
D = 128
B = 2
T = 1024
NT = B * T
TILES = NT // P
CH = 512
NCH = NT // CH
EPS = 1e-5

SPLIT_Q = (0, 0, 0, 1, 1, 2)
SPLIT_K = (0, 1, 2, 0, 1, 0)


class Count:

    def __init__(self, sem, base=0):
        self.sem, self.base, self.n = sem, base, 0

    def inc(self, instruction):
        instruction.then_inc(self.sem, 1)
        self.n += 1
        return self.base + self.n

    def wait(self, engine):
        engine.wait_ge(self.sem, self.base + self.n)


class Tensors:
    pass


def open_scope(nc, g=None):
    s = Tensors()
    s.count = 0
    if g is not None:
        g.count += 1
    tag = f"_{g.count}" if g is not None else ""
    s.ctx = ExitStack()
    s.sb = lambda name, shape, dt=F32: s.ctx.enter_context(nc.sbuf_tensor(name + tag, shape, dt))

    def sem(name):
        handle = s.ctx.enter_context(nc.semaphore(name + tag))
        if g is not None:
            g.used.append(handle)
        return handle
    s.sem = sem
    s.used = []
    return s


def clear_semaphores(nc, semaphores):
    numbers = sorted(sem.num for sem in semaphores)
    with nc.Block() as block:

        @block.gpsimd
        def _(pool):
            while numbers:
                first = last = numbers.pop(0)
                while numbers and numbers[0] <= last + 1:
                    last = numbers.pop(0)
                pool.sem_clear(range(first, last + 1))


def setup(nc, g, A):
    s = open_scope(nc, g)
    with s.ctx:
        loaded = s.sem("setup_loaded")
        copied = s.sem("setup_copied")
        block = s.ctx.enter_context(nc.Block())

        @block.sync
        def _(sp):
            sp.dma_start(g.x[:], A["x"].rearrange("(i p) d -> p i d", p=P)).then_inc(loaded, 16)
            sp.dma_start(g.ident[:], A["ident"]).then_inc(loaded, 16)
            sp.wait_ge(loaded, 32)

        @block.vector
        def _(dve):
            dve.wait_ge(loaded, 32)
            nc.vector.tensor_copy(g.identb[:], g.ident[:]).then_inc(copied, 1)
            dve.wait_ge(copied, 1)


def residual_norm(nc, g, first, last):
    s = open_scope(nc, g)
    ps = g.ps
    with s.ctx:
        stats = s.sb("ln_stats", [P, TILES, 6])
        mv = s.sb("ln_mv", [P, TILES, 2])
        std = s.sb("ln_std", [P, TILES])
        rstd = s.sb("ln_rstd", [P, TILES])
        xn = g.xn
        turned = s.sem("ln_turned")
        added = s.sem("ln_added")
        ve = s.sem("ln_vector_done")
        have_std = s.sem("ln_have_std")
        normed = s.sem("ln_normed")
        xturned = s.sem("ln_xturned")
        xcopied = s.sem("ln_xcopied")
        block = s.ctx.enter_context(nc.Block())

        @block.tensor
        def _(pe):
            if not first:
                for q in range(4):
                    for k in range(4):
                        i = 4 * q + k
                        mm = nc.tensor.transpose(ps[:, q, k * P:(k + 1) * P], g.branchT[:, i * P:(i + 1) * P], g.ident[:])
                    mm.then_inc(turned, 1)
            if not last:
                for q in range(4):
                    pe.wait_ge(normed, q + 1)
                    for k in range(4):
                        i = 4 * q + k
                        mm = nc.tensor.transpose(ps[:, 4 + q, k * P:(k + 1) * P], xn[:, i, :], g.ident[:])
                    mm.then_inc(xturned, 1)

        @block.vector
        def _(dve):
            if not first:
                for q in range(4):
                    dve.wait_ge(turned, q + 1)
                    nc.vector.tensor_tensor(g.x[:, 4 * q:4 * q + 4, :], g.x[:, 4 * q:4 * q + 4, :],
                                            ps[:, q, :].rearrange("p (k d) -> p k d", d=D), ALU.add).then_inc(added, 1)
            if last:
                dve.wait_ge(added, 4)
                return
            done = Count(ve)
            for i in range(TILES):
                if not first:
                    dve.wait_ge(added, i // 4 + 1)
                done.inc(nc.vector.bn_stats(stats[:, i, :], g.x[:, i, :]))
            done.wait(dve)
            for i in range(TILES):
                done.inc(nc.vector.bn_aggr(mv[:, i, :], stats[:, i, :]))
            done.wait(dve)
            done.inc(nc.vector.tensor_scalar(mv[:, :, 1], mv[:, :, 1], EPS, None, ALU.add))
            dve.wait_ge(have_std, 1)
            done.inc(nc.vector.reciprocal(rstd[:], std[:]))
            done.wait(dve)
            for i in range(TILES):
                op = nc.vector.tensor_scalar(xn[:, i, :], g.x[:, i, :], mv[:, i, 0:1], rstd[:, i:i + 1],
                                             ALU.subtract, ALU.mult)
                if i % 4 == 3:
                    op.then_inc(normed, 1)
            for q in range(0, 4, 2):
                dve.wait_ge(xturned, q + 1)
                nc.vector.tensor_copy(g.xnT[:, q * CH:(q + 1) * CH], ps[:, 4 + q, :]).then_inc(xcopied, 1)
            dve.wait_ge(xcopied, 4)

        @block.scalar
        def _(act):
            if last:
                return
            act.wait_ge(ve, 2 * TILES + 1)
            nc.scalar.activation(std[:], mv[:, :, 1], ACT.Sqrt).then_inc(have_std, 1)
            for q in range(1, 4, 2):
                act.wait_ge(xturned, q + 1)
                nc.scalar.copy(g.xnT[:, q * CH:(q + 1) * CH], ps[:, 4 + q, :]).then_inc(xcopied, 1)


def finish(nc, g, out):
    s = open_scope(nc, g)
    with s.ctx:
        stored = s.sem("x_stored")
        block = s.ctx.enter_context(nc.Block())

        @block.sync
        def _(sp):
            sp.dma_start(out.rearrange("(i p) d -> p i d", p=P), g.x[:]).then_inc(stored, 16)
            sp.wait_ge(stored, 16)


HEADS, HD = 16, 8


PAIR_STEPS = 11


def head_mixing(nc, g, s, W):
    QB, KB = 6, 7
    ps = g.ps
    scale = float(HD) ** -0.5
    HH = HEADS // 2
    wq = s.sb("wq", [P, 2, P])
    wup = s.sb("wup", [32, 3, P])
    wdown = s.sb("wdown", [P, 32])
    bdown = s.sb("bdown", [32, 1])
    bias = s.sb("bias", [P, 5, P])
    cos = s.sb("cos", [P, T // P, HD])
    sin = s.sb("sin", [P, T // P, HD])
    wout = s.sb("wout", [P, P])
    bout = s.sb("bout", [P, 1])
    xs = s.sb("xs", [P, 2, P])
    lat = s.sb("lat", [32, 2, P])
    proj = s.sb("proj", [P, 2, 5, P])
    rc = s.sb("rc", [P, 2, 2, P])
    rs = s.sb("rs", [P, 2, 2, P])
    qk = s.sb("qk", [P, 2, 2, P])
    prod = s.sb("prod", [P, 2, HEADS, HEADS, HD])
    att = s.sb("att", [P, 2, HEADS, HEADS])
    top = s.sb("top", [P, 2, HEADS])
    less = s.sb("less", [P, 2, HEADS, HEADS])
    prob = s.sb("prob", [P, 2, HEADS, HEADS])
    total = s.sb("total", [P, 2, HEADS])
    inv = s.sb("inv", [P, 2, HEADS])
    mixed = s.sb("mixed", [P, 2, HEADS, HD])
    norm = s.sb("norm", [P, 2, P])
    oT = s.sb("oT", [P, 2, P])
    loaded = s.sem("hm_loaded")
    staged = s.sem("hm_x_staged")
    latd = s.sem("hm_latent")
    latc = s.sem("hm_latent_copied")
    projd = s.sem("hm_projected")
    biased = s.sem("hm_biased")
    roped = s.sem("hm_roped")
    multd = s.sem("hm_scores_mult_dve")
    multp = s.sem("hm_scores_mult_pool")
    vec = s.sem("hm_vector_steps")
    expd = s.sem("hm_exp")
    wmd = s.sem("hm_weigh_mult_dve")
    wmp = s.sem("hm_weigh_mult_pool")
    normd = s.sem("hm_normal")
    turned = s.sem("hm_turned")
    tcopied = s.sem("hm_turned_copied")
    outd = s.sem("hm_out")
    outc = s.sem("hm_out_copied")
    tiles = dict(wq=wq, wup=wup, wdown=wdown, bdown=bdown, bias=bias, cos=cos, sin=sin, wout=wout, bout=bout)
    ALL = 16 * len(tiles)
    VS = 14

    def sync(sp):
        for n, t in tiles.items():
            sp.dma_start(t[:], W[n]).then_inc(loaded, 16)
        sp.wait_ge(loaded, ALL)

    def scalar(act, i, step, late):
        if (step, late) in ((0, False), (1, False)):
            e = step
            act.wait_ge(projd, i * 2 + e)
            nc.scalar.copy(xs[:, e, :], g.xnT[:, bass.ds((i * 2 + e) * P, P)]).then_inc(staged, 1)
        if (step, late) in ((0, True), (2, False)):
            e = step // 2
            act.wait_ge(latd, i * 2 + e + 1)
            nc.scalar.activation(lat[:, e, :], ps[0:32, KB, 384:512], ACT.Identity, bias=bdown[:]).then_inc(latc, 1)
        if (step, late) in ((4, True), (6, True)):
            e = (step - 4) // 2
            act.wait_ge(vec, i * VS + 4 * (e + 1))
            act.wait_ge(wmd, i * 2)
            act.wait_ge(wmp, i * 2)
            nc.scalar.activation(prob[:, e], less[:, e], ACT.Exp, scale=scale).then_inc(expd, 1)
        if (step, late) in ((9, False), (10, False)):
            e = step - 9
            act.wait_ge(turned, i * 2 + e + 1)
            nc.scalar.copy(oT[:, e, :], ps[:, KB, 0:P]).then_inc(tcopied, 1)
        if (step, late) in ((9, True), (10, True)):
            e = step - 9
            act.wait_ge(outd, i * 2 + e + 1)
            nc.scalar.activation(g.branchT[:, bass.ds((i * 2 + e) * P, P)], ps[:, QB, 384:512], ACT.Identity,
                                 bias=bout[:]).then_inc(outc, 1)

    def tensor(pe, i, step, late):
        if (step, late) in ((0, False), (1, True)):
            e = step
            pe.wait_ge(staged, i * 2 + e + 1)
            pe.wait_ge(biased, i * 2 + e)
            if e == 0:
                pe.wait_ge(outc, i * 2)
            nc.tensor.matmul(ps[0:32, KB, 384:512], wdown[:], xs[:, e, :], start=True, stop=True).then_inc(latd, 1)
            nc.tensor.matmul(ps[:, QB, 0:256], xs[:, e, :], wq[:].rearrange("p a n -> p (a n)"), start=True, stop=True)
        if (step, late) in ((0, True), (2, True)):
            e = step // 2
            pe.wait_ge(latc, i * 2 + e + 1)
            nc.tensor.matmul(ps[:, KB, 0:384], lat[:, e, :], wup[:].rearrange("p a n -> p (a n)"),
                             start=True, stop=True).then_inc(projd, 1)
        if (step, late) in ((9, False), (10, False)):
            e = step - 9
            pe.wait_ge(normd, i * 2 + e + 1)
            nc.tensor.transpose(ps[:, KB, 0:P], norm[:, e, :], g.ident[:]).then_inc(turned, 1)
        if (step, late) in ((9, True), (10, True)):
            e = step - 9
            pe.wait_ge(tcopied, i * 2 + e + 1)
            pe.wait_ge(outc, i * 2 + e)
            nc.tensor.matmul(ps[:, QB, 384:512], wout[:], oT[:, e, :], start=True, stop=True).then_inc(outd, 1)

    def scores_product(eng, e, h0):
        q = qk[:, e, 0, :].rearrange("p (h d) -> p h d", d=HD)[:, h0:h0 + HH, None, :].to_broadcast([P, HH, HEADS, HD])
        k = qk[:, e, 1, :].rearrange("p (g d) -> p g d", d=HD)[:, None, :, :].to_broadcast([P, HH, HEADS, HD])
        return eng.tensor_tensor(prod[:, e, h0:h0 + HH], q, k, ALU.mult)

    def weigh_product(eng, e, h0):
        a = prob[:, e, h0:h0 + HH, None, :].to_broadcast([P, HH, HD, HEADS])
        v = proj[:, e, 4, :].rearrange("p (g d) -> p d g", d=HD)[:, None, :, :].to_broadcast([P, HH, HD, HEADS])
        dst = prod[:, e, h0:h0 + HH].rearrange("p h g d -> p h (g d)").rearrange("p h (d g) -> p h d g", g=HEADS)
        return eng.tensor_tensor(dst, a, v, ALU.mult)

    def gpsimd(pool):
        pool.wait_ge(loaded, ALL)
        with pool.Fori(0, TILES // 2) as i:
            for e in range(2):
                n = (i * 2 + e) * 3
                pool.wait_ge(biased, i * 2 + e + 1)
                where = bass.ds((i * 2 + e) % (T // P), 1)
                c = cos[:, where, :].to_broadcast([P, HEADS, HD])
                sn = sin[:, where, :].to_broadcast([P, HEADS, HD])
                v = lambda t: t.rearrange("p (h d) -> p h d", d=HD)
                for j in range(2):
                    nc.gpsimd.tensor_tensor(v(rc[:, e, j, :]), v(proj[:, e, 2 * j, :]), c, ALU.mult)
                    last = nc.gpsimd.tensor_tensor(v(rs[:, e, j, :]), v(proj[:, e, 2 * j + 1, :]), sn, ALU.mult)
                last.then_inc(roped, 1)
                pool.wait_ge(roped, n + 1)
                pool.wait_ge(multd, i * 2)
                nc.gpsimd.tensor_tensor(qk[:, e], rc[:, e], rs[:, e], ALU.add).then_inc(roped, 1)
                pool.wait_ge(roped, n + 2)
                pool.wait_ge(vec, i * VS)
                scores_product(nc.gpsimd, e, HH).then_inc(roped, 1)
                pool.wait_ge(roped, n + 3)
                pool.sem_inc(multp, 1)
            for e in range(2):
                pool.wait_ge(expd, i * 2 + e + 1)
                weigh_product(nc.gpsimd, e, HH).then_inc(wmp, 1)

    def add_bias(dve, i, e):
        dve.wait_ge(projd, i * 2 + e + 1)
        dve.wait_ge(wmp, i * 2)
        nc.vector.tensor_tensor(proj[:, e, 0:2, :], ps[:, QB, 0:256].rearrange("p (a n) -> p a n", a=2), bias[:, 0:2, :], ALU.add)
        nc.vector.tensor_tensor(proj[:, e, 2:5, :], ps[:, KB, 0:384].rearrange("p (a n) -> p a n", a=3), bias[:, 2:5, :],
                                ALU.add).then_inc(biased, 1)

    def vector(dve, i, step, late):
        base = i * VS
        for e in range(2):
            n = base + 4 * e
            if (step, late) == (2 * e, True):
                add_bias(dve, i, e)
            if (step, late) == (2 + 2 * e, True):
                dve.wait_ge(roped, (i * 2 + e) * 3 + 2)
                scores_product(nc.vector, e, 0).then_inc(multd, 1)
            if (step, late) == (3 + 2 * e, True):
                dve.wait_ge(multd, i * 2 + e + 1)
                dve.wait_ge(multp, i * 2 + e + 1)
                nc.vector.tensor_reduce(att[:, e].rearrange("p h g -> p (h g)"), prod[:, e].rearrange("p h g d -> p (h g) d"),
                                        AX.X, ALU.add).then_inc(vec, 1)
            if (step, late) == (4 + 2 * e, False):
                dve.wait_ge(vec, n + 1)
                nc.vector.tensor_reduce(top[:, e], att[:, e], AX.X, ALU.max).then_inc(vec, 1)
                dve.wait_ge(vec, n + 2)
                nc.vector.tensor_tensor(less[:, e], att[:, e], top[:, e, :, None].to_broadcast([P, HEADS, HEADS]),
                                        ALU.subtract).then_inc(vec, 2)
        for e in range(2):
            n = base + 8 + 3 * e
            if (step, late) == (6 + 2 * e, True):
                dve.wait_ge(expd, i * 2 + e + 1)
                nc.vector.tensor_reduce(total[:, e], prob[:, e], AX.X, ALU.add).then_inc(vec, 1)
                weigh_product(nc.vector, e, 0).then_inc(wmd, 1)
            if (step, late) == (7 + 2 * e, True):
                dve.wait_ge(vec, n + 1)
                nc.vector.reciprocal(inv[:, e], total[:, e]).then_inc(vec, 1)
                dve.wait_ge(wmd, i * 2 + e + 1)
                dve.wait_ge(wmp, i * 2 + e + 1)
                nc.vector.tensor_reduce(mixed[:, e].rearrange("p h d -> p (h d)"),
                                        prod[:, e].rearrange("p h g d -> p h (g d)").rearrange("p h (d g) -> p (h d) g", g=HEADS),
                                        AX.X, ALU.add).then_inc(vec, 1)
            if (step, late) == (8 + 2 * e, False):
                dve.wait_ge(vec, n + 3)
                dve.wait_ge(turned, i * 2)
                nc.vector.tensor_tensor(norm[:, e, :].rearrange("p (h d) -> p h d", d=HD), mixed[:, e],
                                        inv[:, e, :, None].to_broadcast([P, HEADS, HD]), ALU.mult).then_inc(normd, 1)

    steps = Tensors()
    steps.sync, steps.tensor, steps.scalar, steps.vector, steps.gpsimd = sync, tensor, scalar, vector, gpsimd
    steps.loaded, steps.all_loaded, steps.out_copied = loaded, ALL, outc
    return steps


def split_qk(nc, g, qk, W, qscale):
    s = open_scope(nc, g)
    ps = g.ps
    with s.ctx:
        wqk = s.sb("wqk", [P, 2, P])
        bias = s.sb("qk_bias", [P, 2])
        whole = s.sb("whole", [P, 2, CH])
        rest = s.sb("rest", [P, 2, CH])
        parts = s.sb("parts", [P, 2, 3, CH], BF16)
        loaded = s.sem("qk_loaded")
        product = s.sem("qk_product")
        wholed = s.sem("qk_whole")
        hi_done = s.sem("hi_done")
        rest_done = s.sem("rest_done")
        mid_done = s.sem("mid_done")
        lo_done = s.sem("lo_done")
        stored = [s.sem(f"parts_stored{j}") for j in range(2)]
        block = s.ctx.enter_context(nc.Block())

        @block.sync
        def _(sp):
            sp.dma_start(wqk[:], W["wqk"]).then_inc(loaded, 16)
            sp.dma_start(bias[:], W["bqk"]).then_inc(loaded, 16)
            with sp.Fori(0, NCH) as c:
                for j in range(2):
                    sp.wait_ge(lo_done, c * 2 + (j + 1))
                    dst = qk[j].rearrange("s p n -> p s n")[:, :, bass.ds(c * CH, CH)]
                    sp.dma_start(dst, parts[:, j, :, :]).then_inc(stored[j], 16)
            for j in range(2):
                sp.wait_ge(stored[j], 16 * NCH)

        @block.tensor
        def _(pe):
            pe.wait_ge(loaded, 32)
            with pe.Fori(0, NCH) as c:
                for j in range(2):
                    pe.wait_ge(wholed, c * 2 + j)
                    nc.tensor.matmul(ps[:, j, :], wqk[:, j, :], g.xnT[:, bass.ds(c * CH, CH)],
                                     start=True, stop=True).then_inc(product, 1)

        @block.scalar
        def _(act):
            with act.Fori(0, NCH) as c:
                for j in range(2):
                    act.wait_ge(wholed, c * 2 + (j + 1))
                    act.wait_ge(stored[j], c * 16)
                    nc.scalar.copy(parts[:, j, 0, :], whole[:, j, :]).then_inc(hi_done, 1)
                    act.wait_ge(rest_done, c * 2 + (j + 1))
                    nc.scalar.copy(parts[:, j, 1, :], rest[:, j, :]).then_inc(mid_done, 1)

        @block.vector
        def _(dve):
            dve.wait_ge(loaded, 32)
            with dve.Fori(0, NCH) as c:
                for j in range(2):
                    dve.wait_ge(product, c * 2 + (j + 1))
                    dve.wait_ge(lo_done, c * 2 + j)
                    nc.vector.tensor_scalar(whole[:, j, :], ps[:, j, :], bias[:, j:j + 1], qscale if j == 0 else 1.0,
                                            ALU.add, ALU.mult).then_inc(wholed, 1)
                    dve.wait_ge(hi_done, c * 2 + (j + 1))
                    nc.vector.tensor_tensor(rest[:, j, :], whole[:, j, :], parts[:, j, 0, :], ALU.subtract).then_inc(rest_done, 1)
                    dve.wait_ge(mid_done, c * 2 + (j + 1))
                    nc.vector.tensor_tensor(parts[:, j, 2, :], rest[:, j, :], parts[:, j, 1, :], ALU.subtract).then_inc(lo_done, 1)


def value_tiles(nc, g, Vp, W):
    s = open_scope(nc, g)
    with s.ctx:
        wv = s.sb("wv", [P, P])
        bv = s.sb("bv", [P, P])
        loaded = s.sem("v_loaded")
        product = s.sem("v_product")
        written = s.sem("v_written")
        block = s.ctx.enter_context(nc.Block())

        @block.sync
        def _(sp):
            sp.dma_start(wv[:], W["wv"]).then_inc(loaded, 16)
            sp.dma_start(bv[:], W["bv"]).then_inc(loaded, 16)
            sp.wait_ge(loaded, 32)

        @block.tensor
        def _(pe):
            pe.wait_ge(loaded, 32)
            for i in range(TILES):
                mm = nc.tensor.matmul(g.ps[:, i // 4, (i % 4) * P:(i % 4 + 1) * P], g.xnT[:, i * P:(i + 1) * P], wv[:],
                                      start=True, stop=True)
                if i % 4 == 3:
                    mm.then_inc(product, 1)

        @block.vector
        def _(dve):
            dve.wait_ge(loaded, 32)
            for q in range(TILES // 4):
                dve.wait_ge(product, q + 1)
                nc.vector.tensor_tensor(Vp[:, 4 * q:4 * q + 4, :], g.ps[:, q, :].rearrange("p (i n) -> p i n", n=P),
                                        bv[:, None, :].to_broadcast([P, 4, P]), ALU.add).then_inc(written, 1)
            dve.wait_ge(written, TILES // 4)


STACK = HD * len(SPLIT_Q)
QUAD = 4
STEPS = B * HEADS // QUAD
KT = T // P


def stage_heads(sp, nc, qk, Q, K, n, landed):
    b, h0 = n // 4, (n % 4) * 4
    for dst, which, terms in ((Q, 0, SPLIT_Q), (K, 1, SPLIT_K)):
        src = qk[which].rearrange("s (h j) n -> s j h n", j=HD)
        for t, part in enumerate(terms):
            sp.dma_start(dst[HD * t:HD * (t + 1), :, :],
                         src[part][:, bass.ds(h0, 4), bass.ds(b * T, T)]).then_inc(landed, 16)


def column_softmax_attention(nc, g, qk, Vp, W):
    s = open_scope(nc, g)
    ps = g.ps
    AV = 6
    UN = KT * QUAD
    RING = 3
    PR = 8
    with s.ctx:
        Q = [s.sb(f"Q{i}", [P, QUAD, T], BF16) for i in range(2)]
        K = [s.sb(f"K{i}", [P, QUAD, T], BF16) for i in range(2)]
        V = [s.sb(f"V{i}", [P, KT, QUAD, HD]) for i in range(2)]
        probs = s.sb("probs", [P, PR, T])
        negmax = s.sb("negmax", [P, PR])
        total = s.sb("total", [P, PR])
        inv = s.sb("inv", [P, 2, QUAD])
        vdiv = s.sb("vdiv", [P, 2, QUAD, 32])
        outT = s.sb("outT", [P, 4, NT])
        mask = s.sb("mask", [P, P])
        maskb = s.sb("maskb", [P, P], BF16)
        wout = s.sb("wout", [P, 4, P])
        bout = s.sb("bout", [P, 1])
        const = s.sem("ca_const")
        cleared = s.sem("ca_cleared")
        vcleared = s.sem("ca_v_cleared")
        maskd = s.sem("ca_mask")
        landed = [s.sem(f"ca_landed{i}") for i in range(2)]
        vstaged = s.sem("ca_v_staged")
        sc = s.sem("ca_scores")
        mx = s.sem("ca_max")
        ex = s.sem("ca_exp")
        invd = s.sem("ca_inverse")
        vd = s.sem("ca_v_divided")
        av = s.sem("ca_weighed")
        oc = s.sem("ca_out_copied")
        oproj = s.sem("ca_projected")
        ocopy = s.sem("ca_projected_copied")
        block = s.ctx.enter_context(nc.Block())

        @block.sync
        def _(sp):
            sp.dma_start(mask[:], W["mask"]).then_inc(const, 16)
            sp.dma_start(wout[:], W["wout"]).then_inc(const, 16)
            sp.dma_start(bout[:], W["bout"]).then_inc(const, 16)
            sp.wait_ge(cleared, 4)
            for e in range(2):
                stage_heads(sp, nc, qk, Q[e], K[e], e, landed[e])
            with sp.Fori(0, STEPS // 2 - 1) as i:
                for e in range(2):
                    sp.wait_ge(sc, i * 2 * UN + (e + 1) * UN)
                    stage_heads(sp, nc, qk, Q[e], K[e], i * 2 + (e + 2), landed[e])
            sp.wait_ge(const, 48)
            for e in range(2):
                sp.wait_ge(landed[e], 16 * 12 * STEPS // 2)

        @block.gpsimd
        def _(pool):
            nc.gpsimd.memset(vdiv[:], 0.0).then_inc(vcleared, 1)
            pool.wait_ge(vcleared, 1)

            def stage_v(n, e):
                nc.gpsimd.tensor_copy(V[e][:], Vp[:, bass.ds((n // 4) * KT, KT), bass.ds((n % 4) * QUAD * HD, QUAD * HD)]
                                      .rearrange("p i (h d) -> p i h d", d=HD)).then_inc(vstaged, 1)

            def divide(n, e):
                for jt in range(KT):
                    pool.wait_ge(invd, n * KT + (jt + 1))
                    pool.wait_ge(vstaged, n + 1)
                    pool.wait_ge(av, n * KT + max(jt - 1, 0))
                    nc.gpsimd.tensor_tensor(vdiv[:, jt % 2, :, 0:HD], V[e][:, jt],
                                            inv[:, jt % 2, :, None].to_broadcast([P, QUAD, HD]), ALU.mult).then_inc(vd, 1)

            for e in range(2):
                nc.gpsimd.tensor_copy(V[e][:], Vp[:, 0:KT, e * QUAD * HD:(e + 1) * QUAD * HD]
                                      .rearrange("p i (h d) -> p i h d", d=HD)).then_inc(vstaged, 1)
            with pool.Fori(0, STEPS // 2 - 1) as i:
                for e in range(2):
                    divide(i * 2 + e, e)
                    pool.wait_ge(vd, i * 2 * KT + (e + 1) * KT)
                    stage_v(i * 2 + (e + 2), e)
            for e in range(2):
                divide(STEPS - 2 + e, e)

        @block.tensor
        def _(pe):
            def scores(n, e, rnd, u):
                jt, h = u // QUAD, u % QUAD
                if u == 0:
                    pe.wait_ge(landed[e], rnd * 192 + 192)
                if u >= RING:
                    pe.wait_ge(ex, n * UN + (u - RING + 1))
                else:
                    pe.wait_ge(ex, n * UN)
                bank = 2 * (u % RING)
                for half in range(2):
                    a, b = max(jt * P, half * CH), (half + 1) * CH
                    if a >= b:
                        continue
                    diag = jt // 4 == half
                    mm = nc.tensor.matmul(ps[:, bank + half, a % CH:CH], K[e][:, h, jt * P:(jt + 1) * P], Q[e][:, h, a:b],
                                          start=True, stop=not diag)
                    if diag:
                        a = jt % 4 * P
                        mm = nc.tensor.matmul(ps[:, bank + half, a:a + P], g.identb[:], maskb[:], start=False, stop=True)
                mm.then_inc(sc, 1)

            def weigh(n, jt):
                pe.wait_ge(vd, n * KT + (jt + 1))
                if jt == 0:
                    pe.wait_ge(oc, n)
                for half in range(2):
                    a, b = max(jt * P, half * CH), (half + 1) * CH
                    if a >= b:
                        continue
                    for h in range(QUAD):
                        mm = nc.tensor.matmul(ps[32 * h:32 * h + 32, AV + half, a % CH:CH], vdiv[:, jt % 2, h, :],
                                              probs[:, (jt * QUAD + h) % PR, a:b],
                                              start=(jt == 0), stop=(jt == (3 if half == 0 else KT - 1)))
                mm.then_inc(av, 1)

            def step(n, e, rnd):
                for u in range(UN):
                    scores(n, e, rnd, u)
                    if u % QUAD == QUAD - 1 and u > QUAD:
                        weigh(n, u // QUAD - 1)
                weigh(n, KT - 1)

            pe.wait_ge(const, 48)
            pe.wait_ge(maskd, 1)
            with pe.Fori(0, STEPS // 2) as i:
                for e in range(2):
                    step(i * 2 + e, e, i)
            pe.wait_ge(oc, STEPS)
            for c in range(NCH):
                if c >= 2:
                    pe.wait_ge(ocopy, c - 1)
                for q in range(4):
                    mm = nc.tensor.matmul(ps[:, c % 2, :], wout[:, q, :], outT[:, q, c * CH:(c + 1) * CH],
                                          start=(q == 0), stop=(q == 3))
                mm.then_inc(oproj, 1)

        @block.scalar
        def _(act):
            with act.Fori(0, STEPS) as n:
                for u in range(UN):
                    jt = u // QUAD
                    act.wait_ge(mx, n * UN + (u + 1))
                    if u % QUAD == 0:
                        act.wait_ge(av, n * KT + max(jt - 1, 0))
                    bank = 2 * (u % RING)
                    src = ps[:, bank:bank + 2, :].rearrange("p b n -> p (b n)")[:, jt * P:T]
                    nc.scalar.activation(probs[:, u % PR, jt * P:T], src, ACT.Exp, bias=negmax[:, u % PR:u % PR + 1],
                                         accum_out=total[:, u % PR:u % PR + 1]).then_inc(ex, 1)
                act.wait_ge(av, n * KT + KT)
                dst = outT[:, bass.ds(n % 4, 1), bass.ds((n // 4) * T, T)].rearrange("p a n -> p (a n)")
                nc.scalar.copy(dst, ps[:, AV:AV + 2, :].rearrange("p b n -> p (b n)")).then_inc(oc, 1)
            for c in range(NCH):
                act.wait_ge(oproj, c + 1)
                nc.scalar.activation(g.branchT[:, c * CH:(c + 1) * CH], ps[:, c % 2, :], ACT.Identity,
                                     bias=bout[:]).then_inc(ocopy, 1)
            act.wait_ge(ocopy, NCH)

        @block.vector
        def _(dve):
            for t in (*Q, *K):
                nc.vector.memset(t[:], 0.0).then_inc(cleared, 1)
            dve.wait_ge(const, 48)
            nc.vector.tensor_copy(maskb[:], mask[:]).then_inc(maskd, 1)

            def inverse(n, jt):
                dve.wait_ge(ex, n * UN + (jt + 1) * QUAD)
                dve.wait_ge(vd, n * KT + max(jt - 1, 0))
                a = jt % 2 * QUAD
                nc.vector.reciprocal(inv[:, jt % 2, :], total[:, a:a + QUAD]).then_inc(invd, 1)

            with dve.Fori(0, STEPS) as n:
                for u in range(UN):
                    jt = u // QUAD
                    dve.wait_ge(sc, n * UN + (u + 1))
                    if u % QUAD == 0:
                        dve.wait_ge(ex, n * UN + max(u - QUAD, 0))
                    bank = 2 * (u % RING)
                    src = ps[:, bank:bank + 2, :].rearrange("p b n -> p (b n)")[:, jt * P:T]
                    nc.vector.tensor_reduce(negmax[:, u % PR:u % PR + 1], src, AX.X, ALU.max, negate=True).then_inc(mx, 1)
                    if u % QUAD == 1 and jt:
                        inverse(n, jt - 1)
                inverse(n, KT - 1)


def route(nc, g, W, combT, experts, top, kind):
    s = open_scope(nc, g)
    ps = g.ps
    E = experts
    with s.ctx:
        wr = s.sb("wr", [P, E])
        br = s.sb("br", [P, E])
        wh = s.sb("wh", [P, 32])
        hT = s.sb("hT", [32, NT])
        wkeys = s.sb("wkeys", [32, E])
        scale = s.sb("scale", [P, 1])
        iota = s.sb("iota", [P, E])
        logit = s.sb("logit", [P, TILES, E])
        val = s.sb("val", [P, TILES, E])
        pick = s.sb("pick", [P, TILES, E])
        top8 = s.sb("top8", [P, TILES, 8])
        idx8 = s.sb("idx8", [P, TILES, 8], U32)
        idxf = s.sb("idxf", [P, TILES, 8])
        same = s.sb("same", [P, top, TILES, E])
        total = s.sb("total", [P, TILES])
        inv = s.sb("inv", [P, TILES])
        rest = s.sb("rest", [P, TILES, E])
        parts = s.sb("parts", [P, TILES, 3, E], BF16)
        loaded = s.sem("rt_loaded")
        hashed = s.sem("rt_hashed")
        hcopied = s.sem("rt_hash_copied")
        product = s.sem("rt_logits")
        activ = s.sem("rt_activated")
        ve = s.sem("rt_vector_done")
        split = s.sem("rt_split")
        cleared = s.sem("rt_cleared")
        turned = s.sem("rt_turned")
        copied = s.sem("rt_copied")
        block = s.ctx.enter_context(nc.Block())
        tiles = dict(wr=wr, br=br, iota=iota)
        if kind == "keys":
            tiles = dict(wh=wh, wkeys=wkeys, scale=scale, iota=iota)
        ALL = 16 * len(tiles)

        @block.sync
        def _(sp):
            for n, t in tiles.items():
                sp.dma_start(t[:], W[n]).then_inc(loaded, 16)
            sp.wait_ge(loaded, ALL)

        @block.gpsimd
        def _(pool):
            nc.gpsimd.memset(combT[:], 0.0).then_inc(cleared, 1)

        @block.tensor
        def _(pe):
            pe.wait_ge(loaded, ALL)
            if kind == "keys":
                for c in range(NCH):
                    nc.tensor.matmul(ps[0:32, 1 + c, :], wh[:], g.xnT[:, c * CH:(c + 1) * CH], start=True, stop=True).then_inc(hashed, 1)
                pe.wait_ge(hcopied, NCH)
            for i in range(TILES):
                lhs, rhs = (hT, wkeys) if kind == "keys" else (g.xnT, wr)
                mm = nc.tensor.matmul(ps[:, 0, i * E:(i + 1) * E], lhs[:, i * P:(i + 1) * P], rhs[:], start=True, stop=True)
            mm.then_inc(product, 1)
            pe.wait_ge(split, 1)
            for c in range(NCH):
                for k in range(4):
                    mm = nc.tensor.matmul(ps[0:3 * E, 4 + c, k * P:(k + 1) * P],
                                          parts[:, 4 * c + k].rearrange("p s e -> p (s e)"), g.identb[:], start=True, stop=True)
                mm.then_inc(turned, 1)

        @block.scalar
        def _(act):
            if kind == "keys":
                for c in range(NCH):
                    act.wait_ge(hashed, c + 1)
                    nc.scalar.copy(hT[:, c * CH:(c + 1) * CH], ps[0:32, 1 + c, :]).then_inc(hcopied, 1)
            act.wait_ge(ve, 1)
            if kind == "sigmoid":
                nc.scalar.activation(val[:], logit[:], ACT.Sigmoid).then_inc(activ, 1)
            else:
                act.wait_ge(ve, 2 + TILES)
                nc.scalar.activation(val[:], rest[:], ACT.Exp).then_inc(activ, 1)
            act.wait_ge(cleared, 1)
            for c in range(NCH):
                act.wait_ge(turned, c + 1)
                nc.scalar.copy(combT[0:3 * E, c * CH:(c + 1) * CH], ps[0:3 * E, 4 + c, :]).then_inc(copied, 1)
            act.wait_ge(copied, NCH)

        @block.vector
        def _(dve):
            done = Count(ve)
            wide = lambda t, k: t[:, :, k:k + 1].to_broadcast([P, TILES, E])
            dve.wait_ge(loaded, ALL)
            dve.wait_ge(product, 1)
            lg = ps[:, 0, 0:TILES * E].rearrange("p (i e) -> p i e", e=E)
            if kind == "softmax":
                done.inc(nc.vector.tensor_tensor(logit[:], lg, br[:, None, :].to_broadcast([P, TILES, E]), ALU.add))
            else:
                done.inc(nc.vector.tensor_copy(logit[:], lg))
            done.wait(dve)
            chosen_by = logit
            if kind == "sigmoid":
                dve.wait_ge(activ, 1)
                done.inc(nc.vector.tensor_tensor(rest[:], val[:], br[:, None, :].to_broadcast([P, TILES, E]), ALU.add))
                done.wait(dve)
                chosen_by = rest
            for i in range(TILES):
                done.inc(nc.vector.max(top8[:, i, :], chosen_by[:, i, :]))
            done.wait(dve)
            if kind != "sigmoid":
                done.inc(nc.vector.tensor_tensor(rest[:], logit[:], wide(top8, 0), ALU.subtract))
            for i in range(TILES):
                done.inc(nc.vector.max_index(idx8[:, i, :], top8[:, i, :], chosen_by[:, i, :]))
            done.wait(dve)
            done.inc(nc.vector.tensor_copy(idxf[:], idx8[:]))
            done.wait(dve)
            for k in range(top):
                done.inc(nc.vector.tensor_tensor(same[:, k], iota[:, None, :].to_broadcast([P, TILES, E]), wide(idxf, k), ALU.is_equal))
            done.wait(dve)
            done.inc(nc.vector.tensor_tensor(pick[:], same[:, 0], same[:, 1], ALU.add))
            for k in range(2, top):
                done.wait(dve)
                done.inc(nc.vector.tensor_tensor(pick[:], pick[:], same[:, k], ALU.add))
            dve.wait_ge(activ, 1)
            done.wait(dve)
            done.inc(nc.vector.tensor_tensor(pick[:], pick[:], val[:], ALU.mult))
            done.wait(dve)
            done.inc(nc.vector.tensor_reduce(total[:], pick[:], AX.X, ALU.add))
            done.wait(dve)
            done.inc(nc.vector.reciprocal(inv[:], total[:]))
            done.wait(dve)
            if kind == "keys":
                done.inc(nc.vector.tensor_scalar(inv[:], inv[:], scale[:, 0:1], None, ALU.mult))
                done.wait(dve)
            done.inc(nc.vector.tensor_tensor(val[:], pick[:], inv[:, :, None].to_broadcast([P, TILES, E]), ALU.mult))
            done.wait(dve)
            done.inc(nc.vector.tensor_copy(parts[:, :, 0, :], val[:]))
            done.wait(dve)
            done.inc(nc.vector.tensor_tensor(rest[:], val[:], parts[:, :, 0, :], ALU.subtract))
            done.wait(dve)
            done.inc(nc.vector.tensor_copy(parts[:, :, 1, :], rest[:]))
            done.wait(dve)
            nc.vector.tensor_tensor(parts[:, :, 2, :], rest[:], parts[:, :, 1, :], ALU.subtract).then_inc(split, 1)


def gated_experts(nc, g, W, experts, hidden, top, kind, gated=True, add=False, add_xn=False, beside=None):
    units = experts * hidden
    FT = -(-units // P)
    s = open_scope(nc, g)
    ps = g.ps
    GB, UB, CB, OB = 0, 2, 4, 5
    with s.ctx:
        combT = s.sb("combT", [P, NT], BF16)
        route(nc, g, W, combT, experts, top, kind)
        wg = s.sb("wg", [P, FT, P])
        wu = s.sb("wu", [P, FT, P]) if gated else None
        wd = s.sb("wd", [P, FT, P])
        sel = s.sb("sel", [P, FT, P], BF16)
        act_g = s.sb("act_g", [P, 2, CH])
        gu = s.sb("gu", [P, 2, CH])
        hid = s.sb("hid", [P, 2, CH])
        PIECE = 4
        pieces = -(-FT // PIECE)
        loaded = [s.sem(f"ge_loaded{k}") for k in range(pieces)]
        up = s.sem("ge_up")
        silud = s.sem("ge_silu")
        gud = s.sem("ge_gu")
        hidd = s.sem("ge_hidden")
        down = s.sem("ge_down")
        stored = s.sem("ge_out_copied")
        summed = s.sem("ge_out_summed")
        side = beside(nc, g, s, W) if beside else None
        block = s.ctx.enter_context(nc.Block())

        def along(engine, work, c, f, late):
            if side and f < 2 * PAIR_STEPS:
                work(engine, c * 2 + f // PAIR_STEPS, f % PAIR_STEPS, late)
        todo = [("wg", wg), ("wd", wd), ("sel", sel)] + ([("wu", wu)] if gated else [])

        @block.sync
        def _(sp):
            if side:
                side.sync(sp)
            for k in range(pieces):
                a, b = k * PIECE, min((k + 1) * PIECE, FT)
                for n, t in todo:
                    sp.dma_start(t[:, a:b, :], W[n][:, a:b, :]).then_inc(loaded[k], 16)
            for k in range(pieces):
                sp.wait_ge(loaded[k], 16 * len(todo))

        @block.gpsimd
        def _(pool):
            if side:
                side.gpsimd(pool)

        @block.tensor
        def _(pe):
            if side:
                pe.wait_ge(side.loaded, side.all_loaded)
            with pe.Fori(0, NCH) as c:
                where = bass.ds(c * CH, CH)
                n = c * FT

                def down_proj(f):
                    pe.wait_ge(hidd, n + (f + 1))
                    if f == 0:
                        pe.wait_ge(stored, c)
                    nc.tensor.matmul(ps[:, OB, :], wd[:, f, :], hid[:, f % 2, :], start=(f == 0), stop=(f == FT - 1)).then_inc(down, 1)

                for f in range(FT):
                    if f % PIECE == 0:
                        pe.wait_ge(loaded[f // PIECE], 16 * len(todo))
                    if f >= 2:
                        pe.wait_ge(hidd, n + (f - 1))
                    if side:
                        along(pe, side.tensor, c, f, False)
                    nc.tensor.matmul(ps[:, GB + f % 2, :], wg[:, f, :], g.xnT[:, where], start=True, stop=True).then_inc(up, 1)
                    if gated:
                        nc.tensor.matmul(ps[:, UB + f % 2, :], wu[:, f, :], g.xnT[:, where], start=True, stop=True)
                    pe.wait_ge(hidd, n + f)
                    nc.tensor.matmul(ps[:, CB, :], sel[:, f, :], combT[:, where], start=True, stop=True).then_inc(up, 1)
                    if f >= 1:
                        down_proj(f - 1)
                    if side:
                        along(pe, side.tensor, c, f, True)
                down_proj(FT - 1)

        @block.scalar
        def _(act):
            if side:
                act.wait_ge(side.loaded, side.all_loaded)
            with act.Fori(0, NCH) as c:
                n = c * FT
                for f in range(FT):
                    if side:
                        along(act, side.scalar, c, f, False)
                    act.wait_ge(up, n * 2 + (2 * f + 1))
                    act.wait_ge(gud if gated else hidd, n + (f - 1) if f >= 2 else n)
                    nc.scalar.activation(act_g[:, f % 2, :], ps[:, GB + f % 2, :], ACT.Silu).then_inc(silud, 1)
                    if side:
                        along(act, side.scalar, c, f, True)

        @block.vector
        def _(dve):
            if side:
                dve.wait_ge(side.loaded, side.all_loaded)
            with dve.Fori(0, NCH) as c:
                n = c * FT
                where = bass.ds(c * CH, CH)
                for f in range(FT):
                    if side:
                        along(dve, side.vector, c, f, False)
                    dve.wait_ge(up, n * 2 + (2 * f + 2))
                    dve.wait_ge(silud, n + (f + 1))
                    if f >= 2:
                        dve.wait_ge(down, n + (f - 1))
                    if gated:
                        nc.vector.tensor_tensor(gu[:, f % 2, :], act_g[:, f % 2, :], ps[:, UB + f % 2, :], ALU.mult).then_inc(gud, 1)
                        dve.wait_ge(gud, n + (f + 1))
                    nc.vector.tensor_tensor(hid[:, f % 2, :], (gu if gated else act_g)[:, f % 2, :], ps[:, CB, :],
                                            ALU.mult).then_inc(hidd, 1)
                    if side:
                        along(dve, side.vector, c, f, True)
                dve.wait_ge(down, n + FT)
                if side:
                    dve.wait_ge(side.out_copied, c * 4 + 4)
                if add or side:
                    nc.vector.tensor_tensor(g.branchT[:, where], g.branchT[:, where], ps[:, OB, :], ALU.add).then_inc(stored, 1)
                else:
                    nc.vector.tensor_copy(g.branchT[:, where], ps[:, OB, :]).then_inc(stored, 1)
                if add_xn:
                    dve.wait_ge(stored, c + 1)
                    nc.vector.tensor_tensor(g.branchT[:, where], g.branchT[:, where], g.xnT[:, where], ALU.add).then_inc(summed, 1)
            dve.wait_ge(stored, NCH)
            if add_xn:
                dve.wait_ge(summed, NCH)


DI, NS, DTR, TAPS = 256, 16, 64, 4
G = DI // P
PADT = T + TAPS - 1
DT_MIN, DT_MAX = 0.001, 0.1


def scan_inputs(nc, g, W, t):
    s = open_scope(nc, g)
    ps = g.ps
    XS, RES, CV, DTB, BCB = 0, 2, 4, 6, 7
    with s.ctx:
        win = s.sb("win", [P, 4, P])
        convk = s.sb("convk", [P, G, TAPS, P])
        convb = s.sb("convb", [P, G])
        wxdt = s.sb("wxdt", [P, G, DTR])
        wxbc = s.sb("wxbc", [P, G, 96])
        wdt = s.sb("wdt", [DTR, G, P])
        bdt = s.sb("bdt", [P, G])
        alog = s.sb("alog", [P, G, NS])
        xs = s.sb("xs", [P, G, B * PADT])
        dtraw = s.sb("dtraw", [DTR, 2, CH])
        rest = s.sb("rest", [96, 2, CH])
        mid = s.sb("mid", [96, 2, CH], BF16)
        loaded = s.sem("si_loaded")
        cleared = s.sem("si_cleared")
        xsd, xsc = s.sem("si_xs"), s.sem("si_xs_copied")
        resd, resc = s.sem("si_res"), s.sem("si_res_silu")
        cvd, cvc = s.sem("si_conv"), s.sem("si_u")
        prd, dtc = s.sem("si_dt_bc"), s.sem("si_dt_copied")
        bcs = s.sem("si_bc_split")
        dpd, dpc = s.sem("si_dt_projected"), s.sem("si_dt_clamped")
        expd, lnd, clipd, dud = s.sem("si_exp"), s.sem("si_ln"), s.sem("si_clipped"), s.sem("si_du")
        block = s.ctx.enter_context(nc.Block())
        tiles = dict(win=win, convk=convk, convb=convb, wxdt=wxdt, wxbc=wxbc, wdt=wdt, bdt=bdt, alog=alog)
        ALL = 16 * (len(tiles) + 2)

        @block.sync
        def _(sp):
            for n, d in tiles.items():
                sp.dma_start(d[:], W[n]).then_inc(loaded, 16)
            sp.dma_start(t.seln[:], W["seln"]).then_inc(loaded, 16)
            sp.dma_start(t.Dskip[:], W["D"]).then_inc(loaded, 16)
            sp.wait_ge(loaded, ALL)

        def at(c, tap=TAPS - 1):
            return bass.ds(c * CH + (c // 2) * (TAPS - 1) + tap, CH)

        @block.tensor
        def _(pe):
            pe.wait_ge(loaded, ALL)
            pe.wait_ge(cleared, 1)
            with pe.Fori(0, NCH) as c:
                here = bass.ds(c * CH, CH)
                pe.wait_ge(xsc, c)
                pe.wait_ge(dpc, c)
                for k in range(G):
                    mm = nc.tensor.matmul(ps[:, XS + k, :], win[:, k, :], g.xnT[:, here], start=True, stop=True)
                mm.then_inc(xsd, 1)
                pe.wait_ge(resc, c)
                for k in range(G):
                    mm = nc.tensor.matmul(ps[:, RES + k, :], win[:, G + k, :], g.xnT[:, here], start=True, stop=True)
                mm.then_inc(resd, 1)
                pe.wait_ge(xsc, c + 1)
                pe.wait_ge(cvc, c)
                for k in range(G):
                    for tap in range(TAPS):
                        mm = nc.tensor.matmul(ps[:, CV + k, :], convk[:, k, tap, :], xs[:, k, at(c, tap)],
                                              start=(tap == 0), stop=(tap == TAPS - 1))
                mm.then_inc(cvd, 1)
                pe.wait_ge(cvc, c + 1)
                pe.wait_ge(dtc, c)
                pe.wait_ge(bcs, c * 5)
                for k in range(G):
                    nc.tensor.matmul(ps[0:DTR, DTB, :], wxdt[:, k, :], t.uT[:, k, here], start=(k == 0), stop=(k == G - 1))
                for k in range(G):
                    mm = nc.tensor.matmul(ps[0:96, BCB, :], wxbc[:, k, :], t.uT[:, k, here], start=(k == 0), stop=(k == G - 1))
                mm.then_inc(prd, 1)
                pe.wait_ge(dtc, c + 1)
                for k in range(G):
                    mm = nc.tensor.matmul(ps[:, XS + k, :], wdt[:, k, :], dtraw[:, 0, :], start=True, stop=True)
                mm.then_inc(dpd, 1)

        @block.scalar
        def _(act):
            act.wait_ge(loaded, ALL)
            with act.Fori(0, NCH) as c:
                here = bass.ds(c * CH, CH)
                act.wait_ge(xsd, c + 1)
                nc.scalar.copy(xs[:, :, at(c)], ps[:, XS:XS + G, :]).then_inc(xsc, 1)
                act.wait_ge(resd, c + 1)
                nc.scalar.activation(t.sres[:, :, here], ps[:, RES:RES + G, :], ACT.Silu).then_inc(resc, 1)
                act.wait_ge(cvd, c + 1)
                nc.scalar.activation(t.uT[:, 0, here], ps[:, CV, :], ACT.Silu, bias=convb[:, 0:1])
                nc.scalar.activation(t.uT[:, 1, here], ps[:, CV + 1, :], ACT.Silu, bias=convb[:, 1:2]).then_inc(cvc, 1)
                act.wait_ge(prd, c + 1)
                act.wait_ge(dpd, c)
                nc.scalar.copy(dtraw[:, 0, :], ps[0:DTR, DTB, :]).then_inc(dtc, 1)
            act.wait_ge(dpc, NCH)
            nc.scalar.activation(t.delta[:], t.delta[:], ACT.Exp).then_inc(expd, 1)
            nc.scalar.activation(t.A[:], alog[:], ACT.Exp).then_inc(expd, 1)
            act.wait_ge(expd, 2)
            nc.scalar.activation(t.delta[:], t.delta[:], ACT.Ln, bias=1.0).then_inc(lnd, 1)

        @block.gpsimd
        def _(pool):
            nc.gpsimd.memset(xs[:], 0.0).then_inc(cleared, 1)

        @block.vector
        def _(dve):
            dve.wait_ge(loaded, ALL)
            with dve.Fori(0, NCH) as c:
                here = bass.ds(c * CH, CH)
                n = c * 5
                dve.wait_ge(prd, c + 1)
                nc.vector.tensor_copy(t.bc[:, here], ps[0:96, BCB, :]).then_inc(bcs, 1)
                dve.wait_ge(bcs, n + 1)
                nc.vector.tensor_tensor(rest[:, 0, :], ps[0:96, BCB, :], t.bc[:, here], ALU.subtract).then_inc(bcs, 1)
                dve.wait_ge(bcs, n + 2)
                nc.vector.tensor_copy(mid[:, 0, :], rest[:, 0, :]).then_inc(bcs, 1)
                dve.wait_ge(bcs, n + 3)
                nc.vector.tensor_copy(t.bc[32:64, here], mid[32:64, 0, :]).then_inc(bcs, 1)
                nc.vector.tensor_tensor(t.bc[64:96, here], rest[64:96, 0, :], mid[64:96, 0, :], ALU.subtract).then_inc(bcs, 1)
                dve.wait_ge(dpd, c + 1)
                nc.vector.tensor_scalar(t.delta[:, 0, here], ps[:, XS, :], bdt[:, 0:1], 0.0, ALU.add, ALU.min)
                nc.vector.tensor_scalar(t.delta[:, 1, here], ps[:, XS + 1, :], bdt[:, 1:2], 0.0, ALU.add, ALU.min).then_inc(dpc, 1)
            dve.wait_ge(lnd, 1)
            nc.vector.tensor_scalar(t.delta[:], t.delta[:], DT_MIN, DT_MAX, ALU.max, ALU.min).then_inc(clipd, 1)
            nc.vector.tensor_scalar(t.A[:], t.A[:], -1.0, None, ALU.mult).then_inc(clipd, 1)
            dve.wait_ge(clipd, 2)
            nc.vector.tensor_tensor(t.du[:], t.delta[:], t.uT[:], ALU.mult).then_inc(dud, 1)
            dve.wait_ge(dud, 1)


def state_scan(nc, g, W, t):
    s = open_scope(nc, g)
    ps = g.ps
    BB, CB, Y = 0, 2, 4
    with s.ctx:
        bsp = s.sb("b_spread", [P, 2, T])
        csp = s.sb("c_spread", [P, 2, T])
        decay = s.sb("decay", [P, 2, G, T])
        drive = s.sb("drive", [P, 2, G, T])
        state = s.sb("state", [P, G, T])
        read = s.sb("read", [P, 2, G, T])
        zero = s.sb("zero", [P, CH], BF16)
        skip = read[:, 0]
        gated = t.du
        wo = s.sb("wo", [P, G, P])
        loaded = s.sem("ss_loaded")
        zeroed = s.sem("ss_zeroed")
        spread = s.sem("ss_spread")
        copied = s.sem("ss_spread_copied")
        decayd = s.sem("ss_decay")
        drived = s.sem("ss_drive")
        scand = s.sem("ss_scan")
        readd = s.sem("ss_read")
        summed = s.sem("ss_summed")
        ycopied = s.sem("ss_y_copied")
        gatedd = s.sem("ss_gated")
        outd = s.sem("ss_out")
        outc = s.sem("ss_out_copied")
        block = s.ctx.enter_context(nc.Block())

        @block.sync
        def _(sp):
            sp.dma_start(wo[:], W["wo"]).then_inc(loaded, 16)
            sp.wait_ge(loaded, 16)

        @block.tensor
        def _(pe):
            pe.wait_ge(zeroed, 1)
            pe.wait_ge(loaded, 16)

            def spread_state(b, m):
                n = m + b * NS
                for j, bank in ((0, BB), (1, CB)):
                    pe.wait_ge(copied, n * 2 + j)
                    for half in range(2):
                        mm = nc.tensor.matmul(ps[:, bank + half, :], t.seln[:, bass.ds(m + j * NS, 1), :].rearrange("k a p -> k (a p)"),
                                              t.bc[:, b * T + half * CH:b * T + (half + 1) * CH], start=True, stop=True)
                    mm.then_inc(spread, 1)

            def sum_state(m, e):
                for k in range(G):
                    pe.wait_ge(readd, m * G + (k + 1))
                    for half in range(2):
                        mm = nc.tensor.matmul(ps[:, Y + 2 * k + half, :], g.ident[:], read[:, e, k, half * CH:(half + 1) * CH],
                                              start=False, stop=False, skip_group_check=True)
                mm.then_inc(summed, 1)

            for b in range(B):
                pe.wait_ge(ycopied, b * G)
                for k in range(2 * G):
                    nc.tensor.matmul(ps[:, Y + k, :], zero[:, 0:P], zero[:], start=True, stop=False, skip_group_check=True)
                spread_state(b, 0)
                with pe.Fori(0, NS // 2 - 1) as i:
                    for e in range(2):
                        spread_state(b, i * 2 + (e + 1))
                        sum_state(i * 2 + (b * NS + e), e)
                spread_state(b, NS - 1)
                sum_state(b * NS + NS - 2, 0)
                sum_state(b * NS + NS - 1, 1)
            for c in range(NCH):
                pe.wait_ge(gatedd, (c // 2 + 1) * G)
                if c >= 2:
                    pe.wait_ge(outc, c - 1)
                for k in range(G):
                    mm = nc.tensor.matmul(ps[:, BB + c % 2, :], wo[:, k, :], gated[:, k, c * CH:(c + 1) * CH],
                                          start=(k == 0), stop=(k == G - 1))
                mm.then_inc(outd, 1)

        @block.scalar
        def _(act):
            for b in range(B):
                with act.Fori(0, NS // 2) as i:
                    for e in range(2):
                        m = i * 2 + e
                        n = i * 2 + (b * NS + e)
                        act.wait_ge(spread, n * 2 + 1)
                        act.wait_ge(drived, i * 2 * G + (b * NS * G))
                        nc.scalar.copy(bsp[:, e, :], ps[:, BB:BB + 2, :].rearrange("p b n -> p (b n)")).then_inc(copied, 1)
                        act.wait_ge(scand, i * 2 * G + (b * NS * G))
                        for k in range(G):
                            nc.scalar.activation(decay[:, e, k, :], t.delta[:, k, b * T:(b + 1) * T], ACT.Exp,
                                                 scale=t.A[:, k, bass.ds(m, 1)]).then_inc(decayd, 1)
                        act.wait_ge(spread, n * 2 + 2)
                        act.wait_ge(readd, i * 2 * G + (b * NS * G))
                        nc.scalar.copy(csp[:, e, :], ps[:, CB:CB + 2, :].rearrange("p b n -> p (b n)")).then_inc(copied, 1)
            for c in range(NCH):
                act.wait_ge(outd, c + 1)
                nc.scalar.copy(g.branchT[:, c * CH:(c + 1) * CH], ps[:, BB + c % 2, :]).then_inc(outc, 1)
            act.wait_ge(outc, NCH)

        @block.gpsimd
        def _(pool):
            for b in range(B):
                with pool.Fori(0, NS // 2) as i:
                    for e in range(2):
                        n = i * 2 + (b * NS + e)
                        pool.wait_ge(copied, n * 2 + 1)
                        pool.wait_ge(scand, i * 2 * G + (b * NS * G))
                        for k in range(G):
                            nc.gpsimd.tensor_tensor(drive[:, e, k, :], t.du[:, k, b * T:(b + 1) * T], bsp[:, e, :],
                                                    ALU.mult).then_inc(drived, 1)

        @block.vector
        def _(dve):
            nc.vector.memset(zero[:], 0.0).then_inc(zeroed, 1)
            for b in range(B):
                with dve.Fori(0, NS // 2) as i:
                    for e in range(2):
                        n = i * 2 + (b * NS + e)
                        dve.wait_ge(summed, i * 2 + b * NS)
                        dve.wait_ge(readd, i * 2 * G + (b * NS + e) * G)
                        for k in range(G):
                            dve.wait_ge(decayd, n * G + (k + 1))
                            dve.wait_ge(drived, n * G + (k + 1))
                            nc.vector.tensor_tensor_scan(state[:, k, :], decay[:, e, k, :], drive[:, e, k, :], 0.0,
                                                         ALU.mult, ALU.add).then_inc(scand, 1)
                        for k in range(G):
                            dve.wait_ge(scand, n * G + (k + 1))
                            dve.wait_ge(copied, n * 2 + 2)
                            nc.vector.tensor_tensor(read[:, e, k, :], state[:, k, :], csp[:, e, :], ALU.mult).then_inc(readd, 1)
                dve.wait_ge(summed, (b + 1) * NS)
                here = slice(b * T, (b + 1) * T)
                for k in range(G):
                    nc.vector.scalar_tensor_tensor(skip[:, k, :], t.uT[:, k, here], t.Dskip[:, k:k + 1],
                                                   ps[:, Y + 2 * k:Y + 2 * k + 2, :].rearrange("p b n -> p (b n)"),
                                                   ALU.mult, ALU.add).then_inc(ycopied, 1)
                dve.wait_ge(ycopied, (b + 1) * G)
                for k in range(G):
                    nc.vector.tensor_tensor(gated[:, k, here], skip[:, k, :], t.sres[:, k, here], ALU.mult).then_inc(gatedd, 1)
            dve.wait_ge(gatedd, B * G)


def selective_scan(nc, g, W):
    s = open_scope(nc, g)
    t = Tensors()
    with s.ctx:
        t.sres = s.sb("sres", [P, G, NT])
        t.uT = s.sb("uT", [P, G, NT])
        t.delta = s.sb("delta", [P, G, NT])
        t.du = s.sb("du", [P, G, NT])
        t.A = s.sb("A", [P, G, NS])
        t.bc = s.sb("bc", [96, NT], BF16)
        t.seln = s.sb("seln", [96, 2 * NS, P], BF16)
        t.Dskip = s.sb("Dskip", [P, G])
        scan_inputs(nc, g, W, t)
        state_scan(nc, g, W, t)


ES, CAP, FH = 16, P, 512
FS = FH // P
DUMP = ES * CAP


def switch_route(nc, g, W, r):
    s = open_scope(nc, g)
    ps = g.ps
    with s.ctx:
        wr = s.sb("wr", [P, ES])
        iota = s.sb("iota", [P, ES])
        tri = s.sb("tri", [P, P], BF16)
        ones = s.sb("ones", [P, P], BF16)
        token = s.sb("token", [P, TILES])
        restart = s.sb("restart", [P, ES, TILES])
        logit = s.sb("logit", [P, TILES, ES])
        less = s.sb("less", [P, TILES, ES])
        ex = s.sb("ex", [P, TILES, ES])
        top8 = s.sb("top8", [P, TILES, 8])
        idx8 = s.sb("idx8", [P, TILES, 8], U32)
        idxf = s.sb("idxf", [P, TILES])
        hot = s.sb("hot", [P, TILES, ES])
        hotb = s.sb("hotb", [P, TILES, ES], BF16)
        tot = s.sb("tot", [P, ES, TILES])
        upto = s.sb("upto", [P, ES, TILES])
        place = s.sb("place", [P, TILES, ES])
        loc = s.sb("loc", [P, TILES])
        valid = s.sb("valid", [P, TILES])
        total = s.sb("total", [P, TILES])
        row = s.sb("row", [P, 4, TILES])
        loaded = s.sem("sr_loaded")
        product = s.sem("sr_logits")
        expd = s.sem("sr_exp")
        hotd = s.sem("sr_hot")
        counted = s.sem("sr_counted")
        ve = s.sem("sr_vector_done")
        block = s.ctx.enter_context(nc.Block())
        tiles = dict(wr=wr, iota=iota, tri=tri, ones=ones, token=token, restart=restart)
        ALL = 16 * len(tiles)

        @block.sync
        def _(sp):
            for n, d in tiles.items():
                sp.dma_start(d[:], W[n]).then_inc(loaded, 16)
            sp.wait_ge(loaded, ALL)

        @block.tensor
        def _(pe):
            pe.wait_ge(loaded, ALL)
            for i in range(TILES):
                mm = nc.tensor.matmul(ps[:, 0, i * ES:(i + 1) * ES], g.xnT[:, i * P:(i + 1) * P], wr[:], start=True, stop=True)
            mm.then_inc(product, 1)
            pe.wait_ge(hotd, 1)
            flat = hotb[:].rearrange("p i e -> p (i e)")
            nc.tensor.matmul(ps[:, 1, 0:TILES * ES], tri[:], flat, start=True, stop=True)
            nc.tensor.matmul(ps[:, 2, 0:TILES * ES], ones[:], flat, start=True, stop=True).then_inc(counted, 1)

        @block.scalar
        def _(act):
            act.wait_ge(expd, 1)
            nc.scalar.activation(ex[:], less[:], ACT.Exp).then_inc(expd, 1)
            act.wait_ge(expd, 2)

        @block.vector
        def _(dve):
            done = Count(ve)

            def then(instruction):
                done.inc(instruction)
                done.wait(dve)
            wide = lambda a: a[:, :, None].to_broadcast([P, TILES, ES])
            dve.wait_ge(loaded, ALL)
            dve.wait_ge(product, 1)
            then(nc.vector.tensor_copy(logit[:], ps[:, 0, 0:TILES * ES].rearrange("p (i e) -> p i e", e=ES)))
            for i in range(TILES):
                done.inc(nc.vector.max(top8[:, i, :], logit[:, i, :]))
            done.wait(dve)
            nc.vector.tensor_tensor(less[:], logit[:], top8[:, :, 0:1].to_broadcast([P, TILES, ES]), ALU.subtract).then_inc(expd, 1)
            for i in range(TILES):
                done.inc(nc.vector.max_index(idx8[:, i, :], top8[:, i, :], logit[:, i, :]))
            done.wait(dve)
            then(nc.vector.tensor_copy(idxf[:], idx8[:, :, 0]))
            then(nc.vector.tensor_tensor(hot[:], iota[:, None, :].to_broadcast([P, TILES, ES]), wide(idxf), ALU.is_equal))
            nc.vector.tensor_copy(hotb[:], hot[:]).then_inc(hotd, 1)
            dve.wait_ge(expd, 2)
            then(nc.vector.tensor_reduce(total[:], ex[:], AX.X, ALU.add))
            then(nc.vector.reciprocal(total[:], total[:]))
            dve.wait_ge(counted, 1)
            then(nc.vector.tensor_copy(tot[:], ps[:, 2, 0:TILES * ES].rearrange("p (i e) -> p e i", e=ES)))
            then(nc.vector.tensor_tensor_scan(upto[:].rearrange("p e i -> p (e i)"), restart[:].rearrange("p e i -> p (e i)"),
                                              tot[:].rearrange("p e i -> p (e i)"), 0.0, ALU.mult, ALU.add))
            then(nc.vector.tensor_tensor(upto[:], upto[:], tot[:], ALU.subtract))
            then(nc.vector.tensor_tensor(place[:], ps[:, 1, 0:TILES * ES].rearrange("p (i e) -> p i e", e=ES),
                                         upto[:].rearrange("p e i -> p i e"), ALU.add))
            then(nc.vector.tensor_tensor(place[:], place[:], hot[:], ALU.mult))
            then(nc.vector.tensor_reduce(loc[:], place[:], AX.X, ALU.add))
            then(nc.vector.tensor_scalar(valid[:], loc[:], CAP + 0.5, None, ALU.is_lt))
            then(nc.vector.tensor_tensor(r.factor[:], total[:], valid[:], ALU.mult))
            then(nc.vector.tensor_scalar(loc[:], loc[:], float(CAP), -1.0, ALU.min, ALU.add))
            then(nc.vector.scalar_tensor_tensor(row[:, 0], idxf[:], float(CAP), loc[:], ALU.mult, ALU.add))
            then(nc.vector.tensor_tensor(row[:, 1], row[:, 0], token[:], ALU.subtract))
            then(nc.vector.tensor_tensor(row[:, 2], row[:, 1], valid[:], ALU.mult))
            then(nc.vector.tensor_tensor(row[:, 3], row[:, 2], token[:], ALU.add))
            then(nc.vector.tensor_copy(r.gather[:], row[:, 0]))
            then(nc.vector.tensor_copy(r.scatter[:], row[:, 3]))


def switch_experts(nc, g, W, dispatch, expert_out):
    s = open_scope(nc, g)
    ps = g.ps
    r = Tensors()
    HB, OB, TB = 0, 2, 4
    with s.ctx:
        r.factor = s.sb("factor", [P, TILES])
        r.gather = s.sb("gather", [P, TILES], U32)
        r.scatter = s.sb("scatter", [P, TILES], U32)
        switch_route(nc, g, W, r)
        zero = s.sb("zero", [P, ES, D])
        rows = s.sb("rows", [P, ES, D])
        rowsT = s.sb("rowsT", [P, ES * CAP])
        w1 = s.sb("w1", [P, 2, FH])
        w2 = s.sb("w2", [P, 2, FS, D])
        hid = s.sb("hid", [P, 2, FS, CAP])
        eo = s.sb("eo", [P, 2, D])
        back = s.sb("back", [P, TILES, D])
        zeroed = s.sem("se_zeroed")
        cleared = s.sem("se_table_cleared")
        sent = s.sem("se_sent")
        rowsl = s.sem("se_rows_loaded")
        turned = s.sem("se_turned")
        tcopied = s.sem("se_turned_copied")
        wl = [s.sem(f"se_weights_loaded{e}") for e in range(2)]
        hd, hc = s.sem("se_hidden"), s.sem("se_hidden_relu")
        od, oc = s.sem("se_out"), s.sem("se_out_copied")
        os_ = [s.sem(f"se_out_stored{e}") for e in range(2)]
        got = s.sem("se_got")
        addd = s.sem("se_added")
        block = s.ctx.enter_context(nc.Block())

        @block.sync
        def _(sp):
            sp.wait_ge(zeroed, 1)
            sp.dma_start(dispatch[0:DUMP, :].rearrange("(e p) d -> p e d", p=P), zero[:]).then_inc(cleared, 16)
            for e in range(2):
                sp.dma_start(w1[:, e, :], W["w1"][e]).then_inc(wl[e], 16)
                sp.dma_start(w2[:, e], W["w2"][e]).then_inc(wl[e], 16)
            sp.wait_ge(sent, 16 * TILES)
            sp.dma_start(rows[:], dispatch[0:DUMP, :].rearrange("(e p) d -> p e d", p=P)).then_inc(rowsl, 16)
            with sp.Fori(0, ES // 2 - 1) as i:
                for e in range(2):
                    sp.wait_ge(od, i * 2 + (e + 1))
                    nxt = bass.ds(i * 2 + (e + 2), 1)
                    sp.dma_start(w1[:, e, :], W["w1"][nxt].rearrange("a p f -> p (a f)")).then_inc(wl[e], 16)
                    sp.dma_start(w2[:, e], W["w2"][nxt].rearrange("a p f m -> p (a f) m")).then_inc(wl[e], 16)
                    sp.wait_ge(oc, i * 2 + (e + 1))
                    sp.dma_start(expert_out[bass.ds((i * 2 + e) * CAP, CAP), :], eo[:, e, :]).then_inc(os_[e], 16)
            for e in range(2):
                sp.wait_ge(oc, ES - 1 + e)
                sp.dma_start(expert_out[(ES - 2 + e) * CAP:(ES - 1 + e) * CAP, :], eo[:, e, :]).then_inc(os_[e], 16)
            for e in range(2):
                sp.wait_ge(os_[e], 16 * ES // 2)
                sp.wait_ge(wl[e], 32 * ES // 2)

        @block.gpsimd
        def _(pool):
            pool.wait_ge(cleared, 16)
            for i in range(TILES):
                nc.gpsimd.indirect_dma_start(dispatch, bass.IndirectOffsetOnAxis(ap=r.scatter[:, i:i + 1], axis=0),
                                             g.xn[:, i, :], None).then_inc(sent, 16)
            for e in range(2):
                pool.wait_ge(os_[e], 16 * ES // 2)
            for i in range(TILES):
                nc.gpsimd.indirect_dma_start(back[:, i, :], None, expert_out,
                                             bass.IndirectOffsetOnAxis(ap=r.gather[:, i:i + 1], axis=0)).then_inc(got, 16)
            pool.wait_ge(sent, 16 * TILES)
            pool.wait_ge(got, 16 * TILES)

        @block.tensor
        def _(pe):
            pe.wait_ge(rowsl, 16)
            for q in range(4):
                for k in range(4):
                    mm = nc.tensor.transpose(ps[:, TB + q, k * P:(k + 1) * P], rows[:, 4 * q + k, :], g.ident[:])
                mm.then_inc(turned, 1)
            pe.wait_ge(tcopied, 4)
            with pe.Fori(0, ES // 2) as i:
                for e in range(2):
                    pe.wait_ge(wl[e], i * 32 + 32)
                    pe.wait_ge(hc, i * 2)
                    for f in range(FS):
                        mm = nc.tensor.matmul(ps[:, HB + e, f * CAP:(f + 1) * CAP], w1[:, e, f * P:(f + 1) * P],
                                              rowsT[:, bass.ds((i * 2 + e) * CAP, CAP)], start=True, stop=True)
                    mm.then_inc(hd, 1)
                for e in range(2):
                    pe.wait_ge(hc, i * 2 + (e + 1))
                    pe.wait_ge(oc, i * 2)
                    for f in range(FS):
                        mm = nc.tensor.matmul(ps[:, OB + e, 0:D], hid[:, e, f, :], w2[:, e, f, :], start=(f == 0), stop=(f == FS - 1))
                    mm.then_inc(od, 1)

        @block.scalar
        def _(act):
            with act.Fori(0, ES // 2) as i:
                for e in range(2):
                    act.wait_ge(hd, i * 2 + (e + 1))
                    act.wait_ge(od, i * 2)
                    nc.scalar.activation(hid[:, e].rearrange("p f n -> p (f n)"), ps[:, HB + e, :], ACT.Relu).then_inc(hc, 1)

        @block.vector
        def _(dve):
            nc.vector.memset(zero[:], 0.0).then_inc(zeroed, 1)
            for q in range(4):
                dve.wait_ge(turned, q + 1)
                nc.vector.tensor_copy(rowsT[:, q * CH:(q + 1) * CH], ps[:, TB + q, :]).then_inc(tcopied, 1)
            with dve.Fori(0, ES // 2) as i:
                for e in range(2):
                    dve.wait_ge(od, i * 2 + (e + 1))
                    dve.wait_ge(os_[e], i * 16)
                    nc.vector.tensor_copy(eo[:, e, :], ps[:, OB + e, 0:D]).then_inc(oc, 1)
            dve.wait_ge(got, 16 * TILES)
            for i in range(TILES):
                nc.vector.scalar_tensor_tensor(g.x[:, i, :], back[:, i, :], r.factor[:, i:i + 1], g.x[:, i, :],
                                               ALU.mult, ALU.add).then_inc(addd, 1)
            dve.wait_ge(addd, TILES)


PAIRS = 8
HEAD3 = 64
NEAR = 2


def near_tiles(qt):
    return range(max(0, qt - NEAR), min(KT - 1, qt + NEAR) + 1)


def dilated_attention(nc, g, W):
    s = open_scope(nc, g)
    ps = g.ps
    TB, OB = 4, 6
    WIDE = (2 * NEAR + 1) * P
    UN = 2 * KT
    with s.ctx:
        w = s.sb("w3", [P, 3, P])
        wo = s.sb("wo3", [P, PAIRS, P])
        mask = s.sb("mask3", [P, WIDE])
        Q = [[s.sb(f"Q3_{b}{h}", [P, T]) for h in range(2)] for b in range(B)]
        K = [s.sb(f"K3_{b}", [P, T]) for b in range(B)]
        V = [s.sb(f"V3_{b}", [P, KT, P]) for b in range(B)]
        masked = [s.sb(f"masked{h}", [P, WIDE]) for h in range(2)]
        probs = [[s.sb(f"probs3_{k}{h}", [P, WIDE]) for h in range(2)] for k in range(2)]
        probsT = [[s.sb(f"probsT3_{k}{h}", [P, WIDE]) for h in range(2)] for k in range(2)]
        mx = s.sb("mx3", [P, UN])
        negmax = s.sb("negmax3", [P, UN])
        total = s.sb("total3", [P, UN])
        inv = s.sb("inv3", [P, UN])
        outT = s.sb("outT3", [P, PAIRS, NT])
        const = s.sem("da_const")
        wloaded = s.sem("da_weights")
        cleared = s.sem("da_cleared")
        projected = s.sem("da_projected")
        copied = s.sem("da_copied")
        sc = s.sem("da_scores")
        mxd = s.sem("da_max")
        maxd = s.sem("da_masked")
        ex = s.sem("da_exp")
        invd = s.sem("da_inverse")
        divd = s.sem("da_divided")
        tr = s.sem("da_turned")
        ev_dve = s.sem("da_turned_copied_dve")
        ev_act = s.sem("da_turned_copied_act")
        av = s.sem("da_weighed")
        oc = s.sem("da_out_copied")
        oproj = s.sem("da_out_projected")
        ocopy = s.sem("da_out_stored")
        block = s.ctx.enter_context(nc.Block())

        def at_least(engine, sem, value):
            if not isinstance(value, int) or value > 0:
                engine.wait_ge(sem, value)

        def before(n, b, i, k):
            if i >= k:
                return n, b, i - k
            return None if isinstance(n, int) and n == 0 else (n - 1, 1 - b, i - k + KT)

        PROJ = [("q", 0), ("q", 1), ("k", 0), ("k", 1), ("v", 0), ("v", 1)]

        def proj_bank(i):
            return OB if i < 2 else OB + 1

        @block.sync
        def _(sp):
            sp.dma_start(w[:], W["wqkv"][0]).then_inc(wloaded, 16)
            sp.dma_start(mask[:], W["mask"]).then_inc(const, 16)
            sp.dma_start(wo[:], W["wo"]).then_inc(const, 16)
            with sp.Fori(0, PAIRS - 1) as hp:
                sp.wait_ge(projected, hp * 12 + 12)
                sp.dma_start(w[:], W["wqkv"][bass.ds(hp + 1, 1)].rearrange("a p s n -> (a p) s n")).then_inc(wloaded, 16)
            sp.wait_ge(wloaded, 16 * PAIRS)
            sp.wait_ge(const, 32)

        @block.tensor
        def _(pe):
            def project(n, b, j, bank):
                which, c = PROJ[j]
                if j == 0:
                    pe.wait_ge(wloaded, (n // B) * 16 + 16)
                if which != "v":
                    a = b * T + c * CH
                    mm = nc.tensor.matmul(ps[:, bank, :], w[:, "qk".index(which), :], g.xnT[:, a:a + CH], start=True, stop=True)
                else:
                    for k in range(4):
                        a = b * T + (4 * c + k) * P
                        mm = nc.tensor.matmul(ps[:, bank, k * P:(k + 1) * P], g.xnT[:, a:a + P], w[:, 2, :], start=True, stop=True)
                mm.then_inc(projected, 1)

            def scores(n, b, qt, h):
                u = 2 * qt + h
                if qt == 0:
                    pe.wait_ge(copied, n * 6 + 6)
                at_least(pe, maxd, n * UN + (u - 1))
                kts = near_tiles(qt)
                for a in range(0, len(kts), 4):
                    k0, k1 = kts[a], kts[min(a + 4, len(kts)) - 1] + 1
                    mm = nc.tensor.matmul(ps[:, 2 * h + a // 4, 0:(k1 - k0) * P], Q[b][h][:, qt * P:(qt + 1) * P],
                                          K[b][:, k0 * P:k1 * P], start=True, stop=True)
                mm.then_inc(sc, 1)

            def turn(n, b, qt, h):
                u = 2 * qt + h
                pe.wait_ge(divd, n * UN + (u + 1))
                at_least(pe, ev_dve, n * UN + u)
                at_least(pe, ev_act, n * UN + u)
                m = len(near_tiles(qt))
                for k in range(m):
                    bank, at = (TB, k) if k < (m + 1) // 2 else (TB + 1, k - (m + 1) // 2)
                    mm = nc.tensor.transpose(ps[:, bank, at * P:(at + 1) * P], probs[qt % 2][h][:, k * P:(k + 1) * P], g.ident[:])
                mm.then_inc(tr, 1)

            def weigh(n, b, qt, more=True):
                pe.wait_ge(ev_dve, n * UN + (2 * qt + 2))
                pe.wait_ge(ev_act, n * UN + (2 * qt + 2))
                if qt % 4 == 0:
                    if more:
                        pe.wait_ge(copied, (n + 1) * 6 + (2 if qt == 0 else 6))
                    at_least(pe, oc, n * 2)
                kts = near_tiles(qt)
                for k, kt in enumerate(kts):
                    for h in range(2):
                        mm = nc.tensor.matmul(ps[HEAD3 * h:HEAD3 * (h + 1), OB + qt // 4, qt % 4 * P:(qt % 4 + 1) * P],
                                              V[b][:, kt, HEAD3 * h:HEAD3 * (h + 1)], probsT[qt % 2][h][:, k * P:(k + 1) * P],
                                              start=(k == 0), stop=(k == len(kts) - 1))
                mm.then_inc(av, 1)

            def slot(n, b, i, more):
                last, older = before(n, b, i, 1), before(n, b, i, 2)
                scores(n, b, i, 0)
                if last:
                    turn(*last, 0)
                scores(n, b, i, 1)
                if older:
                    weigh(*older, more)
                if more and i < len(PROJ):
                    if i == 0:
                        at_least(pe, oc, n * 2 - 1)
                    elif i == 2:
                        at_least(pe, oc, n * 2)
                    else:
                        pe.wait_ge(copied, (n + 1) * 6 + i)
                    project(n + 1, 1 - b, i, proj_bank(i))
                if last:
                    turn(*last, 1)

            for j in range(len(PROJ)):
                project(0, 0, j, j)
            for i in range(2):
                slot(0, 0, i, True)
            with pe.Fori(0, PAIRS - 1) as hp:
                for i in range(2, B * KT + 2):
                    slot(hp * B + i // KT, i // KT % B, i % KT, True)
            for i in range(2, B * KT):
                slot((PAIRS - 1) * B + i // KT, i // KT, i % KT, i < KT)
            end = B * PAIRS - 1
            turn(end, 1, KT - 1, 0)
            weigh(end, 1, KT - 2)
            turn(end, 1, KT - 1, 1)
            weigh(end, 1, KT - 1)
            pe.wait_ge(oc, 2 * B * PAIRS)
            pe.wait_ge(const, 32)
            for c in range(NCH):
                for q in range(PAIRS):
                    mm = nc.tensor.matmul(ps[:, c, :], wo[:, q, :], outT[:, q, c * CH:(c + 1) * CH],
                                          start=(q == 0), stop=(q == PAIRS - 1))
                mm.then_inc(oproj, 1)

        @block.scalar
        def _(act):
            def copy_projected(n, b, j, bank):
                which, c = PROJ[j]
                act.wait_ge(projected, n * 6 + (j + 1))
                act.wait_ge(copied, n * 6 + j)
                if which == "q":
                    rows = slice(0, HEAD3)
                    nc.scalar.activation(Q[b][0][rows, c * CH:(c + 1) * CH], ps[rows, bank, :], ACT.Copy, scale=HEAD3 ** -0.5)
                    rows = slice(HEAD3, 2 * HEAD3)
                    nc.scalar.activation(Q[b][1][rows, c * CH:(c + 1) * CH], ps[rows, bank, :], ACT.Copy,
                                         scale=HEAD3 ** -0.5).then_inc(copied, 1)
                elif which == "v":
                    nc.scalar.copy(V[b][:, 4 * c:4 * c + 4, :], ps[:, bank, :].rearrange("p (k d) -> p k d", d=P)).then_inc(copied, 1)

            def exp(n, b, qt, h):
                u = 2 * qt + h
                m = len(near_tiles(qt)) * P
                act.wait_ge(mxd, n * UN + (u + 1))
                at_least(act, tr, n * UN + (u - 3))
                nc.scalar.activation(probs[qt % 2][h][:, 0:m], masked[h][:, 0:m], ACT.Exp, bias=negmax[:, u:u + 1],
                                     accum_out=total[:, u:u + 1]).then_inc(ex, 1)

            def copy_turned(n, b, qt, h):
                m = len(near_tiles(qt))
                first = (m + 1) // 2
                act.wait_ge(tr, n * UN + (2 * qt + h + 1))
                at_least(act, av, n * KT + (qt - 1))
                nc.scalar.copy(probsT[qt % 2][h][:, first * P:m * P], ps[:, TB + 1, 0:(m - first) * P]).then_inc(ev_act, 1)

            def copy_out(n, b, half):
                act.wait_ge(av, n * KT + 4 * (half + 1))
                dst = outT[:, bass.ds(n // B, 1), b * T + half * CH:b * T + (half + 1) * CH].rearrange("p a n -> p (a n)")
                nc.scalar.copy(dst, ps[:, OB + half, :]).then_inc(oc, 1)

            def slot(n, b, i, more):
                last = before(n, b, i, 1)
                exp(n, b, i, 0)
                if last:
                    copy_turned(*last, 0)
                exp(n, b, i, 1)
                if i == 5:
                    copy_out(n, b, 0)
                elif i == 1 and before(n, b, i, 2):
                    copy_out(n - 1, 1 - b, 1)
                if more and i < len(PROJ) and PROJ[i][0] != "k":
                    copy_projected(n + 1, 1 - b, i, proj_bank(i))
                if last:
                    copy_turned(*last, 1)

            act.wait_ge(cleared, 2 * B)
            for j in range(len(PROJ)):
                if PROJ[j][0] != "k":
                    copy_projected(0, 0, j, j)
            for i in range(2):
                slot(0, 0, i, True)
            with act.Fori(0, PAIRS - 1) as hp:
                for i in range(2, B * KT + 2):
                    slot(hp * B + i // KT, i // KT % B, i % KT, True)
            for i in range(2, B * KT):
                slot((PAIRS - 1) * B + i // KT, i // KT, i % KT, i < KT)
            end = B * PAIRS - 1
            copy_turned(end, 1, KT - 1, 0)
            copy_turned(end, 1, KT - 1, 1)
            copy_out(end, 1, 1)
            for c in range(1, NCH, 2):
                act.wait_ge(oproj, c + 1)
                nc.scalar.copy(g.branchT[:, c * CH:(c + 1) * CH], ps[:, c, :]).then_inc(ocopy, 1)
            act.wait_ge(ocopy, NCH)

        @block.gpsimd
        def _(pool):
            for b in range(B):
                for h in range(2):
                    nc.gpsimd.memset(Q[b][h][:], 0.0).then_inc(cleared, 1)

        @block.vector
        def _(dve):
            def copy_k(n, b, j, bank):
                c = PROJ[j][1]
                dve.wait_ge(projected, n * 6 + (j + 1))
                dve.wait_ge(copied, n * 6 + j)
                nc.vector.tensor_copy(K[b][:, c * CH:(c + 1) * CH], ps[:, bank, :]).then_inc(copied, 1)

            def largest(n, b, qt, h):
                u = 2 * qt + h
                kts = near_tiles(qt)
                m = len(kts) * P
                a = (kts[0] - qt + NEAR) * P
                nc.vector.tensor_tensor_reduce(masked[h][:, 0:m], ps[:, 2 * h:2 * h + 2, :].rearrange("p c n -> p (c n)")[:, 0:m],
                                               mask[:, a:a + m], 1.0, -3.0e38, ALU.add, ALU.max,
                                               accum_out=mx[:, u:u + 1]).then_inc(maxd, 1)
                dve.wait_ge(maxd, n * UN + (u + 1))
                nc.vector.tensor_scalar(negmax[:, u:u + 1], mx[:, u:u + 1], -1.0, None, ALU.mult).then_inc(mxd, 1)

            def inverse(n, b, qt, h):
                u = 2 * qt + h
                dve.wait_ge(ex, n * UN + (u + 1))
                at_least(dve, divd, n * UN + u)
                nc.vector.reciprocal(inv[:, u:u + 1], total[:, u:u + 1]).then_inc(invd, 1)

            def divide(n, b, qt, h):
                u = 2 * qt + h
                m = len(near_tiles(qt)) * P
                p = probs[qt % 2][h]
                dve.wait_ge(invd, n * UN + (u + 1))
                nc.vector.tensor_scalar(p[:, 0:m], p[:, 0:m], inv[:, u:u + 1], None, ALU.mult).then_inc(divd, 1)

            def copy_turned(n, b, qt, h):
                m = (len(near_tiles(qt)) + 1) // 2 * P
                dve.wait_ge(tr, n * UN + (2 * qt + h + 1))
                at_least(dve, av, n * KT + (qt - 1))
                nc.vector.tensor_copy(probsT[qt % 2][h][:, 0:m], ps[:, TB, 0:m]).then_inc(ev_dve, 1)

            def slot(n, b, i, more):
                last = before(n, b, i, 1)
                dve.wait_ge(sc, n * UN + (2 * i + 1))
                if last:
                    inverse(*last, 1)
                largest(n, b, i, 0)
                if last:
                    divide(*last, 1)
                    copy_turned(*last, 0)
                dve.wait_ge(sc, n * UN + (2 * i + 2))
                inverse(n, b, i, 0)
                largest(n, b, i, 1)
                divide(n, b, i, 0)
                if more and i < len(PROJ) and PROJ[i][0] == "k":
                    copy_k(n + 1, 1 - b, i, proj_bank(i))
                if last:
                    copy_turned(*last, 1)

            dve.wait_ge(const, 32)
            for j in range(len(PROJ)):
                if PROJ[j][0] == "k":
                    copy_k(0, 0, j, j)
            for i in range(2):
                slot(0, 0, i, True)
            with dve.Fori(0, PAIRS - 1) as hp:
                for i in range(2, B * KT + 2):
                    slot(hp * B + i // KT, i // KT % B, i % KT, True)
            for i in range(2, B * KT):
                slot((PAIRS - 1) * B + i // KT, i // KT, i % KT, i < KT)
            end = B * PAIRS - 1
            inverse(end, 1, KT - 1, 1)
            divide(end, 1, KT - 1, 1)
            copy_turned(end, 1, KT - 1, 0)
            copy_turned(end, 1, KT - 1, 1)
            for c in range(0, NCH, 2):
                dve.wait_ge(oproj, c + 1)
                nc.vector.tensor_copy(g.branchT[:, c * CH:(c + 1) * CH], ps[:, c, :]).then_inc(ocopy, 1)


def program(nc, A, out, scratch, layers=(0, 1, 2, 3), parts=("attn", "ffn")):
    g = open_scope(nc)
    with g.ctx:
        g.x = g.sb("x", [P, TILES, D])
        g.xn = g.sb("xn", [P, TILES, D])
        g.xnT = g.sb("xnT", [P, NT])
        g.branchT = g.sb("branchT", [P, NT])
        g.ident = g.sb("ident", [P, P])
        g.identb = g.sb("identb", [P, P], BF16)
        g.ps = g.ctx.enter_context(nc.psum_tensor("ps", [P, 8, CH], F32))
        setup(nc, g, A)
        for n, layer in enumerate(layers):
            if n == 2:
                clear_semaphores(nc, g.used)
            residual_norm(nc, g, first=(n == 0), last=False)
            LAYERS[layer](nc, g, A, scratch, parts)
        residual_norm(nc, g, first=False, last=True)
        finish(nc, g, out)


def weights(A, layer):
    return {k[3:]: v for k, v in A.items() if k.startswith(f"L{layer}_")}


def layer0(nc, g, A, scratch, parts):
    W = weights(A, 0)
    gated_experts(nc, g, W, experts=8, hidden=344, top=2, kind="softmax", beside=head_mixing)


def clear_branch(nc, g):
    with ExitStack() as ctx:
        done = ctx.enter_context(nc.semaphore("branch_cleared"))
        block = ctx.enter_context(nc.Block())

        @block.vector
        def _(dve):
            nc.vector.memset(g.branchT[:], 0.0).then_inc(done, 1)
            dve.wait_ge(done, 1)


def layer1(nc, g, A, scratch, parts):
    W = weights(A, 1)
    if "attn" in parts:
        selective_scan(nc, g, W)
    else:
        clear_branch(nc, g)
    if "ffn" in parts:
        switch_experts(nc, g, W, scratch["dispatch"], scratch["expert_out"])


def layer2(nc, g, A, scratch, parts):
    W = weights(A, 2)
    if "attn" in parts:
        s = open_scope(nc, g)
        with s.ctx:
            Vp = s.sb("Vp", [P, TILES, P])
            split_qk(nc, g, scratch["qk"], W, float(HD) ** -0.5)
            value_tiles(nc, g, Vp, W)
            column_softmax_attention(nc, g, scratch["qk"], Vp, W)
    if "ffn" in parts:
        gated_experts(nc, g, W, experts=32, hidden=96, top=4, kind="sigmoid", add="attn" in parts)


def layer3(nc, g, A, scratch, parts):
    W = weights(A, 3)
    if "attn" in parts:
        dilated_attention(nc, g, W)
    if "ffn" in parts:
        gated_experts(nc, g, W, experts=32, hidden=32, top=4, kind="keys", gated=False, add="attn" in parts, add_xn=True)


LAYERS = {0: layer0, 1: layer1, 2: layer2, 3: layer3}


def _layouts(i):
    f, bf = np.float32, np.dtype("bfloat16")
    A = {"x": i["L0_attn_x"].reshape(NT, D), "ident": np.eye(P, dtype=f)}

    def wide_rows(w):
        out = np.zeros((P, 4, P), f)
        for h in range(HEADS):
            out[32 * (h % 4):32 * (h % 4) + 8, h // 4, :] = w[8 * h:8 * h + 8, :]
        return out

    swap = np.array([8 * h + (j + 4) % 8 for h in range(HEADS) for j in range(8)])
    kcols = np.array([16 * h + j for h in range(HEADS) for j in range(8)])
    inv = (1.0 / 10000.0 ** (np.arange(0, 8, 2, dtype=f) / f(8))).astype(f)
    freqs = np.arange(T, dtype=f)[:, None] * inv[None, :]
    rows = lambda a: a.astype(f).reshape(T // P, P, 8).transpose(1, 0, 2)
    A["L0_cos"] = rows(np.concatenate([np.cos(freqs), np.cos(freqs)], 1))
    A["L0_sin"] = rows(np.concatenate([-np.sin(freqs), np.sin(freqs)], 1))
    Wq, bq, Wup, bup = i["L0_attn_Wq"], i["L0_attn_bq"], i["L0_attn_Wup"], i["L0_attn_bup"]
    A["L0_wq"] = np.stack([Wq, Wq[:, swap]], 1)
    A["L0_wup"] = np.stack([Wup[:, kcols], Wup[:, kcols[swap]], Wup[:, kcols + 8]], 1)
    A["L0_bias"] = np.broadcast_to(np.stack([bq, bq[swap], bup[kcols], bup[kcols[swap]], bup[kcols + 8]]), (P, 5, P))
    A["L0_wdown"], A["L0_bdown"] = i["L0_attn_Wdown"], i["L0_attn_bdown"][:, None]
    A["L0_wout"] = i["L0_attn_Wout"]
    A["L0_bout"] = i["L0_attn_bout"][:, None]

    half = lambda v: v.reshape(G, P).T
    wx = i["L1_attn_W_x"].reshape(G, P, DTR + 2 * NS).transpose(1, 0, 2)
    A["L1_win"] = i["L1_attn_W_in"].reshape(D, 4, P)
    A["L1_convk"] = i["L1_attn_conv_k"].reshape(TAPS, P, G, P).transpose(1, 2, 0, 3)
    A["L1_convb"] = half(i["L1_attn_conv_b"])
    A["L1_wxdt"] = wx[:, :, 0:DTR]
    A["L1_wxbc"] = np.concatenate([wx[:, :, DTR:]] * 3, 2)
    A["L1_wdt"] = i["L1_attn_W_dt"].reshape(DTR, G, P)
    A["L1_bdt"] = half(i["L1_attn_b_dt"])
    A["L1_alog"] = i["L1_attn_A_log"].reshape(G, P, NS).transpose(1, 0, 2)
    A["L1_D"] = half(i["L1_attn_D"])
    A["L1_wo"] = i["L1_attn_W_out"].reshape(G, P, D).transpose(1, 0, 2)
    A["L1_seln"] = np.broadcast_to(np.concatenate([np.eye(2 * NS)] * 3)[:, :, None], (96, 2 * NS, P)).astype(bf)
    A["L1_wr"] = i["L1_ffn_Wg"]
    A["L1_iota"] = np.broadcast_to(np.arange(ES, dtype=f), (P, ES))
    A["L1_tri"] = (np.arange(P)[:, None] <= np.arange(P)[None, :]).astype(bf)
    A["L1_ones"] = np.ones((P, P), bf)
    A["L1_token"] = (DUMP + np.arange(NT)).reshape(TILES, P).T.astype(f)
    A["L1_restart"] = np.broadcast_to((np.arange(TILES) > 0).astype(f), (P, ES, TILES))
    A["L1_w1"] = i["L1_ffn_w1"]
    A["L1_w2"] = i["L1_ffn_w2"].reshape(ES, FS, P, D).transpose(0, 2, 1, 3)
    wqkv, bqkv = i["L2_attn_W_qkv"], i["L2_attn_b_qkv"]
    A["L2_wqk"] = wqkv[:, 0:2 * P].reshape(D, 2, P)
    A["L2_bqk"] = bqkv[0:2 * P].reshape(2, P).T
    A["L2_wv"] = wqkv[:, 2 * P:]
    A["L2_bv"] = np.broadcast_to(bqkv[2 * P:], (P, P))
    A["L2_mask"] = np.where(np.arange(P)[None, :] < np.arange(P)[:, None], f(-1e30), f(0)).astype(f)
    A["L2_wout"] = wide_rows(i["L2_attn_W_proj"])
    A["L2_bout"] = i["L2_attn_b_proj"][:, None]

    pairs = lambda w: w.reshape(D, PAIRS, 2 * HEAD3).transpose(1, 0, 2)
    A["L3_wqkv"] = np.stack([pairs(i[f"L3_attn_w_{n}"]) for n in "qkv"], 2)
    A["L3_wo"] = i["L3_attn_w_o"].reshape(PAIRS, 2 * HEAD3, D).transpose(1, 0, 2)
    query, key = np.arange(P)[:, None], np.arange((2 * NEAR + 1) * P)[None, :] - NEAR * P
    gap = np.abs(key - query)
    seen = (key // 64 == query // 64) | ((gap > 0) & (gap % 4 == 0) & (gap <= 256))
    A["L3_mask"] = np.where(seen, f(0), f(-1e30)).astype(f)

    def experts(layer, up, gate, down, n, hidden):
        ft = -(-n * hidden // P)
        pad = ft * P - n * hidden

        def cols(w):
            w = np.pad(w.transpose(1, 0, 2).reshape(D, n * hidden), ((0, 0), (0, pad)))
            return w.reshape(D, ft, P)
        A[f"L{layer}_wg"] = cols(gate)
        if up is not None:
            A[f"L{layer}_wu"] = cols(up)
        w = np.pad(down.reshape(n * hidden, D), ((0, pad), (0, 0)))
        A[f"L{layer}_wd"] = w.reshape(ft, P, D).transpose(1, 0, 2)
        owner = np.arange(ft * P) // hidden
        one = (owner[None, :] == np.arange(n)[:, None]).astype(bf)
        A[f"L{layer}_sel"] = np.concatenate([one] * 3 + [np.zeros((P - 3 * n, ft * P), bf)]).reshape(P, ft, P)
        A[f"L{layer}_iota"] = np.broadcast_to(np.arange(n, dtype=f), (P, n))

    experts(0, i["L0_ffn_Wu"], i["L0_ffn_Wg"], i["L0_ffn_Wd"], 8, 344)
    A["L0_wr"] = i["L0_ffn_Ws"]
    A["L0_br"] = np.broadcast_to(i["L0_ffn_bs"], (P, 8))
    experts(2, i["L2_ffn_w3"], i["L2_ffn_w1"], i["L2_ffn_w2"], 32, 96)
    A["L2_wr"] = i["L2_ffn_gate_w"].T
    A["L2_br"] = np.broadcast_to(i["L2_ffn_e_bias"], (P, 32))
    experts(3, None, i["L3_ffn_values_down"], i["L3_ffn_values_up"], 32, 32)
    A["L3_wh"] = i["L3_ffn_hasher_w"].T
    A["L3_wkeys"] = i["L3_ffn_keys"].T
    A["L3_scale"] = np.broadcast_to(i["L3_ffn_scale"], (P, 1))
    return {k: np.ascontiguousarray(v) for k, v in A.items()}


def _make(nc, A, out_shape, **options):
    aps = {k: nc.dram_tensor("in_" + k, v.shape, mybir.dt.from_np(v.dtype), kind="ExternalInput").ap() for k, v in A.items()}
    out = nc.dram_tensor("out_x", out_shape, F32, kind="ExternalOutput").ap()
    scratch = {"qk": nc.dram_tensor("qk_parts", (2, 3, P, NT), BF16, kind="Internal").ap(),
               "dispatch": nc.dram_tensor("dispatch", (DUMP + NT, D), F32, kind="Internal").ap(),
               "expert_out": nc.dram_tensor("expert_out", (DUMP, D), F32, kind="Internal").ap()}
    program(nc, aps, out, scratch, **options)


def kernel(**inputs):
    import concourse.bacc as bacc
    from concourse.bass_utils import run_bass_kernel_spmd

    nc = bacc.Bacc("TRN2", target_bir_lowering=False, num_devices=1)
    A = _layouts({k: np.asarray(v) for k, v in inputs.items()})
    _make(nc, A, (NT, D))
    r = run_bass_kernel_spmd(nc, [{"in_" + k: v for k, v in A.items()}], core_ids=[0])
    return r.results[0]["out_x"].reshape(B, T, D)
```

```python
from contextlib import ExitStack

import numpy as np

import concourse.bass as bass
from concourse import mybir

F32 = mybir.dt.float32
BF16 = mybir.dt.bfloat16
U32 = mybir.dt.uint32
ALU = mybir.AluOpType
ACT = mybir.ActivationFunctionType
AX = mybir.AxisListType

P = 128
D = 128
B = 2
T = 1024
NT = B * T
TILES = NT // P
CH = 512
NCH = NT // CH
EPS = 1e-5

SPLIT_Q = (0, 0, 0, 1, 1, 2)
SPLIT_K = (0, 1, 2, 0, 1, 0)


class Count:

    def __init__(self, sem, base=0):
        self.sem, self.base, self.n = sem, base, 0

    def inc(self, instruction):
        instruction.then_inc(self.sem, 1)
        self.n += 1
        return self.base + self.n

    def wait(self, engine):
        engine.wait_ge(self.sem, self.base + self.n)


class Tensors:
    pass


def open_scope(nc, g=None):
    s = Tensors()
    s.count = 0
    if g is not None:
        g.count += 1
    tag = f"_{g.count}" if g is not None else ""
    s.ctx = ExitStack()
    s.sb = lambda name, shape, dt=F32: s.ctx.enter_context(nc.sbuf_tensor(name + tag, shape, dt))

    def sem(name):
        handle = s.ctx.enter_context(nc.semaphore(name + tag))
        if g is not None:
            g.used.append(handle)
        return handle
    s.sem = sem
    s.used = []
    return s


def clear_semaphores(nc, semaphores):
    numbers = sorted(sem.num for sem in semaphores)
    with nc.Block() as block:

        @block.gpsimd
        def _(pool):
            while numbers:
                first = last = numbers.pop(0)
                while numbers and numbers[0] <= last + 1:
                    last = numbers.pop(0)
                pool.sem_clear(range(first, last + 1))


def setup(nc, g, A):
    s = open_scope(nc, g)
    with s.ctx:
        loaded = s.sem("setup_loaded")
        copied = s.sem("setup_copied")
        block = s.ctx.enter_context(nc.Block())

        @block.sync
        def _(sp):
            sp.dma_start(g.x[:], A["x"].rearrange("(i p) d -> p i d", p=P)).then_inc(loaded, 16)
            sp.dma_start(g.ident[:], A["ident"]).then_inc(loaded, 16)
            sp.wait_ge(loaded, 32)

        @block.vector
        def _(dve):
            dve.wait_ge(loaded, 32)
            nc.vector.tensor_copy(g.identb[:], g.ident[:]).then_inc(copied, 1)
            dve.wait_ge(copied, 1)


def residual_norm(nc, g, first, last):
    s = open_scope(nc, g)
    ps = g.ps
    with s.ctx:
        stats = s.sb("ln_stats", [P, TILES, 6])
        mv = s.sb("ln_mv", [P, TILES, 2])
        std = s.sb("ln_std", [P, TILES])
        rstd = s.sb("ln_rstd", [P, TILES])
        xn = g.xn
        turned = s.sem("ln_turned")
        added = s.sem("ln_added")
        ve = s.sem("ln_vector_done")
        have_std = s.sem("ln_have_std")
        normed = s.sem("ln_normed")
        xturned = s.sem("ln_xturned")
        xcopied = s.sem("ln_xcopied")
        block = s.ctx.enter_context(nc.Block())

        @block.tensor
        def _(pe):
            if not first:
                for q in range(4):
                    for k in range(4):
                        i = 4 * q + k
                        mm = nc.tensor.transpose(ps[:, q, k * P:(k + 1) * P], g.branchT[:, i * P:(i + 1) * P], g.ident[:])
                    mm.then_inc(turned, 1)
            if not last:
                for q in range(4):
                    pe.wait_ge(normed, q + 1)
                    for k in range(4):
                        i = 4 * q + k
                        mm = nc.tensor.transpose(ps[:, 4 + q, k * P:(k + 1) * P], xn[:, i, :], g.ident[:])
                    mm.then_inc(xturned, 1)

        @block.vector
        def _(dve):
            if not first:
                for q in range(4):
                    dve.wait_ge(turned, q + 1)
                    nc.vector.tensor_tensor(g.x[:, 4 * q:4 * q + 4, :], g.x[:, 4 * q:4 * q + 4, :],
                                            ps[:, q, :].rearrange("p (k d) -> p k d", d=D), ALU.add).then_inc(added, 1)
            if last:
                dve.wait_ge(added, 4)
                return
            done = Count(ve)
            for i in range(TILES):
                if not first:
                    dve.wait_ge(added, i // 4 + 1)
                done.inc(nc.vector.bn_stats(stats[:, i, :], g.x[:, i, :]))
            done.wait(dve)
            for i in range(TILES):
                done.inc(nc.vector.bn_aggr(mv[:, i, :], stats[:, i, :]))
            done.wait(dve)
            done.inc(nc.vector.tensor_scalar(mv[:, :, 1], mv[:, :, 1], EPS, None, ALU.add))
            dve.wait_ge(have_std, 1)
            done.inc(nc.vector.reciprocal(rstd[:], std[:]))
            done.wait(dve)
            for i in range(TILES):
                op = nc.vector.tensor_scalar(xn[:, i, :], g.x[:, i, :], mv[:, i, 0:1], rstd[:, i:i + 1],
                                             ALU.subtract, ALU.mult)
                if i % 4 == 3:
                    op.then_inc(normed, 1)
            for q in range(0, 4, 2):
                dve.wait_ge(xturned, q + 1)
                nc.vector.tensor_copy(g.xnT[:, q * CH:(q + 1) * CH], ps[:, 4 + q, :]).then_inc(xcopied, 1)
            dve.wait_ge(xcopied, 4)

        @block.scalar
        def _(act):
            if last:
                return
            act.wait_ge(ve, 2 * TILES + 1)
            nc.scalar.activation(std[:], mv[:, :, 1], ACT.Sqrt).then_inc(have_std, 1)
            for q in range(1, 4, 2):
                act.wait_ge(xturned, q + 1)
                nc.scalar.copy(g.xnT[:, q * CH:(q + 1) * CH], ps[:, 4 + q, :]).then_inc(xcopied, 1)


def finish(nc, g, out):
    s = open_scope(nc, g)
    with s.ctx:
        stored = s.sem("x_stored")
        block = s.ctx.enter_context(nc.Block())

        @block.sync
        def _(sp):
            sp.dma_start(out.rearrange("(i p) d -> p i d", p=P), g.x[:]).then_inc(stored, 16)
            sp.wait_ge(stored, 16)


HEADS, HD = 16, 8


PAIR_STEPS = 11


def head_mixing(nc, g, s, W):
    QB, KB = 6, 7
    ps = g.ps
    scale = float(HD) ** -0.5
    VH = 6
    wq = s.sb("wq", [P, 2, P])
    wup = s.sb("wup", [32, 3, P])
    wdown = s.sb("wdown", [P, 32])
    bdown = s.sb("bdown", [32, 1])
    bias = s.sb("bias", [P, 5, P])
    cos = s.sb("cos", [P, T // P, HD])
    sin = s.sb("sin", [P, T // P, HD])
    wout = s.sb("wout", [P, P])
    bout = s.sb("bout", [P, 1])
    xs = s.sb("xs", [P, 2, P])
    lat = s.sb("lat", [32, 2, P])
    proj = s.sb("proj", [P, 2, 5, P])
    rc = s.sb("rc", [P, 2, 2, P])
    rs = s.sb("rs", [P, 2, 2, P])
    qk = s.sb("qk", [P, 2, 2, P])
    prod = s.sb("prod", [P, 2, HEADS, HEADS, HD])
    att = s.sb("att", [P, 2, HEADS, HEADS])
    top = s.sb("top", [P, 2, HEADS])
    less = s.sb("less", [P, 2, HEADS, HEADS])
    prob = s.sb("prob", [P, 2, HEADS, HEADS])
    total = s.sb("total", [P, 2, HEADS])
    inv = s.sb("inv", [P, 2, HEADS])
    mixed = s.sb("mixed", [P, 2, HEADS, HD])
    norm = s.sb("norm", [P, 2, P])
    oT = s.sb("oT", [P, 2, P])
    loaded = s.sem("hm_loaded")
    staged = s.sem("hm_x_staged")
    latd = s.sem("hm_latent")
    latc = s.sem("hm_latent_copied")
    projd = s.sem("hm_projected")
    biased = s.sem("hm_biased")
    roped = s.sem("hm_roped")
    multd = s.sem("hm_scores_mult_dve")
    multp = s.sem("hm_scores_mult_pool")
    vec = s.sem("hm_vector_steps")
    expd = s.sem("hm_exp")
    wmd = s.sem("hm_weigh_mult_dve")
    wmp = s.sem("hm_weigh_mult_pool")
    normd = s.sem("hm_normal")
    turned = s.sem("hm_turned")
    tcopied = s.sem("hm_turned_copied")
    outd = s.sem("hm_out")
    outc = s.sem("hm_out_copied")
    tiles = dict(wq=wq, wup=wup, wdown=wdown, bdown=bdown, bias=bias, cos=cos, sin=sin, wout=wout, bout=bout)
    ALL = 16 * len(tiles)
    VS = 14

    def sync(sp):
        for n, t in tiles.items():
            sp.dma_start(t[:], W[n]).then_inc(loaded, 16)
        sp.wait_ge(loaded, ALL)

    def scalar(act, i, step, late):
        if (step, late) in ((0, False), (1, False)):
            e = step
            act.wait_ge(projd, i * 2 + e)
            nc.scalar.copy(xs[:, e, :], g.xnT[:, bass.ds((i * 2 + e) * P, P)]).then_inc(staged, 1)
        if (step, late) in ((0, True), (2, False)):
            e = step // 2
            act.wait_ge(latd, i * 2 + e + 1)
            nc.scalar.activation(lat[:, e, :], ps[0:32, KB, 384:512], ACT.Identity, bias=bdown[:]).then_inc(latc, 1)
        if (step, late) in ((4, True), (6, True)):
            e = (step - 4) // 2
            act.wait_ge(vec, i * VS + 4 * (e + 1))
            act.wait_ge(wmd, i * 2)
            act.wait_ge(wmp, i * 2)
            nc.scalar.activation(prob[:, e], less[:, e], ACT.Exp, scale=scale).then_inc(expd, 1)
        if (step, late) in ((9, False), (10, False)):
            e = step - 9
            act.wait_ge(turned, i * 2 + e + 1)
            nc.scalar.copy(oT[:, e, :], ps[:, KB, 0:P]).then_inc(tcopied, 1)
        if (step, late) in ((9, True), (10, True)):
            e = step - 9
            act.wait_ge(outd, i * 2 + e + 1)
            nc.scalar.activation(g.branchT[:, bass.ds((i * 2 + e) * P, P)], ps[:, QB, 384:512], ACT.Identity,
                                 bias=bout[:]).then_inc(outc, 1)

    def tensor(pe, i, step, late):
        if (step, late) in ((0, False), (1, True)):
            e = step
            pe.wait_ge(staged, i * 2 + e + 1)
            pe.wait_ge(biased, i * 2 + e)
            if e == 0:
                pe.wait_ge(outc, i * 2)
            nc.tensor.matmul(ps[0:32, KB, 384:512], wdown[:], xs[:, e, :], start=True, stop=True).then_inc(latd, 1)
            nc.tensor.matmul(ps[:, QB, 0:256], xs[:, e, :], wq[:].rearrange("p a n -> p (a n)"), start=True, stop=True)
        if (step, late) in ((0, True), (2, True)):
            e = step // 2
            pe.wait_ge(latc, i * 2 + e + 1)
            nc.tensor.matmul(ps[:, KB, 0:384], lat[:, e, :], wup[:].rearrange("p a n -> p (a n)"),
                             start=True, stop=True).then_inc(projd, 1)
        if (step, late) in ((9, False), (10, False)):
            e = step - 9
            pe.wait_ge(normd, i * 2 + e + 1)
            nc.tensor.transpose(ps[:, KB, 0:P], norm[:, e, :], g.ident[:]).then_inc(turned, 1)
        if (step, late) in ((9, True), (10, True)):
            e = step - 9
            pe.wait_ge(tcopied, i * 2 + e + 1)
            pe.wait_ge(outc, i * 2 + e)
            nc.tensor.matmul(ps[:, QB, 384:512], wout[:], oT[:, e, :], start=True, stop=True).then_inc(outd, 1)

    def scores_product(eng, e, h0, h1):
        q = qk[:, e, 0, :].rearrange("p (h d) -> p h d", d=HD)[:, h0:h1, None, :].to_broadcast([P, h1 - h0, HEADS, HD])
        k = qk[:, e, 1, :].rearrange("p (g d) -> p g d", d=HD)[:, None, :, :].to_broadcast([P, h1 - h0, HEADS, HD])
        return eng.tensor_tensor(prod[:, e, h0:h1], q, k, ALU.mult)

    def weigh_product(eng, e, h0, h1):
        a = prob[:, e, h0:h1, None, :].to_broadcast([P, h1 - h0, HD, HEADS])
        v = proj[:, e, 4, :].rearrange("p (g d) -> p d g", d=HD)[:, None, :, :].to_broadcast([P, h1 - h0, HD, HEADS])
        dst = prod[:, e, h0:h1].rearrange("p h g d -> p h (g d)").rearrange("p h (d g) -> p h d g", g=HEADS)
        return eng.tensor_tensor(dst, a, v, ALU.mult)

    def gpsimd(pool):
        pool.wait_ge(loaded, ALL)
        with pool.Fori(0, TILES // 2) as i:
            for e in range(2):
                n = (i * 2 + e) * 3
                pool.wait_ge(biased, i * 2 + e + 1)
                where = bass.ds((i * 2 + e) % (T // P), 1)
                c = cos[:, where, :].to_broadcast([P, HEADS, HD])
                sn = sin[:, where, :].to_broadcast([P, HEADS, HD])
                v = lambda t: t.rearrange("p (h d) -> p h d", d=HD)
                for j in range(2):
                    nc.gpsimd.tensor_tensor(v(rc[:, e, j, :]), v(proj[:, e, 2 * j, :]), c, ALU.mult)
                    last = nc.gpsimd.tensor_tensor(v(rs[:, e, j, :]), v(proj[:, e, 2 * j + 1, :]), sn, ALU.mult)
                last.then_inc(roped, 1)
                pool.wait_ge(roped, n + 1)
                pool.wait_ge(multd, i * 2)
                nc.gpsimd.tensor_tensor(qk[:, e], rc[:, e], rs[:, e], ALU.add).then_inc(roped, 1)
                pool.wait_ge(roped, n + 2)
                pool.wait_ge(vec, i * VS)
                scores_product(nc.gpsimd, e, VH, HEADS).then_inc(roped, 1)
                pool.wait_ge(roped, n + 3)
                pool.sem_inc(multp, 1)
            for e in range(2):
                pool.wait_ge(expd, i * 2 + e + 1)
                weigh_product(nc.gpsimd, e, VH, HEADS).then_inc(wmp, 1)

    def add_bias(dve, i, e):
        dve.wait_ge(projd, i * 2 + e + 1)
        dve.wait_ge(wmp, i * 2)
        nc.vector.tensor_tensor(proj[:, e, 0:2, :], ps[:, QB, 0:256].rearrange("p (a n) -> p a n", a=2), bias[:, 0:2, :], ALU.add)
        nc.vector.tensor_tensor(proj[:, e, 2:5, :], ps[:, KB, 0:384].rearrange("p (a n) -> p a n", a=3), bias[:, 2:5, :],
                                ALU.add).then_inc(biased, 1)

    def vector(dve, i, step, late):
        base = i * VS
        for e in range(2):
            n = base + 4 * e
            if (step, late) == (2 * e, True):
                add_bias(dve, i, e)
            if (step, late) == (2 + 2 * e, True):
                dve.wait_ge(roped, (i * 2 + e) * 3 + 2)
                scores_product(nc.vector, e, 0, VH).then_inc(multd, 1)
            if (step, late) == (3 + 2 * e, True):
                dve.wait_ge(multd, i * 2 + e + 1)
                dve.wait_ge(multp, i * 2 + e + 1)
                nc.vector.tensor_reduce(att[:, e].rearrange("p h g -> p (h g)"), prod[:, e].rearrange("p h g d -> p (h g) d"),
                                        AX.X, ALU.add).then_inc(vec, 1)
            if (step, late) == (4 + 2 * e, False):
                dve.wait_ge(vec, n + 1)
                nc.vector.tensor_reduce(top[:, e], att[:, e], AX.X, ALU.max).then_inc(vec, 1)
                dve.wait_ge(vec, n + 2)
                nc.vector.tensor_tensor(less[:, e], att[:, e], top[:, e, :, None].to_broadcast([P, HEADS, HEADS]),
                                        ALU.subtract).then_inc(vec, 2)
        for e in range(2):
            n = base + 8 + 3 * e
            if (step, late) == (6 + 2 * e, True):
                dve.wait_ge(expd, i * 2 + e + 1)
                nc.vector.tensor_reduce(total[:, e], prob[:, e], AX.X, ALU.add).then_inc(vec, 1)
                weigh_product(nc.vector, e, 0, VH).then_inc(wmd, 1)
            if (step, late) == (7 + 2 * e, True):
                dve.wait_ge(vec, n + 1)
                nc.vector.reciprocal(inv[:, e], total[:, e]).then_inc(vec, 1)
                dve.wait_ge(wmd, i * 2 + e + 1)
                dve.wait_ge(wmp, i * 2 + e + 1)
                nc.vector.tensor_reduce(mixed[:, e].rearrange("p h d -> p (h d)"),
                                        prod[:, e].rearrange("p h g d -> p h (g d)").rearrange("p h (d g) -> p (h d) g", g=HEADS),
                                        AX.X, ALU.add).then_inc(vec, 1)
            if (step, late) == (8 + 2 * e, False):
                dve.wait_ge(vec, n + 3)
                dve.wait_ge(turned, i * 2)
                nc.vector.tensor_tensor(norm[:, e, :].rearrange("p (h d) -> p h d", d=HD), mixed[:, e],
                                        inv[:, e, :, None].to_broadcast([P, HEADS, HD]), ALU.mult).then_inc(normd, 1)

    steps = Tensors()
    steps.sync, steps.tensor, steps.scalar, steps.vector, steps.gpsimd = sync, tensor, scalar, vector, gpsimd
    steps.loaded, steps.all_loaded, steps.out_copied = loaded, ALL, outc
    return steps


def project_qkv(nc, g, qk, Vp, W, qscale, to_clear):
    s = open_scope(nc, g)
    ps = g.ps
    with s.ctx:
        wqk = s.sb("wqk", [P, 2, P])
        bias = s.sb("qk_bias", [P, 2])
        wv = s.sb("wv", [P, P])
        bv = s.sb("bv", [P, P])
        whole = s.sb("whole", [P, 2, CH])
        rest = s.sb("rest", [P, 2, CH])
        parts = s.sb("parts", [P, 2, 3, CH], BF16)
        loaded = s.sem("qk_loaded")
        product = s.sem("qk_product")
        vproduct = s.sem("v_product")
        written = s.sem("v_written")
        cleared = s.sem("qk_cleared")
        wholed = s.sem("qk_whole")
        hi_done = s.sem("hi_done")
        rest_done = s.sem("rest_done")
        mid_done = s.sem("mid_done")
        lo_done = s.sem("lo_done")
        stored = [s.sem(f"parts_stored{j}") for j in range(2)]
        block = s.ctx.enter_context(nc.Block())

        @block.sync
        def _(sp):
            sp.dma_start(wqk[:], W["wqk"]).then_inc(loaded, 16)
            sp.dma_start(bias[:], W["bqk"]).then_inc(loaded, 16)
            sp.dma_start(wv[:], W["wv"]).then_inc(loaded, 16)
            sp.dma_start(bv[:], W["bv"]).then_inc(loaded, 16)
            with sp.Fori(0, NCH) as c:
                for j in range(2):
                    sp.wait_ge(lo_done, c * 2 + (j + 1))
                    dst = qk[j].rearrange("s p n -> p s n")[:, :, bass.ds(c * CH, CH)]
                    sp.dma_start(dst, parts[:, j, :, :]).then_inc(stored[j], 16)
            for j in range(2):
                sp.wait_ge(stored[j], 16 * NCH)

        @block.gpsimd
        def _(pool):
            for t in to_clear:
                nc.gpsimd.memset(t[:], 0.0).then_inc(cleared, 1)

        @block.tensor
        def _(pe):
            pe.wait_ge(loaded, 64)
            for i in range(TILES):
                mm = nc.tensor.matmul(ps[:, 4 + i // 4, (i % 4) * P:(i % 4 + 1) * P], g.xnT[:, i * P:(i + 1) * P], wv[:],
                                      start=True, stop=True)
                if i % 4 == 3:
                    mm.then_inc(vproduct, 1)
            with pe.Fori(0, NCH) as c:
                for j in range(2):
                    pe.wait_ge(wholed, c * 2 + j)
                    nc.tensor.matmul(ps[:, j, :], wqk[:, j, :], g.xnT[:, bass.ds(c * CH, CH)],
                                     start=True, stop=True).then_inc(product, 1)

        @block.scalar
        def _(act):
            with act.Fori(0, NCH) as c:
                for j in range(2):
                    act.wait_ge(wholed, c * 2 + (j + 1))
                    act.wait_ge(stored[j], c * 16)
                    nc.scalar.copy(parts[:, j, 0, :], whole[:, j, :]).then_inc(hi_done, 1)
                    act.wait_ge(rest_done, c * 2 + (j + 1))
                    nc.scalar.copy(parts[:, j, 1, :], rest[:, j, :]).then_inc(mid_done, 1)

        @block.vector
        def _(dve):
            dve.wait_ge(loaded, 64)
            for q in range(TILES // 4):
                dve.wait_ge(vproduct, q + 1)
                nc.vector.tensor_tensor(Vp[:, 4 * q:4 * q + 4, :], ps[:, 4 + q, :].rearrange("p (i n) -> p i n", n=P),
                                        bv[:, None, :].to_broadcast([P, 4, P]), ALU.add).then_inc(written, 1)
            with dve.Fori(0, NCH) as c:
                for j in range(2):
                    dve.wait_ge(product, c * 2 + (j + 1))
                    dve.wait_ge(lo_done, c * 2 + j)
                    nc.vector.tensor_scalar(whole[:, j, :], ps[:, j, :], bias[:, j:j + 1], qscale if j == 0 else 1.0,
                                            ALU.add, ALU.mult).then_inc(wholed, 1)
                    dve.wait_ge(hi_done, c * 2 + (j + 1))
                    nc.vector.tensor_tensor(rest[:, j, :], whole[:, j, :], parts[:, j, 0, :], ALU.subtract).then_inc(rest_done, 1)
                    dve.wait_ge(mid_done, c * 2 + (j + 1))
                    nc.vector.tensor_tensor(parts[:, j, 2, :], rest[:, j, :], parts[:, j, 1, :], ALU.subtract).then_inc(lo_done, 1)


STACK = HD * len(SPLIT_Q)
QUAD = 4
STEPS = B * HEADS // QUAD
KT = T // P


def stage_heads(sp, nc, qk, Q, K, n, landed):
    b, h0 = n // 4, (n % 4) * 4
    for dst, which, terms in ((Q, 0, SPLIT_Q), (K, 1, SPLIT_K)):
        src = qk[which].rearrange("s (h j) n -> s j h n", j=HD)
        for t, part in enumerate(terms):
            sp.dma_start(dst[HD * t:HD * (t + 1), :, :],
                         src[part][:, bass.ds(h0, 4), bass.ds(b * T, T)]).then_inc(landed, 16)


def column_softmax_attention(nc, g, qk, Vp, Q, K, W):
    s = open_scope(nc, g)
    ps = g.ps
    AV = 6
    UN = KT * QUAD
    RING = 3
    PR = 8
    with s.ctx:
        V = [s.sb(f"V{i}", [P, KT, QUAD, HD]) for i in range(2)]
        probs = s.sb("probs", [P, PR, T])
        negmax = s.sb("negmax", [P, PR])
        total = s.sb("total", [P, PR])
        inv = s.sb("inv", [P, 2, QUAD])
        vdiv = s.sb("vdiv", [P, 2, QUAD, 32])
        outT = s.sb("outT", [P, 4, NT])
        mask = s.sb("mask", [P, P])
        maskb = s.sb("maskb", [P, P], BF16)
        wout = s.sb("wout", [P, 4, P])
        bout = s.sb("bout", [P, 1])
        const = s.sem("ca_const")
        vcleared = s.sem("ca_v_cleared")
        maskd = s.sem("ca_mask")
        landed = [s.sem(f"ca_landed{i}") for i in range(2)]
        vstaged = s.sem("ca_v_staged")
        sc = s.sem("ca_scores")
        mx = s.sem("ca_max")
        ex = s.sem("ca_exp")
        invd = s.sem("ca_inverse")
        vd = s.sem("ca_v_divided")
        av = s.sem("ca_weighed")
        oc = s.sem("ca_out_copied")
        oproj = s.sem("ca_projected")
        ocopy = s.sem("ca_projected_copied")
        block = s.ctx.enter_context(nc.Block())
        AVL, VDL, EXL = 1, 1, QUAD

        @block.sync
        def _(sp):
            sp.dma_start(mask[:], W["mask"]).then_inc(const, 16)
            sp.dma_start(wout[:], W["wout"]).then_inc(const, 16)
            sp.dma_start(bout[:], W["bout"]).then_inc(const, 16)
            for e in range(2):
                stage_heads(sp, nc, qk, Q[e], K[e], e, landed[e])
            with sp.Fori(0, STEPS // 2 - 1) as i:
                for e in range(2):
                    sp.wait_ge(sc, i * 2 * UN + (e + 1) * UN)
                    stage_heads(sp, nc, qk, Q[e], K[e], i * 2 + (e + 2), landed[e])
            sp.wait_ge(const, 48)
            for e in range(2):
                sp.wait_ge(landed[e], 16 * 12 * STEPS // 2)

        @block.gpsimd
        def _(pool):
            pool.sem_inc(vd, VDL)
            nc.gpsimd.memset(vdiv[:], 0.0).then_inc(vcleared, 1)
            pool.wait_ge(vcleared, 1)

            def stage_v(n, e):
                nc.gpsimd.tensor_copy(V[e][:], Vp[:, bass.ds((n // 4) * KT, KT), bass.ds((n % 4) * QUAD * HD, QUAD * HD)]
                                      .rearrange("p i (h d) -> p i h d", d=HD)).then_inc(vstaged, 1)

            def divide(n, e):
                for jt in range(KT):
                    pool.wait_ge(invd, n * KT + (jt + 1))
                    pool.wait_ge(vstaged, n + 1)
                    pool.wait_ge(av, n * KT + (jt - 1 + AVL))
                    nc.gpsimd.tensor_tensor(vdiv[:, jt % 2, :, 0:HD], V[e][:, jt],
                                            inv[:, jt % 2, :, None].to_broadcast([P, QUAD, HD]), ALU.mult).then_inc(vd, 1)

            for e in range(2):
                nc.gpsimd.tensor_copy(V[e][:], Vp[:, 0:KT, e * QUAD * HD:(e + 1) * QUAD * HD]
                                      .rearrange("p i (h d) -> p i h d", d=HD)).then_inc(vstaged, 1)
            with pool.Fori(0, STEPS // 2 - 1) as i:
                for e in range(2):
                    divide(i * 2 + e, e)
                    pool.wait_ge(vd, i * 2 * KT + ((e + 1) * KT + VDL))
                    stage_v(i * 2 + (e + 2), e)
            for e in range(2):
                divide(STEPS - 2 + e, e)

        @block.tensor
        def _(pe):
            def scores(n, e, rnd, u):
                jt, h = u // QUAD, u % QUAD
                if u == 0:
                    pe.wait_ge(landed[e], rnd * 192 + 192)
                before = u - RING if u >= RING else max(k for k in range(UN) if k % RING == u) - UN
                pe.wait_ge(ex, n * UN + (before + 1 + EXL))
                bank = 2 * (u % RING)
                for half in range(2):
                    a, b = max(jt * P, half * CH), (half + 1) * CH
                    if a >= b:
                        continue
                    diag = jt // 4 == half
                    mm = nc.tensor.matmul(ps[:, bank + half, a % CH:CH], K[e][:, h, jt * P:(jt + 1) * P], Q[e][:, h, a:b],
                                          start=True, stop=not diag)
                    if diag:
                        a = jt % 4 * P
                        mm = nc.tensor.matmul(ps[:, bank + half, a:a + P], g.identb[:], maskb[:], start=False, stop=True)
                mm.then_inc(sc, 1)

            def weigh(n, jt):
                pe.wait_ge(vd, n * KT + (jt + 1 + VDL))
                if jt == 0:
                    pe.wait_ge(oc, n)
                for half in range(2):
                    a, b = max(jt * P, half * CH), (half + 1) * CH
                    if a >= b:
                        continue
                    for h in range(QUAD):
                        mm = nc.tensor.matmul(ps[32 * h:32 * h + 32, AV + half, a % CH:CH], vdiv[:, jt % 2, h, :],
                                              probs[:, (jt * QUAD + h) % PR, a:b],
                                              start=(jt == 0), stop=(jt == (3 if half == 0 else KT - 1)))
                mm.then_inc(av, 1)

            def step(n, e, rnd, more):
                for u in range(QUAD, UN):
                    scores(n, e, rnd, u)
                    if u % QUAD == QUAD - 1:
                        weigh(n, u // QUAD - 1)
                for u in range(QUAD) if more else []:
                    scores(n + 1, 1 - e, rnd + e, u)
                weigh(n, KT - 1)

            pe.sem_inc(av, AVL)
            pe.wait_ge(const, 48)
            pe.wait_ge(maskd, 1)
            for u in range(QUAD):
                scores(0, 0, 0, u)
            with pe.Fori(0, STEPS // 2 - 1) as i:
                for e in range(2):
                    step(i * 2 + e, e, i, True)
            for e in range(2):
                step(STEPS - 2 + e, e, STEPS // 2 - 1, e == 0)
            pe.wait_ge(oc, STEPS)
            for c in range(NCH):
                if c >= 2:
                    pe.wait_ge(ocopy, c - 1)
                for q in range(4):
                    mm = nc.tensor.matmul(ps[:, c % 2, :], wout[:, q, :], outT[:, q, c * CH:(c + 1) * CH],
                                          start=(q == 0), stop=(q == 3))
                mm.then_inc(oproj, 1)

        @block.scalar
        def _(act):
            def exp(n, u):
                jt = u // QUAD
                act.wait_ge(mx, n * UN + (u + 1))
                if u % QUAD == 0:
                    act.wait_ge(av, n * KT + (jt - 1 + AVL))
                bank = 2 * (u % RING)
                src = ps[:, bank:bank + 2, :].rearrange("p b n -> p (b n)")[:, jt * P:T]
                nc.scalar.activation(probs[:, u % PR, jt * P:T], src, ACT.Exp, bias=negmax[:, u % PR:u % PR + 1],
                                     accum_out=total[:, u % PR:u % PR + 1]).then_inc(ex, 1)

            def step(n, more):
                for u in range(QUAD, UN):
                    exp(n, u)
                for u in range(QUAD) if more else []:
                    exp(n + 1, u)
                act.wait_ge(av, n * KT + (KT + AVL))
                dst = outT[:, bass.ds(n % 4, 1), bass.ds((n // 4) * T, T)].rearrange("p a n -> p (a n)")
                nc.scalar.copy(dst, ps[:, AV:AV + 2, :].rearrange("p b n -> p (b n)")).then_inc(oc, 1)

            act.sem_inc(ex, EXL)
            for u in range(QUAD):
                exp(0, u)
            with act.Fori(0, STEPS - 1) as n:
                step(n, True)
            step(STEPS - 1, False)
            for c in range(NCH):
                act.wait_ge(oproj, c + 1)
                nc.scalar.activation(g.branchT[:, c * CH:(c + 1) * CH], ps[:, c % 2, :], ACT.Identity,
                                     bias=bout[:]).then_inc(ocopy, 1)
            act.wait_ge(ocopy, NCH)

        @block.vector
        def _(dve):
            dve.wait_ge(const, 48)
            nc.vector.tensor_copy(maskb[:], mask[:]).then_inc(maskd, 1)

            def inverse(n, jt):
                dve.wait_ge(ex, n * UN + ((jt + 1) * QUAD + EXL))
                dve.wait_ge(vd, n * KT + (jt - 1 + VDL))
                a = jt % 2 * QUAD
                nc.vector.reciprocal(inv[:, jt % 2, :], total[:, a:a + QUAD]).then_inc(invd, 1)

            def largest(n, u):
                jt = u // QUAD
                dve.wait_ge(sc, n * UN + (u + 1))
                if u % QUAD == 0:
                    dve.wait_ge(ex, n * UN + (u - QUAD + EXL))
                bank = 2 * (u % RING)
                src = ps[:, bank:bank + 2, :].rearrange("p b n -> p (b n)")[:, jt * P:T]
                nc.vector.tensor_reduce(negmax[:, u % PR:u % PR + 1], src, AX.X, ALU.max, negate=True).then_inc(mx, 1)

            def step(n, more):
                for u in range(QUAD, UN):
                    largest(n, u)
                    if u % QUAD == 1:
                        inverse(n, u // QUAD - 1)
                for u in range(QUAD) if more else []:
                    largest(n + 1, u)
                    if u == 1:
                        inverse(n, KT - 1)
                if not more:
                    inverse(n, KT - 1)

            for u in range(QUAD):
                largest(0, u)
            with dve.Fori(0, STEPS - 1) as n:
                step(n, True)
            step(STEPS - 1, False)


def route(nc, g, W, combT, experts, top, kind, prefetch, meanwhile=None):
    s = open_scope(nc, g)
    ps = g.ps
    E = experts
    with s.ctx:
        wr = s.sb("wr", [P, E])
        br = s.sb("br", [P, E])
        wh = s.sb("wh", [P, 32])
        hT = s.sb("hT", [32, NT])
        wkeys = s.sb("wkeys", [32, E])
        scale = s.sb("scale", [P, 1])
        iota = s.sb("iota", [P, E])
        logit = s.sb("logit", [P, TILES, E])
        val = s.sb("val", [P, TILES, E])
        pick = s.sb("pick", [P, TILES, E])
        top8 = s.sb("top8", [P, TILES, 8])
        idx8 = s.sb("idx8", [P, TILES, 8], U32)
        idxf = s.sb("idxf", [P, TILES, 8])
        same = s.sb("same", [P, top, TILES, E])
        total = s.sb("total", [P, TILES])
        inv = s.sb("inv", [P, TILES])
        rest = s.sb("rest", [P, TILES, E])
        parts = s.sb("parts", [P, TILES, 3, E], BF16)
        loaded = s.sem("rt_loaded")
        hashed = s.sem("rt_hashed")
        hcopied = s.sem("rt_hash_copied")
        product = s.sem("rt_logits")
        activ = s.sem("rt_activated")
        ve = s.sem("rt_vector_done")
        split = s.sem("rt_split")
        cleared = s.sem("rt_cleared")
        turned = s.sem("rt_turned")
        copied = s.sem("rt_copied")
        block = s.ctx.enter_context(nc.Block())
        tiles = dict(wr=wr, br=br, iota=iota)
        if kind == "keys":
            tiles = dict(wh=wh, wkeys=wkeys, scale=scale, iota=iota)
        ALL = 16 * len(tiles)

        @block.sync
        def _(sp):
            for n, t in tiles.items():
                sp.dma_start(t[:], W[n]).then_inc(loaded, 16)
            if meanwhile:
                meanwhile.sync(sp)
            prefetch(sp)
            sp.wait_ge(loaded, ALL)

        @block.gpsimd
        def _(pool):
            nc.gpsimd.memset(combT[:], 0.0).then_inc(cleared, 1)

        @block.tensor
        def _(pe):
            pe.wait_ge(loaded, ALL)
            if kind == "keys":
                for c in range(NCH):
                    nc.tensor.matmul(ps[0:32, 1 + c, :], wh[:], g.xnT[:, c * CH:(c + 1) * CH], start=True, stop=True).then_inc(hashed, 1)
                pe.wait_ge(hcopied, NCH)
            for i in range(TILES):
                lhs, rhs = (hT, wkeys) if kind == "keys" else (g.xnT, wr)
                mm = nc.tensor.matmul(ps[:, 0, i * E:(i + 1) * E], lhs[:, i * P:(i + 1) * P], rhs[:], start=True, stop=True)
            mm.then_inc(product, 1)
            if meanwhile:
                meanwhile.tensor(pe)
            pe.wait_ge(split, 1)
            for c in range(NCH):
                for k in range(4):
                    mm = nc.tensor.matmul(ps[0:3 * E, 4 + c, k * P:(k + 1) * P],
                                          parts[:, 4 * c + k].rearrange("p s e -> p (s e)"), g.identb[:], start=True, stop=True)
                mm.then_inc(turned, 1)

        @block.scalar
        def _(act):
            if kind == "keys":
                for c in range(NCH):
                    act.wait_ge(hashed, c + 1)
                    nc.scalar.copy(hT[:, c * CH:(c + 1) * CH], ps[0:32, 1 + c, :]).then_inc(hcopied, 1)
            act.wait_ge(ve, 1)
            if kind == "sigmoid":
                nc.scalar.activation(val[:], logit[:], ACT.Sigmoid).then_inc(activ, 1)
            else:
                act.wait_ge(ve, 2 + TILES)
                nc.scalar.activation(val[:], rest[:], ACT.Exp).then_inc(activ, 1)
            if meanwhile:
                meanwhile.scalar(act)
            act.wait_ge(cleared, 1)
            for c in range(NCH):
                act.wait_ge(turned, c + 1)
                nc.scalar.copy(combT[0:3 * E, c * CH:(c + 1) * CH], ps[0:3 * E, 4 + c, :]).then_inc(copied, 1)
            act.wait_ge(copied, NCH)

        @block.vector
        def _(dve):
            done = Count(ve)
            wide = lambda t, k: t[:, :, k:k + 1].to_broadcast([P, TILES, E])
            dve.wait_ge(loaded, ALL)
            dve.wait_ge(product, 1)
            lg = ps[:, 0, 0:TILES * E].rearrange("p (i e) -> p i e", e=E)
            if kind == "softmax":
                done.inc(nc.vector.tensor_tensor(logit[:], lg, br[:, None, :].to_broadcast([P, TILES, E]), ALU.add))
            else:
                done.inc(nc.vector.tensor_copy(logit[:], lg))
            done.wait(dve)
            chosen_by = logit
            if kind == "sigmoid":
                dve.wait_ge(activ, 1)
                done.inc(nc.vector.tensor_tensor(rest[:], val[:], br[:, None, :].to_broadcast([P, TILES, E]), ALU.add))
                done.wait(dve)
                chosen_by = rest
            for i in range(TILES):
                done.inc(nc.vector.max(top8[:, i, :], chosen_by[:, i, :]))
            done.wait(dve)
            if kind != "sigmoid":
                done.inc(nc.vector.tensor_tensor(rest[:], logit[:], wide(top8, 0), ALU.subtract))
            for i in range(TILES):
                done.inc(nc.vector.max_index(idx8[:, i, :], top8[:, i, :], chosen_by[:, i, :]))
            done.wait(dve)
            done.inc(nc.vector.tensor_copy(idxf[:], idx8[:]))
            done.wait(dve)
            for k in range(top):
                done.inc(nc.vector.tensor_tensor(same[:, k], iota[:, None, :].to_broadcast([P, TILES, E]), wide(idxf, k), ALU.is_equal))
            done.wait(dve)
            done.inc(nc.vector.tensor_tensor(pick[:], same[:, 0], same[:, 1], ALU.add))
            for k in range(2, top):
                done.wait(dve)
                done.inc(nc.vector.tensor_tensor(pick[:], pick[:], same[:, k], ALU.add))
            dve.wait_ge(activ, 1)
            done.wait(dve)
            done.inc(nc.vector.tensor_tensor(pick[:], pick[:], val[:], ALU.mult))
            done.wait(dve)
            done.inc(nc.vector.tensor_reduce(total[:], pick[:], AX.X, ALU.add))
            done.wait(dve)
            done.inc(nc.vector.reciprocal(inv[:], total[:]))
            done.wait(dve)
            if kind == "keys":
                done.inc(nc.vector.tensor_scalar(inv[:], inv[:], scale[:, 0:1], None, ALU.mult))
                done.wait(dve)
            done.inc(nc.vector.tensor_tensor(val[:], pick[:], inv[:, :, None].to_broadcast([P, TILES, E]), ALU.mult))
            done.wait(dve)
            done.inc(nc.vector.tensor_copy(parts[:, :, 0, :], val[:]))
            done.wait(dve)
            done.inc(nc.vector.tensor_tensor(rest[:], val[:], parts[:, :, 0, :], ALU.subtract))
            done.wait(dve)
            done.inc(nc.vector.tensor_copy(parts[:, :, 1, :], rest[:]))
            done.wait(dve)
            nc.vector.tensor_tensor(parts[:, :, 2, :], rest[:], parts[:, :, 1, :], ALU.subtract).then_inc(split, 1)


def gated_experts(nc, g, W, experts, hidden, top, kind, gated=True, add=False, add_xn=False, beside=None, meanwhile=None):
    units = experts * hidden
    FT = -(-units // P)
    s = open_scope(nc, g)
    ps = g.ps
    GB, UB, CB, OB = 0, 2, 4, 5
    with s.ctx:
        combT = s.sb("combT", [P, NT], BF16)
        wg = s.sb("wg", [P, FT, P])
        wu = s.sb("wu", [P, FT, P]) if gated else None
        wd = s.sb("wd", [P, FT, P])
        sel = s.sb("sel", [P, FT, P], BF16)
        PIECE = 4
        pieces = -(-FT // PIECE)
        loaded = [s.sem(f"ge_loaded{k}") for k in range(pieces)]
        todo = [("wg", wg), ("wd", wd), ("sel", sel)] + ([("wu", wu)] if gated else [])

        def load_weights(sp):
            for k in range(pieces):
                a, b = k * PIECE, min((k + 1) * PIECE, FT)
                for n, t in todo:
                    sp.dma_start(t[:, a:b, :], W[n][:, a:b, :]).then_inc(loaded[k], 16)

        route(nc, g, W, combT, experts, top, kind, load_weights, meanwhile)
        act_g = s.sb("act_g", [P, 2, CH])
        gu = s.sb("gu", [P, 2, CH])
        hid = s.sb("hid", [P, 2, CH])
        up = s.sem("ge_up")
        silud = s.sem("ge_silu")
        gud = s.sem("ge_gu")
        hidd = s.sem("ge_hidden")
        down = s.sem("ge_down")
        stored = s.sem("ge_out_copied")
        summed = s.sem("ge_out_summed")
        side = beside(nc, g, s, W) if beside else None
        block = s.ctx.enter_context(nc.Block())

        def along(engine, work, c, f, late):
            if side and f < 2 * PAIR_STEPS:
                work(engine, c * 2 + f // PAIR_STEPS, f % PAIR_STEPS, late)

        @block.sync
        def _(sp):
            if side:
                side.sync(sp)
            for k in range(pieces):
                sp.wait_ge(loaded[k], 16 * len(todo))

        @block.gpsimd
        def _(pool):
            if side:
                side.gpsimd(pool)

        @block.tensor
        def _(pe):
            if side:
                pe.wait_ge(side.loaded, side.all_loaded)
            with pe.Fori(0, NCH) as c:
                where = bass.ds(c * CH, CH)
                n = c * FT

                def down_proj(f):
                    pe.wait_ge(hidd, n + (f + 1))
                    if f == 0:
                        pe.wait_ge(stored, c)
                    nc.tensor.matmul(ps[:, OB, :], wd[:, f, :], hid[:, f % 2, :], start=(f == 0), stop=(f == FT - 1)).then_inc(down, 1)

                for f in range(FT):
                    if f % PIECE == 0:
                        pe.wait_ge(loaded[f // PIECE], 16 * len(todo))
                    if f >= 2:
                        pe.wait_ge(hidd, n + (f - 1))
                    if side:
                        along(pe, side.tensor, c, f, False)
                    nc.tensor.matmul(ps[:, GB + f % 2, :], wg[:, f, :], g.xnT[:, where], start=True, stop=True).then_inc(up, 1)
                    if gated:
                        nc.tensor.matmul(ps[:, UB + f % 2, :], wu[:, f, :], g.xnT[:, where], start=True, stop=True)
                    pe.wait_ge(hidd, n + f)
                    nc.tensor.matmul(ps[:, CB, :], sel[:, f, :], combT[:, where], start=True, stop=True).then_inc(up, 1)
                    if f >= 1:
                        down_proj(f - 1)
                    if side:
                        along(pe, side.tensor, c, f, True)
                down_proj(FT - 1)

        @block.scalar
        def _(act):
            if side:
                act.wait_ge(side.loaded, side.all_loaded)
            with act.Fori(0, NCH) as c:
                n = c * FT
                for f in range(FT):
                    if side:
                        along(act, side.scalar, c, f, False)
                    act.wait_ge(up, n * 2 + (2 * f + 1))
                    act.wait_ge(gud if gated else hidd, n + (f - 1) if f >= 2 else n)
                    nc.scalar.activation(act_g[:, f % 2, :], ps[:, GB + f % 2, :], ACT.Silu).then_inc(silud, 1)
                    if side:
                        along(act, side.scalar, c, f, True)

        @block.vector
        def _(dve):
            if side:
                dve.wait_ge(side.loaded, side.all_loaded)
            with dve.Fori(0, NCH) as c:
                n = c * FT
                where = bass.ds(c * CH, CH)
                for f in range(FT):
                    if side:
                        along(dve, side.vector, c, f, False)
                    dve.wait_ge(up, n * 2 + (2 * f + 2))
                    dve.wait_ge(silud, n + (f + 1))
                    if f >= 2:
                        dve.wait_ge(down, n + (f - 1))
                    if gated:
                        nc.vector.tensor_tensor(gu[:, f % 2, :], act_g[:, f % 2, :], ps[:, UB + f % 2, :], ALU.mult).then_inc(gud, 1)
                        dve.wait_ge(gud, n + (f + 1))
                    nc.vector.tensor_tensor(hid[:, f % 2, :], (gu if gated else act_g)[:, f % 2, :], ps[:, CB, :],
                                            ALU.mult).then_inc(hidd, 1)
                    if side:
                        along(dve, side.vector, c, f, True)
                dve.wait_ge(down, n + FT)
                if side:
                    dve.wait_ge(side.out_copied, c * 4 + 4)
                if add or side:
                    nc.vector.tensor_tensor(g.branchT[:, where], g.branchT[:, where], ps[:, OB, :], ALU.add).then_inc(stored, 1)
                else:
                    nc.vector.tensor_copy(g.branchT[:, where], ps[:, OB, :]).then_inc(stored, 1)
                if add_xn:
                    dve.wait_ge(stored, c + 1)
                    nc.vector.tensor_tensor(g.branchT[:, where], g.branchT[:, where], g.xnT[:, where], ALU.add).then_inc(summed, 1)
            dve.wait_ge(stored, NCH)
            if add_xn:
                dve.wait_ge(summed, NCH)


DI, NS, DTR, TAPS = 256, 16, 64, 4
G = DI // P
PADT = T + TAPS - 1
DT_MIN, DT_MAX = 0.001, 0.1
ES, CAP, FH = 16, P, 512
FS = FH // P
DUMP = ES * CAP


def scan_inputs(nc, g, W, t, r, dispatch):
    s = open_scope(nc, g)
    ps = g.ps
    XS, RES, CV, DTB, BCB = 0, 2, 4, 6, 7
    with s.ctx:
        win = s.sb("win", [P, 4, P])
        convk = s.sb("convk", [P, G, TAPS, P])
        convb = s.sb("convb", [P, G])
        wxdt = s.sb("wxdt", [P, G, DTR])
        wxbc = s.sb("wxbc", [P, G, 96])
        wdt = s.sb("wdt", [DTR, G, P])
        bdt = s.sb("bdt", [P, G])
        alog = s.sb("alog", [P, G, NS])
        xs = s.sb("xs", [P, G, B * PADT])
        dtraw = s.sb("dtraw", [DTR, 2, CH])
        rest = s.sb("rest", [96, 2, CH])
        mid = s.sb("mid", [96, 2, CH], BF16)
        loaded = s.sem("si_loaded")
        cleared = s.sem("si_cleared")
        xsd, xsc = s.sem("si_xs"), s.sem("si_xs_copied")
        resd, resc = s.sem("si_res"), s.sem("si_res_silu")
        cvd, cvc = s.sem("si_conv"), s.sem("si_u")
        prd, dtc = s.sem("si_dt_bc"), s.sem("si_dt_copied")
        bcs = s.sem("si_bc_split")
        dpd, dpc = s.sem("si_dt_projected"), s.sem("si_dt_clamped")
        zero_rows = s.sb("zero_rows", [P, D])
        zeroed, table_cleared, sent = s.sem("si_zeroed"), s.sem("si_table_cleared"), s.sem("si_sent")
        expd, lnd, clipd, dud = s.sem("si_exp"), s.sem("si_ln"), s.sem("si_clipped"), s.sem("si_du")
        block = s.ctx.enter_context(nc.Block())
        tiles = dict(win=win, convk=convk, convb=convb, wxdt=wxdt, wxbc=wxbc, wdt=wdt, bdt=bdt, alog=alog)
        ALL = 16 * (len(tiles) + 2)

        @block.sync
        def _(sp):
            for n, d in tiles.items():
                sp.dma_start(d[:], W[n]).then_inc(loaded, 16)
            sp.dma_start(t.seln[:], W["seln"]).then_inc(loaded, 16)
            sp.dma_start(t.Dskip[:], W["D"]).then_inc(loaded, 16)
            sp.wait_ge(zeroed, 1)
            for e in range(ES):
                sp.dma_start(dispatch[e * CAP:(e + 1) * CAP, :], zero_rows[:]).then_inc(table_cleared, 16)
            sp.wait_ge(loaded, ALL)

        def at(c, tap=TAPS - 1):
            return bass.ds(c * CH + (c // 2) * (TAPS - 1) + tap, CH)

        @block.tensor
        def _(pe):
            pe.wait_ge(loaded, ALL)
            pe.wait_ge(cleared, 1)
            with pe.Fori(0, NCH) as c:
                here = bass.ds(c * CH, CH)
                pe.wait_ge(xsc, c)
                pe.wait_ge(dpc, c)
                for k in range(G):
                    mm = nc.tensor.matmul(ps[:, XS + k, :], win[:, k, :], g.xnT[:, here], start=True, stop=True)
                mm.then_inc(xsd, 1)
                pe.wait_ge(resc, c)
                for k in range(G):
                    mm = nc.tensor.matmul(ps[:, RES + k, :], win[:, G + k, :], g.xnT[:, here], start=True, stop=True)
                mm.then_inc(resd, 1)
                pe.wait_ge(xsc, c + 1)
                pe.wait_ge(cvc, c)
                for k in range(G):
                    for tap in range(TAPS):
                        mm = nc.tensor.matmul(ps[:, CV + k, :], convk[:, k, tap, :], xs[:, k, at(c, tap)],
                                              start=(tap == 0), stop=(tap == TAPS - 1))
                mm.then_inc(cvd, 1)
                pe.wait_ge(cvc, c + 1)
                pe.wait_ge(dtc, c)
                pe.wait_ge(bcs, c * 5)
                for k in range(G):
                    nc.tensor.matmul(ps[0:DTR, DTB, :], wxdt[:, k, :], t.uT[:, k, here], start=(k == 0), stop=(k == G - 1))
                for k in range(G):
                    mm = nc.tensor.matmul(ps[0:96, BCB, :], wxbc[:, k, :], t.uT[:, k, here], start=(k == 0), stop=(k == G - 1))
                mm.then_inc(prd, 1)
                pe.wait_ge(dtc, c + 1)
                for k in range(G):
                    mm = nc.tensor.matmul(ps[:, XS + k, :], wdt[:, k, :], dtraw[:, 0, :], start=True, stop=True)
                mm.then_inc(dpd, 1)

        @block.scalar
        def _(act):
            act.wait_ge(loaded, ALL)
            with act.Fori(0, NCH) as c:
                here = bass.ds(c * CH, CH)
                act.wait_ge(xsd, c + 1)
                nc.scalar.copy(xs[:, :, at(c)], ps[:, XS:XS + G, :]).then_inc(xsc, 1)
                act.wait_ge(resd, c + 1)
                nc.scalar.activation(t.sres[:, :, here], ps[:, RES:RES + G, :], ACT.Silu).then_inc(resc, 1)
                act.wait_ge(cvd, c + 1)
                nc.scalar.activation(t.uT[:, 0, here], ps[:, CV, :], ACT.Silu, bias=convb[:, 0:1])
                nc.scalar.activation(t.uT[:, 1, here], ps[:, CV + 1, :], ACT.Silu, bias=convb[:, 1:2]).then_inc(cvc, 1)
                act.wait_ge(prd, c + 1)
                act.wait_ge(dpd, c)
                nc.scalar.copy(dtraw[:, 0, :], ps[0:DTR, DTB, :]).then_inc(dtc, 1)
            act.wait_ge(dpc, NCH)
            nc.scalar.activation(t.delta[:], t.delta[:], ACT.Exp).then_inc(expd, 1)
            nc.scalar.activation(t.A[:], alog[:], ACT.Exp).then_inc(expd, 1)
            act.wait_ge(expd, 2)
            nc.scalar.activation(t.delta[:], t.delta[:], ACT.Ln, bias=1.0).then_inc(lnd, 1)

        @block.gpsimd
        def _(pool):
            nc.gpsimd.memset(zero_rows[:], 0.0).then_inc(zeroed, 1)
            nc.gpsimd.memset(xs[:], 0.0).then_inc(cleared, 1)
            pool.wait_ge(table_cleared, 16 * ES)
            for i in range(TILES):
                nc.gpsimd.indirect_dma_start(dispatch, bass.IndirectOffsetOnAxis(ap=r.scatter[:, i:i + 1], axis=0),
                                             g.xn[:, i, :], None).then_inc(sent, 16)
            pool.wait_ge(sent, 16 * TILES)

        @block.vector
        def _(dve):
            dve.wait_ge(loaded, ALL)
            with dve.Fori(0, NCH) as c:
                here = bass.ds(c * CH, CH)
                n = c * 5
                dve.wait_ge(prd, c + 1)
                nc.vector.tensor_copy(t.bc[:, here], ps[0:96, BCB, :]).then_inc(bcs, 1)
                dve.wait_ge(bcs, n + 1)
                nc.vector.tensor_tensor(rest[:, 0, :], ps[0:96, BCB, :], t.bc[:, here], ALU.subtract).then_inc(bcs, 1)
                dve.wait_ge(bcs, n + 2)
                nc.vector.tensor_copy(mid[:, 0, :], rest[:, 0, :]).then_inc(bcs, 1)
                dve.wait_ge(bcs, n + 3)
                nc.vector.tensor_copy(t.bc[32:64, here], mid[32:64, 0, :]).then_inc(bcs, 1)
                nc.vector.tensor_tensor(t.bc[64:96, here], rest[64:96, 0, :], mid[64:96, 0, :], ALU.subtract).then_inc(bcs, 1)
                dve.wait_ge(dpd, c + 1)
                nc.vector.tensor_scalar(t.delta[:, 0, here], ps[:, XS, :], bdt[:, 0:1], 0.0, ALU.add, ALU.min)
                nc.vector.tensor_scalar(t.delta[:, 1, here], ps[:, XS + 1, :], bdt[:, 1:2], 0.0, ALU.add, ALU.min).then_inc(dpc, 1)
            dve.wait_ge(lnd, 1)
            nc.vector.tensor_scalar(t.delta[:], t.delta[:], DT_MIN, DT_MAX, ALU.max, ALU.min).then_inc(clipd, 1)
            nc.vector.tensor_scalar(t.A[:], t.A[:], -1.0, None, ALU.mult).then_inc(clipd, 1)
            dve.wait_ge(clipd, 2)
            nc.vector.tensor_tensor(t.du[:], t.delta[:], t.uT[:], ALU.mult).then_inc(dud, 1)
            dve.wait_ge(dud, 1)


def state_scan(nc, g, W, t, r, expert_out):
    s = open_scope(nc, g)
    ps = g.ps
    BB, CB, Y = 0, 2, 4
    with s.ctx:
        bsp = s.sb("b_spread", [P, 2, T])
        csp = s.sb("c_spread", [P, 2, T])
        decay = s.sb("decay", [P, 2, G, T])
        drive = s.sb("drive", [P, 2, G, T])
        state = s.sb("state", [P, G, T])
        read = s.sb("read", [P, 2, G, T])
        zero = s.sb("zero", [P, CH], BF16)
        skip = read[:, 0]
        gated = t.du
        wo = s.sb("wo", [P, G, P])
        loaded = s.sem("ss_loaded")
        zeroed = s.sem("ss_zeroed")
        spread = s.sem("ss_spread")
        copied = s.sem("ss_spread_copied")
        decayd = s.sem("ss_decay")
        drived = s.sem("ss_drive")
        scand = s.sem("ss_scan")
        readd = s.sem("ss_read")
        summed = s.sem("ss_summed")
        ycopied = s.sem("ss_y_copied")
        gatedd = s.sem("ss_gated")
        outd = s.sem("ss_out")
        outc = s.sem("ss_out_copied")
        back = s.sb("back", [P, TILES, D])
        got, addd = s.sem("ss_got"), s.sem("ss_added")
        block = s.ctx.enter_context(nc.Block())

        @block.sync
        def _(sp):
            sp.dma_start(wo[:], W["wo"]).then_inc(loaded, 16)
            sp.wait_ge(loaded, 16)

        @block.tensor
        def _(pe):
            pe.sem_inc(summed, 1)
            pe.wait_ge(zeroed, 1)
            pe.wait_ge(loaded, 16)

            def spread_state(b, m):
                n = m + b * NS
                pe.wait_ge(copied, n * 2)
                for j, bank in ((0, BB), (1, CB)):
                    for half in range(2):
                        mm = nc.tensor.matmul(ps[:, bank + half, :], t.seln[:, bass.ds(m + j * NS, 1), :].rearrange("k a p -> k (a p)"),
                                              t.bc[:, b * T + half * CH:b * T + (half + 1) * CH], start=True, stop=True)
                    mm.then_inc(spread, 1)

            def sum_state(m, e):
                for k in range(G):
                    pe.wait_ge(readd, m * G + (G + k + 1))
                    for half in range(2):
                        mm = nc.tensor.matmul(ps[:, Y + 2 * k + half, :], g.ident[:], read[:, e, k, half * CH:(half + 1) * CH],
                                              start=False, stop=False, skip_group_check=True)
                mm.then_inc(summed, 1)

            for b in range(B):
                pe.wait_ge(ycopied, b * G)
                for k in range(2 * G):
                    nc.tensor.matmul(ps[:, Y + k, :], zero[:, 0:P], zero[:], start=True, stop=False, skip_group_check=True)
                spread_state(b, 0)
                spread_state(b, 1)
                with pe.Fori(0, NS // 2 - 1) as i:
                    for e in range(2):
                        spread_state(b, i * 2 + (e + 2))
                        sum_state(i * 2 + (b * NS + e), e)
                sum_state(b * NS + NS - 2, 0)
                sum_state(b * NS + NS - 1, 1)
            for c in range(NCH):
                pe.wait_ge(gatedd, (c // 2 + 1) * G)
                if c >= 2:
                    pe.wait_ge(outc, c - 1)
                for k in range(G):
                    mm = nc.tensor.matmul(ps[:, BB + c % 2, :], wo[:, k, :], gated[:, k, c * CH:(c + 1) * CH],
                                          start=(k == 0), stop=(k == G - 1))
                mm.then_inc(outd, 1)

        @block.scalar
        def _(act):
            for b in range(B):
                with act.Fori(0, NS // 2) as i:
                    for e in range(2):
                        m = i * 2 + e
                        n = i * 2 + (b * NS + e)
                        act.wait_ge(spread, n * 2 + 1)
                        act.wait_ge(drived, n * G)
                        nc.scalar.copy(bsp[:, e, :], ps[:, BB:BB + 2, :].rearrange("p b n -> p (b n)")).then_inc(copied, 1)
                        act.wait_ge(spread, n * 2 + 2)
                        act.wait_ge(readd, n * G)
                        nc.scalar.copy(csp[:, e, :], ps[:, CB:CB + 2, :].rearrange("p b n -> p (b n)")).then_inc(copied, 1)
                        act.wait_ge(scand, n * G)
                        for k in range(G):
                            nc.scalar.activation(decay[:, e, k, :], t.delta[:, k, b * T:(b + 1) * T], ACT.Exp,
                                                 scale=t.A[:, k, bass.ds(m, 1)]).then_inc(decayd, 1)
            for c in range(NCH):
                act.wait_ge(outd, c + 1)
                nc.scalar.copy(g.branchT[:, c * CH:(c + 1) * CH], ps[:, BB + c % 2, :]).then_inc(outc, 1)
            act.wait_ge(outc, NCH)

        @block.gpsimd
        def _(pool):
            pool.sem_inc(drived, G)
            for i in range(TILES):
                nc.gpsimd.indirect_dma_start(back[:, i, :], None, expert_out,
                                             bass.IndirectOffsetOnAxis(ap=r.gather[:, i:i + 1], axis=0)).then_inc(got, 16)
            for b in range(B):
                with pool.Fori(0, NS // 2) as i:
                    for e in range(2):
                        n = i * 2 + (b * NS + e)
                        pool.wait_ge(copied, n * 2 + 1)
                        pool.wait_ge(scand, n * G)
                        for k in range(G):
                            nc.gpsimd.tensor_tensor(drive[:, e, k, :], t.du[:, k, b * T:(b + 1) * T], bsp[:, e, :],
                                                    ALU.mult).then_inc(drived, 1)

        @block.vector
        def _(dve):
            dve.sem_inc(scand, G)
            dve.sem_inc(readd, G)
            nc.vector.memset(zero[:], 0.0).then_inc(zeroed, 1)
            for b in range(B):
                if b == 1:
                    dve.wait_ge(got, 16 * TILES)
                    for i in range(TILES):
                        nc.vector.scalar_tensor_tensor(g.x[:, i, :], back[:, i, :], r.factor[:, i:i + 1], g.x[:, i, :],
                                                       ALU.mult, ALU.add).then_inc(addd, 1)
                with dve.Fori(0, NS // 2) as i:
                    for e in range(2):
                        n = i * 2 + (b * NS + e)
                        dve.wait_ge(summed, n)
                        dve.wait_ge(readd, n * G + G)
                        for k in range(G):
                            dve.wait_ge(decayd, n * G + (k + 1))
                            dve.wait_ge(drived, n * G + (G + k + 1))
                            nc.vector.tensor_tensor_scan(state[:, k, :], decay[:, e, k, :], drive[:, e, k, :], 0.0,
                                                         ALU.mult, ALU.add).then_inc(scand, 1)
                        for k in range(G):
                            dve.wait_ge(scand, n * G + (G + k + 1))
                            dve.wait_ge(copied, n * 2 + 2)
                            nc.vector.tensor_tensor(read[:, e, k, :], state[:, k, :], csp[:, e, :], ALU.mult).then_inc(readd, 1)
                dve.wait_ge(summed, (b + 1) * NS + 1)
                here = slice(b * T, (b + 1) * T)
                for k in range(G):
                    nc.vector.scalar_tensor_tensor(skip[:, k, :], t.uT[:, k, here], t.Dskip[:, k:k + 1],
                                                   ps[:, Y + 2 * k:Y + 2 * k + 2, :].rearrange("p b n -> p (b n)"),
                                                   ALU.mult, ALU.add).then_inc(ycopied, 1)
                dve.wait_ge(ycopied, (b + 1) * G)
                for k in range(G):
                    nc.vector.tensor_tensor(gated[:, k, here], skip[:, k, :], t.sres[:, k, here], ALU.mult).then_inc(gatedd, 1)
            dve.wait_ge(gatedd, B * G)
            dve.wait_ge(addd, TILES)


def scan_and_experts(nc, g, W, dispatch, expert_out):
    s = open_scope(nc, g)
    t, r = Tensors(), Tensors()
    with s.ctx:
        r.factor = s.sb("factor", [P, TILES])
        r.gather = s.sb("gather", [P, TILES], U32)
        r.scatter = s.sb("scatter", [P, TILES], U32)
        switch_route(nc, g, W, r)
        t.sres = s.sb("sres", [P, G, NT])
        t.uT = s.sb("uT", [P, G, NT])
        t.delta = s.sb("delta", [P, G, NT])
        t.du = s.sb("du", [P, G, NT])
        t.A = s.sb("A", [P, G, NS])
        t.bc = s.sb("bc", [96, NT], BF16)
        t.seln = s.sb("seln", [96, 2 * NS, P], BF16)
        t.Dskip = s.sb("Dskip", [P, G])
        scan_inputs(nc, g, W, t, r, dispatch)
        switch_experts(nc, g, W, dispatch, expert_out)
        state_scan(nc, g, W, t, r, expert_out)


def switch_route(nc, g, W, r):
    s = open_scope(nc, g)
    ps = g.ps
    with s.ctx:
        wr = s.sb("wr", [P, ES])
        iota = s.sb("iota", [P, ES])
        tri = s.sb("tri", [P, P], BF16)
        ones = s.sb("ones", [P, P], BF16)
        token = s.sb("token", [P, TILES])
        restart = s.sb("restart", [P, ES, TILES])
        logit = s.sb("logit", [P, TILES, ES])
        less = s.sb("less", [P, TILES, ES])
        ex = s.sb("ex", [P, TILES, ES])
        top8 = s.sb("top8", [P, TILES, 8])
        idx8 = s.sb("idx8", [P, TILES, 8], U32)
        idxf = s.sb("idxf", [P, TILES])
        hot = s.sb("hot", [P, TILES, ES])
        hotb = s.sb("hotb", [P, TILES, ES], BF16)
        tot = s.sb("tot", [P, ES, TILES])
        upto = s.sb("upto", [P, ES, TILES])
        place = s.sb("place", [P, TILES, ES])
        loc = s.sb("loc", [P, TILES])
        valid = s.sb("valid", [P, TILES])
        total = s.sb("total", [P, TILES])
        row = s.sb("row", [P, 4, TILES])
        loaded = s.sem("sr_loaded")
        product = s.sem("sr_logits")
        expd = s.sem("sr_exp")
        hotd = s.sem("sr_hot")
        counted = s.sem("sr_counted")
        ve = s.sem("sr_vector_done")
        block = s.ctx.enter_context(nc.Block())
        tiles = dict(wr=wr, iota=iota, tri=tri, ones=ones, token=token, restart=restart)
        ALL = 16 * len(tiles)

        @block.sync
        def _(sp):
            for n, d in tiles.items():
                sp.dma_start(d[:], W[n]).then_inc(loaded, 16)
            sp.wait_ge(loaded, ALL)

        @block.tensor
        def _(pe):
            pe.wait_ge(loaded, ALL)
            for i in range(TILES):
                mm = nc.tensor.matmul(ps[:, 0, i * ES:(i + 1) * ES], g.xnT[:, i * P:(i + 1) * P], wr[:], start=True, stop=True)
            mm.then_inc(product, 1)
            pe.wait_ge(hotd, 1)
            flat = hotb[:].rearrange("p i e -> p (i e)")
            nc.tensor.matmul(ps[:, 1, 0:TILES * ES], tri[:], flat, start=True, stop=True)
            nc.tensor.matmul(ps[:, 2, 0:TILES * ES], ones[:], flat, start=True, stop=True).then_inc(counted, 1)

        @block.scalar
        def _(act):
            act.wait_ge(expd, 1)
            nc.scalar.activation(ex[:], less[:], ACT.Exp).then_inc(expd, 1)
            act.wait_ge(expd, 2)

        @block.vector
        def _(dve):
            done = Count(ve)

            def then(instruction):
                done.inc(instruction)
                done.wait(dve)
            wide = lambda a: a[:, :, None].to_broadcast([P, TILES, ES])
            dve.wait_ge(loaded, ALL)
            dve.wait_ge(product, 1)
            then(nc.vector.tensor_copy(logit[:], ps[:, 0, 0:TILES * ES].rearrange("p (i e) -> p i e", e=ES)))
            for i in range(TILES):
                done.inc(nc.vector.max(top8[:, i, :], logit[:, i, :]))
            done.wait(dve)
            nc.vector.tensor_tensor(less[:], logit[:], top8[:, :, 0:1].to_broadcast([P, TILES, ES]), ALU.subtract).then_inc(expd, 1)
            for i in range(TILES):
                done.inc(nc.vector.max_index(idx8[:, i, :], top8[:, i, :], logit[:, i, :]))
            done.wait(dve)
            then(nc.vector.tensor_copy(idxf[:], idx8[:, :, 0]))
            then(nc.vector.tensor_tensor(hot[:], iota[:, None, :].to_broadcast([P, TILES, ES]), wide(idxf), ALU.is_equal))
            nc.vector.tensor_copy(hotb[:], hot[:]).then_inc(hotd, 1)
            dve.wait_ge(expd, 2)
            then(nc.vector.tensor_reduce(total[:], ex[:], AX.X, ALU.add))
            then(nc.vector.reciprocal(total[:], total[:]))
            dve.wait_ge(counted, 1)
            then(nc.vector.tensor_copy(tot[:], ps[:, 2, 0:TILES * ES].rearrange("p (i e) -> p e i", e=ES)))
            then(nc.vector.tensor_tensor_scan(upto[:].rearrange("p e i -> p (e i)"), restart[:].rearrange("p e i -> p (e i)"),
                                              tot[:].rearrange("p e i -> p (e i)"), 0.0, ALU.mult, ALU.add))
            then(nc.vector.tensor_tensor(upto[:], upto[:], tot[:], ALU.subtract))
            then(nc.vector.tensor_tensor(place[:], ps[:, 1, 0:TILES * ES].rearrange("p (i e) -> p i e", e=ES),
                                         upto[:].rearrange("p e i -> p i e"), ALU.add))
            then(nc.vector.tensor_tensor(place[:], place[:], hot[:], ALU.mult))
            then(nc.vector.tensor_reduce(loc[:], place[:], AX.X, ALU.add))
            then(nc.vector.tensor_scalar(valid[:], loc[:], CAP + 0.5, None, ALU.is_lt))
            then(nc.vector.tensor_tensor(r.factor[:], total[:], valid[:], ALU.mult))
            then(nc.vector.tensor_scalar(loc[:], loc[:], float(CAP), -1.0, ALU.min, ALU.add))
            then(nc.vector.scalar_tensor_tensor(row[:, 0], idxf[:], float(CAP), loc[:], ALU.mult, ALU.add))
            then(nc.vector.tensor_tensor(row[:, 1], row[:, 0], token[:], ALU.subtract))
            then(nc.vector.tensor_tensor(row[:, 2], row[:, 1], valid[:], ALU.mult))
            then(nc.vector.tensor_tensor(row[:, 3], row[:, 2], token[:], ALU.add))
            then(nc.vector.tensor_copy(r.gather[:], row[:, 0]))
            then(nc.vector.tensor_copy(r.scatter[:], row[:, 3]))


def switch_experts(nc, g, W, dispatch, expert_out):
    s = open_scope(nc, g)
    ps = g.ps
    HB, OB, TB = 0, 2, 4
    with s.ctx:
        rows = s.sb("rows", [P, ES, D])
        rowsT = s.sb("rowsT", [P, ES * CAP])
        w1 = s.sb("w1", [P, 2, FH])
        w2 = s.sb("w2", [P, 2, FS, D])
        hid = s.sb("hid", [P, 2, FS, CAP])
        eo = s.sb("eo", [P, 2, D])
        rowsl = s.sem("se_rows_loaded")
        turned = s.sem("se_turned")
        tcopied = s.sem("se_turned_copied")
        wl = [s.sem(f"se_weights_loaded{e}") for e in range(2)]
        hd, hc = s.sem("se_hidden"), s.sem("se_hidden_relu")
        od, oc = s.sem("se_out"), s.sem("se_out_copied")
        os_ = [s.sem(f"se_out_stored{e}") for e in range(2)]
        block = s.ctx.enter_context(nc.Block())

        @block.sync
        def _(sp):
            sp.dma_start(rows[:], dispatch[0:DUMP, :].rearrange("(e p) d -> p e d", p=P)).then_inc(rowsl, 16)
            for e in range(2):
                sp.dma_start(w1[:, e, :], W["w1"][e]).then_inc(wl[e], 16)
                sp.dma_start(w2[:, e], W["w2"][e]).then_inc(wl[e], 16)
            with sp.Fori(0, ES // 2 - 1) as i:
                for e in range(2):
                    sp.wait_ge(od, i * 2 + (e + 1))
                    nxt = bass.ds(i * 2 + (e + 2), 1)
                    sp.dma_start(w1[:, e, :], W["w1"][nxt].rearrange("a p f -> p (a f)")).then_inc(wl[e], 16)
                    sp.dma_start(w2[:, e], W["w2"][nxt].rearrange("a p f m -> p (a f) m")).then_inc(wl[e], 16)
                    sp.wait_ge(oc, i * 2 + (e + 1))
                    sp.dma_start(expert_out[bass.ds((i * 2 + e) * CAP, CAP), :], eo[:, e, :]).then_inc(os_[e], 16)
            for e in range(2):
                sp.wait_ge(oc, ES - 1 + e)
                sp.dma_start(expert_out[(ES - 2 + e) * CAP:(ES - 1 + e) * CAP, :], eo[:, e, :]).then_inc(os_[e], 16)
            for e in range(2):
                sp.wait_ge(os_[e], 16 * ES // 2)
                sp.wait_ge(wl[e], 32 * ES // 2)

        @block.tensor
        def _(pe):
            pe.wait_ge(rowsl, 16)
            for q in range(4):
                for k in range(4):
                    mm = nc.tensor.transpose(ps[:, TB + q, k * P:(k + 1) * P], rows[:, 4 * q + k, :], g.ident[:])
                mm.then_inc(turned, 1)
            pe.wait_ge(tcopied, 4)
            with pe.Fori(0, ES // 2) as i:
                for e in range(2):
                    pe.wait_ge(wl[e], i * 32 + 32)
                    pe.wait_ge(hc, i * 2)
                    for f in range(FS):
                        mm = nc.tensor.matmul(ps[:, HB + e, f * CAP:(f + 1) * CAP], w1[:, e, f * P:(f + 1) * P],
                                              rowsT[:, bass.ds((i * 2 + e) * CAP, CAP)], start=True, stop=True)
                    mm.then_inc(hd, 1)
                for e in range(2):
                    pe.wait_ge(hc, i * 2 + (e + 1))
                    pe.wait_ge(oc, i * 2)
                    for f in range(FS):
                        mm = nc.tensor.matmul(ps[:, OB + e, 0:D], hid[:, e, f, :], w2[:, e, f, :], start=(f == 0), stop=(f == FS - 1))
                    mm.then_inc(od, 1)

        @block.scalar
        def _(act):
            with act.Fori(0, ES // 2) as i:
                for e in range(2):
                    act.wait_ge(hd, i * 2 + (e + 1))
                    act.wait_ge(od, i * 2)
                    nc.scalar.activation(hid[:, e].rearrange("p f n -> p (f n)"), ps[:, HB + e, :], ACT.Relu).then_inc(hc, 1)

        @block.vector
        def _(dve):
            for q in range(4):
                dve.wait_ge(turned, q + 1)
                nc.vector.tensor_copy(rowsT[:, q * CH:(q + 1) * CH], ps[:, TB + q, :]).then_inc(tcopied, 1)
            with dve.Fori(0, ES // 2) as i:
                for e in range(2):
                    dve.wait_ge(od, i * 2 + (e + 1))
                    dve.wait_ge(os_[e], i * 16)
                    nc.vector.tensor_copy(eo[:, e, :], ps[:, OB + e, 0:D]).then_inc(oc, 1)


PAIRS = 8
HEAD3 = 64
SEGMENT = 64
STRIDE = 4
REACH = STRIDE * SEGMENT
RES = P // STRIDE
HALF = KT // 2


def halves(qt):
    near = [kt for kt in range(KT) if kt != qt and P * (abs(kt - qt) - 1) < REACH]
    return sorted({kt // HALF for kt in near})


def width(qt):
    return P * (1 + len(halves(qt)))


def dilated_attention(nc, g, W, outT):
    s = open_scope(nc, g)
    ps = g.ps
    PB, TB, OB = 2, 4, 6
    WIDE = 3 * P
    UN = 2 * KT
    with s.ctx:
        w = s.sb("w3", [P, 3, P])
        mask = s.sb("mask3", [P, KT, WIDE])
        xr = s.sb("xnT_by_residue", [P, NT])
        Q = [[s.sb(f"Q3_{b}{h}", [P, T]) for h in range(2)] for b in range(B)]
        K = [s.sb(f"K3_{b}", [P, T]) for b in range(B)]
        V = [s.sb(f"V3_{b}", [P, KT, P]) for b in range(B)]
        VR = [s.sb(f"VR3_{b}", [P, 2, STRIDE, P]) for b in range(B)]
        masked = [s.sb(f"masked{h}", [P, WIDE]) for h in range(2)]
        probs = [[s.sb(f"probs3_{k}{h}", [P, WIDE]) for h in range(2)] for k in range(2)]
        ownT = [[s.sb(f"ownT{k}{h}", [P, P]) for h in range(2)] for k in range(2)]
        farT = [s.sb(f"farT{h}", [P, 2, STRIDE, KT, RES]) for h in range(2)]
        mx = s.sb("mx3", [P, UN])
        negmax = s.sb("negmax3", [P, UN])
        total = s.sb("total3", [P, UN])
        inv = s.sb("inv3", [P, UN])
        const = s.sem("da_const")
        wloaded = s.sem("da_weights")
        cleared = s.sem("da_cleared")
        permuted = s.sem("da_permuted")
        projected = s.sem("da_projected")
        copied = s.sem("da_copied")
        sc = s.sem("da_scores")
        mxd = s.sem("da_max")
        maxd = s.sem("da_masked")
        ex = s.sem("da_exp")
        invd = s.sem("da_inverse")
        divd = s.sem("da_divided")
        tr = s.sem("da_turned")
        ev_dve = s.sem("da_turned_copied_dve")
        ev_act = s.sem("da_turned_copied_act")
        av = s.sem("da_weighed")
        oc = s.sem("da_out_copied")
        block = s.ctx.enter_context(nc.Block())

        def at_least(engine, sem, value):
            if not isinstance(value, int) or value > 0:
                engine.wait_ge(sem, value)

        def before(n, b, i, k):
            if i >= k:
                return n, b, i - k
            return None if isinstance(n, int) and n == 0 else (n - 1, 1 - b, i - k + KT)

        PROJ = [(which, c) for which in "qkvr" for c in range(2)]
        NPROJ = len(PROJ)
        IN_SLOT = [[0], [1], [2], [3], [4], [5, 6], [7], []]

        @block.sync
        def _(sp):
            sp.dma_start(w[:], W["wqkv"][0]).then_inc(wloaded, 16)
            sp.dma_start(mask[:], W["mask"]).then_inc(const, 16)
            with sp.Fori(0, PAIRS - 1) as hp:
                sp.wait_ge(projected, hp * 2 * NPROJ + 2 * NPROJ)
                sp.dma_start(w[:], W["wqkv"][bass.ds(hp + 1, 1)].rearrange("a p s n -> (a p) s n")).then_inc(wloaded, 16)
            sp.wait_ge(wloaded, 16 * PAIRS)
            sp.wait_ge(const, 16)

        @block.tensor
        def _(pe):
            def project(n, b, j, bank):
                which, c = PROJ[j]
                if j == 0:
                    pe.wait_ge(wloaded, (n // B) * 16 + 16)
                if which in "qk":
                    a = b * T + c * CH
                    mm = nc.tensor.matmul(ps[:, bank, :], w[:, "qk".index(which), :], xr[:, a:a + CH], start=True, stop=True)
                else:
                    for k in range(4):
                        if which == "v":
                            rows = xr[:, b * T + (4 * c + k) * P:b * T + (4 * c + k + 1) * P]
                        else:
                            rows = g.xnT[:, b * T + c * CH + k:b * T + (c + 1) * CH:STRIDE]
                        mm = nc.tensor.matmul(ps[:, bank, k * P:(k + 1) * P], rows, w[:, 2, :], start=True, stop=True)
                mm.then_inc(projected, 1)

            def scores(n, b, qt, h):
                u = 2 * qt + h
                if qt == 0:
                    pe.wait_ge(copied, n * NPROJ + NPROJ)
                at_least(pe, maxd, n * UN + (u - 1))
                nc.tensor.matmul(ps[:, h, 0:P], Q[b][h][:, qt * P:(qt + 1) * P], K[b][:, qt * P:(qt + 1) * P], start=True, stop=True)
                c0, c1 = halves(qt)[0], halves(qt)[-1] + 1
                by_residue = K[b][:, c0 * CH:c1 * CH].rearrange("p (t r m) -> p r t m", r=STRIDE, m=RES)
                for r in range(STRIDE):
                    mm = nc.tensor.matmul(ps[RES * r:RES * (r + 1), h, P:P * (1 + c1 - c0)],
                                          Q[b][h][:, qt * P + RES * r:qt * P + RES * (r + 1)], by_residue[:, r], start=True, stop=True)
                mm.then_inc(sc, 1)

            def turn(n, b, qt, h):
                u = 2 * qt + h
                pe.wait_ge(divd, n * UN + (u + 1))
                at_least(pe, ev_dve, n * UN + u)
                at_least(pe, ev_act, n * UN + u)
                for k in range(width(qt) // P):
                    bank, at = (TB, 0) if k == 0 else (TB + 1, k - 1)
                    mm = nc.tensor.transpose(ps[:, bank, at * P:(at + 1) * P], probs[qt % 2][h][:, k * P:(k + 1) * P], g.ident[:])
                mm.then_inc(tr, 1)

            def weigh(n, b, qt):
                pe.wait_ge(ev_dve, n * UN + (2 * qt + 2))
                pe.wait_ge(ev_act, n * UN + (2 * qt + 2))
                half = qt // HALF
                if qt % HALF == 0:
                    at_least(pe, oc, n * 2)
                for h in range(2):
                    mm = nc.tensor.matmul(ps[HEAD3 * h:HEAD3 * (h + 1), OB + half, qt % HALF * P:(qt % HALF + 1) * P],
                                          V[b][:, qt, HEAD3 * h:HEAD3 * (h + 1)], ownT[qt % 2][h][:],
                                          start=(qt % HALF == 0), stop=False)
                if qt % HALF == HALF - 1:
                    for r in range(STRIDE):
                        for c in range(2):
                            for h in range(2):
                                dst = ps[HEAD3 * h:HEAD3 * (h + 1), OB + half, :].rearrange("p (t r m) -> p r t m", r=STRIDE, m=RES)[:, r]
                                mm = nc.tensor.matmul(dst, VR[b][:, c, r, HEAD3 * h:HEAD3 * (h + 1)],
                                                      farT[h][:, c, r, half * HALF:(half + 1) * HALF, :],
                                                      start=False, stop=(r == STRIDE - 1 and c == 1))
                mm.then_inc(av, 1)

            def slot(n, b, i, more):
                last, older = before(n, b, i, 1), before(n, b, i, 2)
                scores(n, b, i, 0)
                if last:
                    turn(*last, 0)
                scores(n, b, i, 1)
                if older:
                    weigh(*older)
                if more:
                    for j in IN_SLOT[i]:
                        pe.wait_ge(copied, (n + 1) * NPROJ + max(j - 1, 0))
                        project(n + 1, 1 - b, j, PB + j % 2)
                if last:
                    turn(*last, 1)

            pe.wait_ge(permuted, 1)
            for j in range(NPROJ):
                project(0, 0, j, j)
            for i in range(2):
                slot(0, 0, i, True)
            with pe.Fori(0, PAIRS - 1) as hp:
                for i in range(2, B * KT + 2):
                    slot(hp * B + i // KT, i // KT % B, i % KT, True)
            for i in range(2, B * KT):
                slot((PAIRS - 1) * B + i // KT, i // KT, i % KT, i < KT)
            end = B * PAIRS - 1
            turn(end, 1, KT - 1, 0)
            weigh(end, 1, KT - 2)
            turn(end, 1, KT - 1, 1)
            weigh(end, 1, KT - 1)

        @block.scalar
        def _(act):
            def copy_projected(n, b, j, bank):
                which, c = PROJ[j]
                act.wait_ge(projected, n * NPROJ + (j + 1))
                at_least(act, copied, n * NPROJ + j)
                if which == "q":
                    rows = slice(0, HEAD3)
                    nc.scalar.activation(Q[b][0][rows, c * CH:(c + 1) * CH], ps[rows, bank, :], ACT.Copy, scale=HEAD3 ** -0.5)
                    rows = slice(HEAD3, 2 * HEAD3)
                    nc.scalar.activation(Q[b][1][rows, c * CH:(c + 1) * CH], ps[rows, bank, :], ACT.Copy,
                                         scale=HEAD3 ** -0.5).then_inc(copied, 1)
                elif which == "v":
                    nc.scalar.copy(V[b][:, 4 * c:4 * c + 4, :], ps[:, bank, :].rearrange("p (k d) -> p k d", d=P)).then_inc(copied, 1)

            def exp(n, b, qt, h):
                u = 2 * qt + h
                m = width(qt)
                act.wait_ge(mxd, n * UN + (u + 1))
                at_least(act, tr, n * UN + (u - 3))
                nc.scalar.activation(probs[qt % 2][h][:, 0:m], masked[h][:, 0:m], ACT.Exp, bias=negmax[:, u:u + 1],
                                     accum_out=total[:, u:u + 1]).then_inc(ex, 1)

            def copy_turned(n, b, qt, h):
                act.wait_ge(tr, n * UN + (2 * qt + h + 1))
                at_least(act, av, n * KT + (qt - 1))
                c0, c1 = halves(qt)[0], halves(qt)[-1] + 1
                src = ps[:, TB + 1, 0:(c1 - c0) * P].rearrange("p (c r m) -> p c r m", r=STRIDE, m=RES)
                nc.scalar.copy(farT[h][:, c0:c1, :, qt, :], src).then_inc(ev_act, 1)

            def copy_out(n, b, half):
                act.wait_ge(av, n * KT + 4 * (half + 1))
                dst = outT[:, bass.ds(n // B, 1), b * T + half * CH:b * T + (half + 1) * CH].rearrange("p a n -> p (a n)")
                nc.scalar.copy(dst, ps[:, OB + half, :]).then_inc(oc, 1)

            def slot(n, b, i, more):
                last = before(n, b, i, 1)
                exp(n, b, i, 0)
                if last:
                    copy_turned(*last, 0)
                exp(n, b, i, 1)
                if i == 5:
                    copy_out(n, b, 0)
                elif i == 1 and before(n, b, i, 2):
                    copy_out(n - 1, 1 - b, 1)
                if last:
                    copy_turned(*last, 1)
                for j in IN_SLOT[i] if more else []:
                    if PROJ[j][0] in "qv":
                        copy_projected(n + 1, 1 - b, j, PB + j % 2)

            act.wait_ge(cleared, 2 * B + 2)
            for j in range(NPROJ):
                if PROJ[j][0] in "qv":
                    copy_projected(0, 0, j, j)
            for i in range(2):
                slot(0, 0, i, True)
            with act.Fori(0, PAIRS - 1) as hp:
                for i in range(2, B * KT + 2):
                    slot(hp * B + i // KT, i // KT % B, i % KT, True)
            for i in range(2, B * KT):
                slot((PAIRS - 1) * B + i // KT, i // KT, i % KT, i < KT)
            end = B * PAIRS - 1
            copy_turned(end, 1, KT - 1, 0)
            copy_turned(end, 1, KT - 1, 1)
            copy_out(end, 1, 1)
            act.wait_ge(oc, 2 * B * PAIRS)

        @block.gpsimd
        def _(pool):
            for b in range(B):
                for h in range(2):
                    nc.gpsimd.memset(Q[b][h][:], 0.0).then_inc(cleared, 1)
            for h in range(2):
                nc.gpsimd.memset(farT[h][:], 0.0).then_inc(cleared, 1)

        @block.vector
        def _(dve):
            def copy_projected(n, b, j, bank):
                which, c = PROJ[j]
                dve.wait_ge(projected, n * NPROJ + (j + 1))
                dve.wait_ge(copied, n * NPROJ + j)
                if which == "k":
                    nc.vector.tensor_copy(K[b][:, c * CH:(c + 1) * CH], ps[:, bank, :]).then_inc(copied, 1)
                else:
                    nc.vector.tensor_copy(VR[b][:, c], ps[:, bank, :].rearrange("p (r d) -> p r d", d=P)).then_inc(copied, 1)

            def largest(n, b, qt, h):
                u = 2 * qt + h
                m = width(qt)
                nc.vector.tensor_tensor_reduce(masked[h][:, 0:m], ps[:, h, 0:m], mask[:, qt, 0:m], 1.0, -3.0e38, ALU.add, ALU.max,
                                               accum_out=mx[:, u:u + 1]).then_inc(maxd, 1)
                dve.wait_ge(maxd, n * UN + (u + 1))
                nc.vector.tensor_scalar(negmax[:, u:u + 1], mx[:, u:u + 1], -1.0, None, ALU.mult).then_inc(mxd, 1)

            def inverse(n, b, qt, h):
                u = 2 * qt + h
                dve.wait_ge(ex, n * UN + (u + 1))
                at_least(dve, divd, n * UN + u)
                nc.vector.reciprocal(inv[:, u:u + 1], total[:, u:u + 1]).then_inc(invd, 1)

            def divide(n, b, qt, h):
                u = 2 * qt + h
                m = width(qt)
                p = probs[qt % 2][h]
                dve.wait_ge(invd, n * UN + (u + 1))
                nc.vector.tensor_scalar(p[:, 0:m], p[:, 0:m], inv[:, u:u + 1], None, ALU.mult).then_inc(divd, 1)

            def copy_turned(n, b, qt, h):
                dve.wait_ge(tr, n * UN + (2 * qt + h + 1))
                at_least(dve, av, n * KT + (qt - 1))
                nc.vector.tensor_copy(ownT[qt % 2][h][:], ps[:, TB, 0:P]).then_inc(ev_dve, 1)

            def slot(n, b, i, more):
                last = before(n, b, i, 1)
                dve.wait_ge(sc, n * UN + (2 * i + 1))
                if last:
                    inverse(*last, 1)
                largest(n, b, i, 0)
                if last:
                    divide(*last, 1)
                dve.wait_ge(sc, n * UN + (2 * i + 2))
                if last:
                    copy_turned(*last, 0)
                largest(n, b, i, 1)
                inverse(n, b, i, 0)
                divide(n, b, i, 0)
                if last:
                    copy_turned(*last, 1)
                for j in IN_SLOT[i] if more else []:
                    if PROJ[j][0] in "kr":
                        copy_projected(n + 1, 1 - b, j, PB + j % 2)

            dve.wait_ge(const, 16)
            nc.vector.tensor_copy(xr[:].rearrange("p (t r m) -> p t r m", r=STRIDE, m=RES),
                                  g.xnT[:].rearrange("p (t m r) -> p t r m", r=STRIDE, m=RES)).then_inc(permuted, 1)
            for j in range(NPROJ):
                if PROJ[j][0] in "kr":
                    copy_projected(0, 0, j, j)
            for i in range(2):
                slot(0, 0, i, True)
            with dve.Fori(0, PAIRS - 1) as hp:
                for i in range(2, B * KT + 2):
                    slot(hp * B + i // KT, i // KT % B, i % KT, True)
            for i in range(2, B * KT):
                slot((PAIRS - 1) * B + i // KT, i // KT, i % KT, i < KT)
            end = B * PAIRS - 1
            inverse(end, 1, KT - 1, 1)
            divide(end, 1, KT - 1, 1)
            copy_turned(end, 1, KT - 1, 0)
            copy_turned(end, 1, KT - 1, 1)


def output_projection(nc, g, s, W, outT):
    OPB, OPN = 1, 3
    ps = g.ps
    wo = s.sb("wo3", [P, PAIRS, P])
    loaded = s.sem("op_loaded")
    product = s.sem("op_product")
    stored = s.sem("op_stored")

    def sync(sp):
        sp.dma_start(wo[:], W["wo"]).then_inc(loaded, 16)

    def tensor(pe):
        pe.wait_ge(loaded, 16)
        for c in range(NCH):
            if c >= OPN:
                pe.wait_ge(stored, c - OPN + 1)
            for q in range(PAIRS):
                mm = nc.tensor.matmul(ps[:, OPB + c % OPN, :], wo[:, q, :], outT[:, q, c * CH:(c + 1) * CH],
                                      start=(q == 0), stop=(q == PAIRS - 1))
            mm.then_inc(product, 1)

    def scalar(act):
        for c in range(NCH):
            act.wait_ge(product, c + 1)
            by_token = g.branchT[:, c * CH:(c + 1) * CH].rearrange("p (t m r) -> p t r m", r=STRIDE, m=RES)
            nc.scalar.copy(by_token, ps[:, OPB + c % OPN, :].rearrange("p (t r m) -> p t r m", r=STRIDE, m=RES)).then_inc(stored, 1)
        act.wait_ge(stored, NCH)

    steps = Tensors()
    steps.sync, steps.tensor, steps.scalar = sync, tensor, scalar
    return steps


def program(nc, A, out, scratch, layers=(0, 1, 2, 3), parts=("attn", "ffn")):
    g = open_scope(nc)
    with g.ctx:
        g.x = g.sb("x", [P, TILES, D])
        g.xn = g.sb("xn", [P, TILES, D])
        g.xnT = g.sb("xnT", [P, NT])
        g.branchT = g.sb("branchT", [P, NT])
        g.ident = g.sb("ident", [P, P])
        g.identb = g.sb("identb", [P, P], BF16)
        g.ps = g.ctx.enter_context(nc.psum_tensor("ps", [P, 8, CH], F32))
        setup(nc, g, A)
        for n, layer in enumerate(layers):
            if n == 2:
                clear_semaphores(nc, g.used)
            residual_norm(nc, g, first=(n == 0), last=False)
            LAYERS[layer](nc, g, A, scratch, parts)
        residual_norm(nc, g, first=False, last=True)
        finish(nc, g, out)


def weights(A, layer):
    return {k[3:]: v for k, v in A.items() if k.startswith(f"L{layer}_")}


def layer0(nc, g, A, scratch, parts):
    W = weights(A, 0)
    gated_experts(nc, g, W, experts=8, hidden=344, top=2, kind="softmax", beside=head_mixing)


def layer1(nc, g, A, scratch, parts):
    scan_and_experts(nc, g, weights(A, 1), scratch["dispatch"], scratch["expert_out"])


def layer2(nc, g, A, scratch, parts):
    W = weights(A, 2)
    if "attn" in parts:
        s = open_scope(nc, g)
        with s.ctx:
            Vp = s.sb("Vp", [P, TILES, P])
            Q = [s.sb(f"Q{i}", [P, QUAD, T], BF16) for i in range(2)]
            K = [s.sb(f"K{i}", [P, QUAD, T], BF16) for i in range(2)]
            project_qkv(nc, g, scratch["qk"], Vp, W, float(HD) ** -0.5, (*Q, *K))
            column_softmax_attention(nc, g, scratch["qk"], Vp, Q, K, W)
    if "ffn" in parts:
        gated_experts(nc, g, W, experts=32, hidden=96, top=4, kind="sigmoid", add="attn" in parts)


def layer3(nc, g, A, scratch, parts):
    W = weights(A, 3)
    s = open_scope(nc, g)
    with s.ctx:
        outT = s.sb("outT3", [P, PAIRS, NT])
        dilated_attention(nc, g, W, outT)
        projection = output_projection(nc, g, s, W, outT)
        gated_experts(nc, g, W, experts=32, hidden=32, top=4, kind="keys", gated=False, add=True, add_xn=True,
                      meanwhile=projection)


LAYERS = {0: layer0, 1: layer1, 2: layer2, 3: layer3}


def _layouts(i):
    f, bf = np.float32, np.dtype("bfloat16")
    A = {"x": i["L0_attn_x"].reshape(NT, D), "ident": np.eye(P, dtype=f)}

    def wide_rows(w):
        out = np.zeros((P, 4, P), f)
        for h in range(HEADS):
            out[32 * (h % 4):32 * (h % 4) + 8, h // 4, :] = w[8 * h:8 * h + 8, :]
        return out

    swap = np.array([8 * h + (j + 4) % 8 for h in range(HEADS) for j in range(8)])
    kcols = np.array([16 * h + j for h in range(HEADS) for j in range(8)])
    inv = (1.0 / 10000.0 ** (np.arange(0, 8, 2, dtype=f) / f(8))).astype(f)
    freqs = np.arange(T, dtype=f)[:, None] * inv[None, :]
    rows = lambda a: a.astype(f).reshape(T // P, P, 8).transpose(1, 0, 2)
    A["L0_cos"] = rows(np.concatenate([np.cos(freqs), np.cos(freqs)], 1))
    A["L0_sin"] = rows(np.concatenate([-np.sin(freqs), np.sin(freqs)], 1))
    Wq, bq, Wup, bup = i["L0_attn_Wq"], i["L0_attn_bq"], i["L0_attn_Wup"], i["L0_attn_bup"]
    A["L0_wq"] = np.stack([Wq, Wq[:, swap]], 1)
    A["L0_wup"] = np.stack([Wup[:, kcols], Wup[:, kcols[swap]], Wup[:, kcols + 8]], 1)
    A["L0_bias"] = np.broadcast_to(np.stack([bq, bq[swap], bup[kcols], bup[kcols[swap]], bup[kcols + 8]]), (P, 5, P))
    A["L0_wdown"], A["L0_bdown"] = i["L0_attn_Wdown"], i["L0_attn_bdown"][:, None]
    A["L0_wout"] = i["L0_attn_Wout"]
    A["L0_bout"] = i["L0_attn_bout"][:, None]

    half = lambda v: v.reshape(G, P).T
    wx = i["L1_attn_W_x"].reshape(G, P, DTR + 2 * NS).transpose(1, 0, 2)
    A["L1_win"] = i["L1_attn_W_in"].reshape(D, 4, P)
    A["L1_convk"] = i["L1_attn_conv_k"].reshape(TAPS, P, G, P).transpose(1, 2, 0, 3)
    A["L1_convb"] = half(i["L1_attn_conv_b"])
    A["L1_wxdt"] = wx[:, :, 0:DTR]
    A["L1_wxbc"] = np.concatenate([wx[:, :, DTR:]] * 3, 2)
    A["L1_wdt"] = i["L1_attn_W_dt"].reshape(DTR, G, P)
    A["L1_bdt"] = half(i["L1_attn_b_dt"])
    A["L1_alog"] = i["L1_attn_A_log"].reshape(G, P, NS).transpose(1, 0, 2)
    A["L1_D"] = half(i["L1_attn_D"])
    A["L1_wo"] = i["L1_attn_W_out"].reshape(G, P, D).transpose(1, 0, 2)
    A["L1_seln"] = np.broadcast_to(np.concatenate([np.eye(2 * NS)] * 3)[:, :, None], (96, 2 * NS, P)).astype(bf)
    A["L1_wr"] = i["L1_ffn_Wg"]
    A["L1_iota"] = np.broadcast_to(np.arange(ES, dtype=f), (P, ES))
    A["L1_tri"] = (np.arange(P)[:, None] <= np.arange(P)[None, :]).astype(bf)
    A["L1_ones"] = np.ones((P, P), bf)
    A["L1_token"] = (DUMP + np.arange(NT)).reshape(TILES, P).T.astype(f)
    A["L1_restart"] = np.broadcast_to((np.arange(TILES) > 0).astype(f), (P, ES, TILES))
    A["L1_w1"] = i["L1_ffn_w1"]
    A["L1_w2"] = i["L1_ffn_w2"].reshape(ES, FS, P, D).transpose(0, 2, 1, 3)
    wqkv, bqkv = i["L2_attn_W_qkv"], i["L2_attn_b_qkv"]
    A["L2_wqk"] = wqkv[:, 0:2 * P].reshape(D, 2, P)
    A["L2_bqk"] = bqkv[0:2 * P].reshape(2, P).T
    A["L2_wv"] = wqkv[:, 2 * P:]
    A["L2_bv"] = np.broadcast_to(bqkv[2 * P:], (P, P))
    A["L2_mask"] = np.where(np.arange(P)[None, :] < np.arange(P)[:, None], f(-1e30), f(0)).astype(f)
    A["L2_wout"] = wide_rows(i["L2_attn_W_proj"])
    A["L2_bout"] = i["L2_attn_b_proj"][:, None]

    pairs = lambda w: w.reshape(D, PAIRS, 2 * HEAD3).transpose(1, 0, 2)
    A["L3_wqkv"] = np.stack([pairs(i[f"L3_attn_w_{n}"]) for n in "qkv"], 2)
    A["L3_wo"] = i["L3_attn_w_o"].reshape(PAIRS, 2 * HEAD3, D).transpose(1, 0, 2)
    token = np.arange(P) % RES * STRIDE + np.arange(P) // RES
    mask = np.full((KT, P, 3 * P), f(-1e30), f)
    for qt in range(KT):
        keys = [qt * P + token[None, :] + np.zeros((P, 1), int)]
        for c in halves(qt):
            far = c * CH + np.arange(P)[None, :] // RES * P + np.arange(P)[None, :] % RES * STRIDE + token[:, None] % STRIDE
            keys.append(np.where(far // P == qt, -T, far))
        key = np.concatenate(keys, 1)
        query = qt * P + token[:, None]
        gap = np.abs(key - query)
        seen = (key // SEGMENT == query // SEGMENT) | ((gap > 0) & (gap % STRIDE == 0) & (gap <= REACH))
        mask[qt, :, 0:key.shape[1]] = np.where(seen, f(0), f(-1e30))
    A["L3_mask"] = mask.transpose(1, 0, 2)

    def experts(layer, up, gate, down, n, hidden):
        ft = -(-n * hidden // P)
        pad = ft * P - n * hidden

        def cols(w):
            w = np.pad(w.transpose(1, 0, 2).reshape(D, n * hidden), ((0, 0), (0, pad)))
            return w.reshape(D, ft, P)
        A[f"L{layer}_wg"] = cols(gate)
        if up is not None:
            A[f"L{layer}_wu"] = cols(up)
        w = np.pad(down.reshape(n * hidden, D), ((0, pad), (0, 0)))
        A[f"L{layer}_wd"] = w.reshape(ft, P, D).transpose(1, 0, 2)
        owner = np.arange(ft * P) // hidden
        one = (owner[None, :] == np.arange(n)[:, None]).astype(bf)
        A[f"L{layer}_sel"] = np.concatenate([one] * 3 + [np.zeros((P - 3 * n, ft * P), bf)]).reshape(P, ft, P)
        A[f"L{layer}_iota"] = np.broadcast_to(np.arange(n, dtype=f), (P, n))

    experts(0, i["L0_ffn_Wu"], i["L0_ffn_Wg"], i["L0_ffn_Wd"], 8, 344)
    A["L0_wr"] = i["L0_ffn_Ws"]
    A["L0_br"] = np.broadcast_to(i["L0_ffn_bs"], (P, 8))
    experts(2, i["L2_ffn_w3"], i["L2_ffn_w1"], i["L2_ffn_w2"], 32, 96)
    A["L2_wr"] = i["L2_ffn_gate_w"].T
    A["L2_br"] = np.broadcast_to(i["L2_ffn_e_bias"], (P, 32))
    experts(3, None, i["L3_ffn_values_down"], i["L3_ffn_values_up"], 32, 32)
    A["L3_wh"] = i["L3_ffn_hasher_w"].T
    A["L3_wkeys"] = i["L3_ffn_keys"].T
    A["L3_scale"] = np.broadcast_to(i["L3_ffn_scale"], (P, 1))
    return {k: np.ascontiguousarray(v) for k, v in A.items()}


def _make(nc, A, out_shape, **options):
    aps = {k: nc.dram_tensor("in_" + k, v.shape, mybir.dt.from_np(v.dtype), kind="ExternalInput").ap() for k, v in A.items()}
    out = nc.dram_tensor("out_x", out_shape, F32, kind="ExternalOutput").ap()
    scratch = {"qk": nc.dram_tensor("qk_parts", (2, 3, P, NT), BF16, kind="Internal").ap(),
               "dispatch": nc.dram_tensor("dispatch", (DUMP + NT, D), F32, kind="Internal").ap(),
               "expert_out": nc.dram_tensor("expert_out", (DUMP, D), F32, kind="Internal").ap()}
    program(nc, aps, out, scratch, **options)


def kernel(**inputs):
    import concourse.bacc as bacc
    from concourse.bass_utils import run_bass_kernel_spmd

    nc = bacc.Bacc("TRN2", target_bir_lowering=False, num_devices=1)
    A = _layouts({k: np.asarray(v) for k, v in inputs.items()})
    _make(nc, A, (NT, D))
    r = run_bass_kernel_spmd(nc, [{"in_" + k: v for k, v in A.items()}], core_ids=[0])
    return r.results[0]["out_x"].reshape(B, T, D)
```
